# Optimizing a Trainium2 kernel written in Bass

```python
import numpy as np
import jax
import jax.numpy as jnp

def _softmax(x, axis=-1):
    return jax.nn.softmax(x, axis=axis)

def _gelu(x):
    return jax.nn.gelu(x, approximate=True)

def _silu(x):
    return jax.nn.silu(x)

def _sigmoid(x):
    return jax.nn.sigmoid(x)

def _layernorm(x, axis=-1, eps=1e-05):
    m = jnp.mean(x, axis=axis, keepdims=True)
    v = jnp.var(x, axis=axis, keepdims=True)
    return (x - m) / jnp.sqrt(v + eps)

def _scatter_add(tgt, idx, src, axis=0):
    return tgt.at[idx].add(src)

def _segment_sum(src, seg, n):
    return jax.ops.segment_sum(src, seg, n)
kernel_name = 'mk_adj_ffn_d1_adj_r2_2e2aad'

def setup_inputs(seed: int=0):
    np.random.seed(seed)
    _w = jnp.asarray

    def _rec_inputs():
        import jax
        import jax.numpy as jnp
        _gk = jax.random.key(seed)
        x = -0.0002928 + 1 * jax.random.normal(jax.random.fold_in(_gk, 1), (4096, 256), jnp.float32)
        _a = jax.random.bernoulli(jax.random.fold_in(_gk, 2), 0.000488281, (4096, 4096))
        adj = _a
        return (x, adj)
    x, adj = _rec_inputs()

    def _L0_gnn_setup():
        import jax, jax.numpy as jnp
        import numpy as np
        N = 4096
        D = 256
        NEG = -1e+30
        key = jax.random.key(seed)
        ks = jax.random.split(key, 5)
        neuron_states = jax.random.normal(ks[0], (N, D), dtype=jnp.float32)
        adjacency = jax.random.bernoulli(ks[1], 0.05, (N, N))
        Wq = jax.random.normal(ks[2], (D, D), dtype=jnp.float32) / np.sqrt(D)
        Wk = jax.random.normal(ks[3], (D, D), dtype=jnp.float32) / np.sqrt(D)
        Wv = jax.random.normal(ks[4], (D, D), dtype=jnp.float32) / np.sqrt(D)
        return {'neuron_states': neuron_states, 'adjacency': adjacency, 'Wq': Wq, 'Wk': Wk, 'Wv': Wv}
    _L0_gnn_all = _L0_gnn_setup()
    _L0_gnn_in = {k: v for k, v in _L0_gnn_all.items() if k in ('Wq', 'Wk', 'Wv')}
    del _L0_gnn_all

    def _L0_ffn_setup():
        import jax, jax.numpy as jnp
        import numpy as np
        TOP_K = 2
        key = jax.random.key(seed)
        ks = jax.random.split(key, 6)
        B, T, C, E, H = (4, 2048, 256, 8, 1024)
        x = jax.random.normal(ks[0], (B, T, C), dtype=jnp.float32)
        W_router = jax.random.normal(ks[1], (C, E), dtype=jnp.float32) * 0.02
        W1 = jax.random.normal(ks[2], (E, C, H), dtype=jnp.float32) * 0.02
        b1 = jnp.zeros((E, H), dtype=jnp.float32)
        W2 = jax.random.normal(ks[3], (E, H, C), dtype=jnp.float32) * 0.02
        b2 = jnp.zeros((E, C), dtype=jnp.float32)
        return {'x': x, 'W_router': W_router, 'W1': W1, 'b1': b1, 'W2': W2, 'b2': b2}
    _L0_ffn_all = _L0_ffn_setup()
    _L0_ffn_in = {k: v for k, v in _L0_ffn_all.items() if k in ('W_router', 'W1', 'b1', 'W2', 'b2')}
    del _L0_ffn_all
    return {'x': x, 'adj': adj, 'L0_gnn_Wq': _L0_gnn_in['Wq'], 'L0_gnn_Wk': _L0_gnn_in['Wk'], 'L0_gnn_Wv': _L0_gnn_in['Wv'], 'L0_ffn_W_router': _L0_ffn_in['W_router'], 'L0_ffn_W1': _L0_ffn_in['W1'], 'L0_ffn_b1': _L0_ffn_in['b1'], 'L0_ffn_W2': _L0_ffn_in['W2'], 'L0_ffn_b2': _L0_ffn_in['b2']}

def reference(x, adj, L0_gnn_Wq, L0_gnn_Wk, L0_gnn_Wv, L0_ffn_W_router, L0_ffn_W1, L0_ffn_b1, L0_ffn_W2, L0_ffn_b2):
    import jax
    import jax.numpy as jnp

    def _L0_gnn_ref(neuron_states, adjacency, Wq, Wk, Wv):
        import jax, jax.numpy as jnp
        import numpy as np
        N = 4096
        D = 256
        NEG = -1e+30
        q = neuron_states @ Wq.T
        k = neuron_states @ Wk.T
        v = neuron_states @ Wv.T
        mask = adjacency.T
        scores = jnp.where(mask, q @ k.T, NEG)
        attn = jax.nn.softmax(scores, axis=1)
        attn = jnp.where(mask, attn, 0.0)
        return attn @ v

    def _L0_ffn_ref(x, W_router, W1, b1, W2, b2):
        import jax, jax.numpy as jnp
        import numpy as np
        TOP_K = 2
        B, T, C = x.shape
        E = W_router.shape[1]
        x_flat = x.reshape(B * T, C)
        logits = x_flat @ W_router
        probs = jax.nn.softmax(logits, axis=-1)
        topk_p, topk_i = jax.lax.top_k(probs, TOP_K)
        topk_p = topk_p / topk_p.sum(axis=-1, keepdims=True)
        combine = (jax.nn.one_hot(topk_i, E, dtype=x_flat.dtype) * topk_p[..., None]).sum(axis=1)
        out = jnp.zeros_like(x_flat)
        for e in range(E):
            h = jax.nn.relu(x_flat @ W1[e] + b1[e])
            y = h @ W2[e] + b2[e]
            out = out + combine[:, e:e + 1] * y
        return out.reshape(B, T, C)
    x = x + _L0_gnn_ref(_layernorm(x, axis=-1), adj, L0_gnn_Wq, L0_gnn_Wk, L0_gnn_Wv)
    x = x + _L0_ffn_ref(_layernorm(x, axis=-1)[None], L0_ffn_W_router, L0_ffn_W1, L0_ffn_b1, L0_ffn_W2, L0_ffn_b2)[0]
    return x

_drawn_inputs = setup_inputs


def setup_inputs(seed=0):
    import zlib

    import numpy as np

    out = dict(_drawn_inputs(seed))
    spreads = {'L0_ffn_b1': (0.0, 0.338), 'L0_ffn_b2': (0.0, 0.1)}
    factors = {}
    for name, (base, spread) in spreads.items():
        noise = np.random.default_rng([zlib.crc32(name.encode()), seed]).standard_normal(out[name].shape)
        drawn = base * np.exp(spread * noise) if base else spread * noise
        out[name] = jnp.asarray(drawn.astype(out[name].dtype))
    for name, factor in factors.items():
        out[name] = (out[name] * factor).astype(out[name].dtype)
    return out
```

```python
from contextlib import ExitStack

import numpy as np

import concourse.bass as bass
from concourse import mybir

F32 = mybir.dt.float32
F32R = mybir.dt.float32r
F16 = mybir.dt.float16
F8 = mybir.dt.float8e4
U8 = mybir.dt.uint8
U16 = mybir.dt.uint16
U32 = mybir.dt.uint32
I32 = mybir.dt.int32
ALU = mybir.AluOpType
ACT = mybir.ActivationFunctionType
AX = mybir.AxisListType

P = 128
N = 4096
C = 256
E = 8
H = 1024
EPS = 1e-5
NEG = -1e30
NT = N // P
CC = C // P
HC = H // P
GT = 4
NG = NT // GT
K = 8
QW = 1024
NQ = N // QW
CODE0 = 0x4000
T = 256
TS = T // P
MAX_TILES = 2 * N // T + E
REGION = N + T


def attention_and_experts(nc, x, adj, Wq, Wk, Wv, Wr, W1, b1, W2, b2, out):
    ctx = ExitStack()

    def sb(name, shape, dt, stack=ctx):
        return stack.enter_context(nc.sbuf_tensor(name, shape, dt))

    def ps(name, shape, dt, stack=ctx):
        return stack.enter_context(nc.psum_tensor(name, shape, dt))

    def sem(name):
        return ctx.enter_context(nc.semaphore(name))

    with ctx:
        xn_rows = nc.dram_tensor("xn_rows", (N, C), F32).ap()
        expert_in = nc.dram_tensor("expert_in", (E * REGION, C), F32).ap()
        expert_out = nc.dram_tensor("expert_out", ((MAX_TILES + 1) * T, C), F32).ap()

        x_all = sb("x_all", [P, NT, C], F32)
        ident = sb("ident", [P, P], F32)
        stats = sb("stats", [P, 2, 6], F32)
        mv = sb("mv", [P, NT, 2], F32)
        rstd = sb("rstd", [P, NT], F32)
        nr = sb("nr", [P, 2, NT], F32)
        wvT = sb("wvT", [P, CC, C], F32)
        wr = sb("wr", [P, CC, E], F32)
        b1T = sb("b1T", [P, E * HC], F32)
        b1e = sb("b1e", [P, 2, HC], F32)
        zero_rows = sb("zero_rows", [P, 1, C], F32)
        tri = sb("tri", [P, P], F32)
        ones = sb("ones", [P, P], F32)
        iota_i = sb("iota_i", [P, 2, E], I32)
        iota_f = sb("iota_f", [P, 2, E], F32)
        rl = sb("rl", [P, 3, NT], F32)
        row0 = sb("row0", [P, GT + 1, E], F32)
        pos_all = sb("pos_all", [P, 2, NT], U32)
        d_all = sb("d_all", [P, NT], F32)
        gates = sb("gates", [P, 3, NT], F32)
        gpos = sb("gpos", [P, 2, 2, GT], U32)
        plan_f = sb("plan_f", [P, 5, E], F32)
        tile_f = sb("tile_f", [1, 3, MAX_TILES], F32)
        tile_n = sb("tile_n", [1, MAX_TILES], I32)
        tile_rows = sb("tile_rows", [1, MAX_TILES], I32)
        plan_i = sb("plan_i", [P, 2, E], I32)
        plan = sb("plan", [1, 5, E], I32)

        sums = ExitStack()
        y_all = sb("y_all", [P, NT, C], F32, sums)
        ml_all = sb("ml_all", [P, NT, 2], F32, sums)
        deg_all = sb("deg_all", [P, NT], F32, sums)
        att = ExitStack()
        row_all = sb("row_all", [P, NT, C], F32, att)
        adj_raw = sb("adj_raw", [P, NT, GT * P], U8, att)
        adj_f8 = sb("adj_f8", [P, NT, GT * P], U8, att)
        codediag = sb("codediag", [P, NT, P], F16, att)
        half16 = sb("half16", [P, 1], F16, att)
        code_i = sb("code_i", [P, NT], I32, att)
        code_u = sb("code_u", [P, NT], U16, att)
        wqk = sb("wqk", [P, CC, C], F32, att)
        wraw = sb("wraw", [P, 3, CC, C], F32, att)
        b1raw = sb("b1raw", [E * HC, P], F32, att)
        xt = sb("xt", [P, C], F32, att)
        xT = sb("xT", [P, CC, P], F32, att)
        q_sb = sb("q_sb", [P, 2, C], F32, att)
        best = sb("best", [P, NQ * K], F16, att)
        top = sb("top", [P, 2, K], F16, att)
        idx = sb("idx", [P, GT, K], U32, att)
        valid = sb("valid", [P, 2, K], F32, att)
        neg = sb("neg", [P, 2, K], F32, att)
        nbr = sb("nbr", [P, GT, K, C], F32, att)
        prod = sb("prod", [P, K, C], F32, att)
        s = sb("s", [P, 2, K], F32, att)
        sv = sb("sv", [P, K], F32, att)
        sm = sb("sm", [P, 2, K], F32, att)
        ml = sb("ml", [P, 2, 2], F32, att)
        p = sb("p", [P, 2, K], F32, att)
        diag = sb("diag", [P, 2, K, P], F32, att)

        rounds_f = sb("rounds_f", [NT, 2], F32, att)
        ident16 = sb("ident16", [P, P], F16, att)
        rounds_row = sb("rounds_row", [1, 6, NT], F32, att)
        rounds_i = sb("rounds_i", [1, 2, NT], I32, att)
        sched = sb("sched", [1, 2, NT], I32, att)
        run = sb("run", [P, 8], F32, att)
        run_y = diag[:, 1, 0:CC, :].rearrange("p k c -> p (k c)")

        attp = ExitStack()
        codes = ps("codes", [P, 2, QW], F32, attp)
        psT = ps("psT", [P, 512], F32, attp)
        psQ = ps("psQ", [P, 512], F32, attp)
        psY = ps("psY", [P, 512], F32, attp)
        psD = ps("psD", [P, 512], F32, attp)
        attp.close()
        att.close()

        mid = ExitStack()
        yt = sb("yt", [P, 2, C], F32, mid)
        yT = sb("yT", [P, 2, C], F32, mid)
        st2 = sb("st2", [P, GT, 6], F32, mid)
        mv2 = sb("mv2", [P, GT, 2], F32, mid)
        rs2 = sb("rs2", [P, 4, GT], F32, mid)
        xg = sb("xg", [P, 2, GT, C], F32, mid)
        xgT = sb("xgT", [P, 2, C], F32, mid)
        lg = sb("lg", [P, GT, E], F32, mid)
        m8 = sb("m8", [P, GT, 8], F32, mid)
        i8 = sb("i8", [P, GT, 8], U32, mid)
        ef = sb("ef", [P, GT, 2], F32, mid)
        oh = sb("oh", [P, 3, GT, E], F32, mid)
        z = sb("z", [P, 3, GT, E], F32, mid)
        posf = sb("posf", [P, 2, GT], F32, mid)
        out_f = sb("out_f", [P, 2, 2, NT], F32, mid)
        out_s = sb("out_s", [P, 2, NT], F32, mid)
        pos = sb("pos", [P, 2, 2, GT], U32, mid)
        psYT = ps("psYT", [P, 2, 512], F32, mid)
        psPr = ps("psPr", [P, 2, 512], F32, mid)
        psXT = ps("psXT", [P, 2, 512], F32, mid)
        psL = ps("psL", [P, 512], F32, mid)
        psR = ps("psR", [P, 2, GT * E], F32, mid)
        mid.close()
        sums.close()

        ffn = ExitStack()
        w1_raw = sb("w1_raw", [P, CC, H], F32, ffn)
        w2_raw = sb("w2_raw", [P, HC, C], F32, ffn)
        w1_hi = sb("w1_hi", [P, 2, CC, H], F32R, ffn)
        w1_lo = sb("w1_lo", [P, 2, CC, H], F32R, ffn)
        w2_hi = sb("w2_hi", [P, 2, HC, C], F32R, ffn)
        w2_lo = sb("w2_lo", [P, 2, HC, C], F32R, ffn)
        b2_rows = sb("b2_rows", [P, E, C], F32, ffn)
        x_in = sb("x_in", [P, TS, C], F32, ffn)
        x_hi = sb("x_hi", [P, CC, T], F32R, ffn)
        x_lo = sb("x_lo", [P, CC, T], F32R, ffn)
        h_f = sb("h_f", [P, HC, T], F32, ffn)
        h_hi = sb("h_hi", [P, HC, T], F32R, ffn)
        h_lo = sb("h_lo", [P, HC, T], F32R, ffn)
        y_out = sb("y_out", [P, TS, C], F32, ffn)
        e_rows = sb("e_rows", [P, 4, 2, C], F32, ffn)
        ffnp = ExitStack()
        psX = ps("psX", [P, 512], F32, ffnp)
        psH = ps("psH", [P, 4, 512], F32, ffnp)
        psE = ps("psE", [P, TS, 512], F32, ffnp)
        ffnp.close()
        ffn.close()

        x_loaded = [sem(f"x_loaded{i}") for i in range(4)]
        w_loaded = sem("w_loaded")
        adj_loaded = sem("adj_loaded")
        xn_stored = sem("xn_stored")
        gathered = [sem(f"gathered{i}") for i in range(GT)]
        passed = {e.engine: sem(f"passed_{n}") for n, e in (("pe", nc.tensor), ("dve", nc.vector), ("pool", nc.gpsimd), ("sp", nc.sync), ("act", nc.scalar))}
        zeroed = sem("zeroed")
        counted = sem("counted")
        ident_ready = sem("ident_ready")
        cast16 = sem("cast16")
        half_ready = sem("half_ready")
        codediag_ready = sem("codediag_ready")
        ln_step = sem("ln_step")
        rstd_sqrt = sem("rstd_sqrt")
        xn_ready = sem("xn_ready")
        w_t = sem("w_t")
        w_sb = sem("w_sb")
        adj_shifted = sem("adj_shifted")
        codes_ready = sem("codes_ready")
        codes_used = sem("codes_used")
        xt_ready = sem("xt_ready")
        xT_ps = sem("xT_ps")
        xT_ready = sem("xT_ready")
        q_ps = sem("q_ps")
        q_ready = sem("q_ready")
        found = sem("found")
        idx_ready = sem("idx_ready")
        scored = sem("scored")
        sm_ready = sem("sm_ready")
        p_ready = sem("p_ready")
        diag_ready = sem("diag_ready")
        y_ps = sem("y_ps")
        y_used = sem("y_used")
        deg_ps = sem("deg_ps")
        deg_copied = sem("deg_copied")
        out_stored = sem("out_stored")
        deg_T = sem("deg_T"); deg_max = sem("deg_max"); deg_row = sem("deg_row")
        plan_step = sem("plan_step"); rounds_known = sem("rounds_known")
        more_free = sem("more_free"); more_adj = sem("more_adj"); more_shift = sem("more_shift")
        more_codes = sem("more_codes"); more_used = sem("more_used"); more_idx = sem("more_idx")
        more_rows = sem("more_rows"); more_xt = sem("more_xt"); more_xTps = sem("more_xTps")
        more_xT = sem("more_xT"); more_qps = sem("more_qps"); more_q = sem("more_q")
        more_m = sem("more_m"); more_p = sem("more_p"); more_diag = sem("more_diag")
        more_y = sem("more_y"); more_step = sem("more_step"); more_done = sem("more_done")
        route_consts = sem("route_consts"); rl_step = sem("rl_step")
        yt_ready = sem("yt_ready"); yT_ps = sem("yT_ps"); yT_ready = sem("yT_ready")
        proj_ps = sem("proj_ps"); x2_ready = sem("x2_ready"); ln2_step = sem("ln2_step")
        var_ready = sem("var_ready"); std_ready = sem("std_ready")
        xg_ready = sem("xg_ready"); xg_ps = sem("xg_ps"); xgT_ready = sem("xgT_ready")
        lg_done = sem("lg_done"); lg_ready = sem("lg_ready"); oh_ready = sem("oh_ready")
        rank_ps = sem("rank_ps"); pos_ready = sem("pos_ready")
        xg_free = sem("xg_free")
        scattered = [sem("scattered0"), sem("scattered1")]
        planned = sem("planned"); tails_zeroed = sem("tails_zeroed"); d_exp = sem("d_exp")
        rest_zeroed = sem("rest_zeroed"); rest_known = sem("rest_known")
        b2_loaded = sem("b2_loaded"); x_ps = sem("x_ps"); b1_moved = sem("b1_moved")
        w_raw = sem("w_raw"); w_hi = sem("w_hi"); w_split = sem("w_split"); w_used = sem("w_used")
        xin_loaded = sem("xin_loaded"); xin_used = sem("xin_used"); xh_ready = sem("xh_ready"); xl_ready = sem("xl_ready")
        h_ps = sem("h_ps"); hf_ready = sem("hf_ready"); hh_ready = sem("hh_ready"); hl_ready = sem("hl_ready")
        e_ps = sem("e_ps"); yo_ready = sem("yo_ready"); yo_stored = sem("yo_stored")
        results = [sem(f"results{i}") for i in range(4)]
        gpos_ready = sem("gpos_ready"); mixed = sem("mixed"); mix_step = sem("mix_step")

        x_t = x.rearrange("(t p) c -> p t c", p=P)
        out_t = out.rearrange("(t p) c -> p t c", p=P)
        adj_u8 = adj.rearrange("(b p) i -> p b i", p=P)
        XL = NT // 4

        def wait_alone(eng, what, value):
            eng.wait_ge(what, value)
            if not isinstance(value, int):
                eng.sem_inc(passed[eng.engine], 1)

        block = ctx.enter_context(nc.Block())

        @block.sync
        def _(sp):
            for i in range(4):
                sp.dma_start(x_all[:, i * XL:(i + 1) * XL, :], x_t[:, i * XL:(i + 1) * XL, :]).then_inc(x_loaded[i], 16)
                if i == 0:
                    for n, w in enumerate((Wq, Wk, Wv)):
                        sp.dma_start(wraw[:, n], w.rearrange("(k p) c -> p k c", p=P)).then_inc(w_loaded, 16)
                    sp.dma_start(wr[:], Wr.rearrange("(k p) e -> p k e", p=P)).then_inc(w_loaded, 16)
                    sp.dma_start(b1raw[:], b1.rearrange("e (k h) -> (e k) h", h=P)).then_inc(w_loaded, 16)
                    sp.dma_start(adj_raw[:], adj_u8[:, :, 0:GT * P]).then_inc(adj_loaded, 16)
            for i in range(4):
                sp.wait_ge(xn_ready, (i + 1) * XL)
                sp.dma_start(xn_rows.rearrange("(t p) c -> p t c", p=P)[:, i * XL:(i + 1) * XL, :],
                             row_all[:, i * XL:(i + 1) * XL, :]).then_inc(xn_stored, 16)
            with sp.Fori(1, NG) as g:
                wait_alone(sp, adj_shifted, g)
                sp.dma_start(adj_raw[:], adj_u8[:, :, bass.ds(g * (GT * P), GT * P)]).then_inc(adj_loaded, 16)
            sp.wait_ge(rounds_known, 1)
            with sp.Fori(0, NT) as t:
                r = sp.value_load(sched[0:1, 0, bass.ds(t, 1)], min_val=0, max_val=N // K)
                before = sp.value_load(sched[0:1, 1, bass.ds(t, 1)], min_val=0, max_val=NT * N // K)
                with sp.If(r > 0):
                    with sp.Fori(0, r) as i:
                        wait_alone(sp, more_free, before + i + 1)
                        sp.dma_start(adj_raw[:, :, 0:P], adj_u8[:, :, bass.ds(t * P, P)]).then_inc(more_adj, 16)
            sp.wait_ge(planned, 1)
            for e in range(E):
                end = sp.value_load(plan[0:1, 2, e:e + 1], min_val=0, max_val=E * REGION - T)
                sp.dma_start(expert_in[bass.ds(end, T), :].rearrange("(s p) c -> p s c", p=P), zero_rows[:].to_broadcast([P, TS, C])).then_inc(tails_zeroed, 16)
            sp.wait_ge(tails_zeroed, E * 16)
            for b in range(2):
                sp.wait_ge(scattered[b], 16 * 2 * GT * (NG // 2))

            sp.dma_start(b2_rows[:].rearrange("p e c -> p (e c)"), b2.rearrange("(a e) c -> a (e c)", a=1).to_broadcast([P, E * C])).then_inc(b2_loaded, 16)

            def tile_row(n):
                return sp.value_load(tile_rows[0:1, bass.ds(n, 1)], min_val=0, max_val=E * REGION - T)

            def load_tile(n, r):
                wait_alone(sp, x_ps, n + 1)
                sp.dma_start(x_in[:], expert_in[bass.ds(r, T), :].rearrange("(s p) c -> p s c", p=P)).then_inc(xin_loaded, 16)

            def store_tile(n):
                wait_alone(sp, yo_ready, n * TS + TS + TS)
                sp.dma_start(expert_out[bass.ds(n * T, T), :].rearrange("(s p) c -> p s c", p=P), y_out[:]).then_inc(yo_stored, 16)
            total = sp.value_load(plan[0:1, 3, 0:1], min_val=E, max_val=MAX_TILES)
            with sp.Fori(total, MAX_TILES + 1) as n:
                sp.dma_start(expert_out[bass.ds(n * T, T), :].rearrange("(s p) c -> p s c", p=P),
                             zero_rows[:].to_broadcast([P, TS, C])).then_inc(rest_zeroed, 16)
            load_tile(0, 0)
            with sp.Fori(1, total) as n:
                load_tile(n, tile_row(n))
                store_tile(n - 1)
            store_tile(total - 1)
            rest = sp.value_load(plan[0:1, 4, 0:1], min_val=1, max_val=MAX_TILES + 1)
            wait_alone(sp, rest_zeroed, rest * 16)
            sp.sem_inc(rest_known, 1)
            with sp.Fori(0, NG) as g:
                wait_alone(sp, mixed, g * GT + GT + GT)
                sp.dma_start(out_t[:, bass.ds(g * GT, GT), :], x_all[:, bass.ds(g * GT, GT), :]).then_inc(out_stored, 16)
            sp.wait_ge(out_stored, 16 * NG)

        @block.gpsimd
        def _(pool):
            pool.memset(ident[:], 0.0).then_inc(zeroed, 1)
            pool.iota(code_i[:], pattern=[[P, NT]], base=CODE0 - 0x400, channel_multiplier=1).then_inc(counted, 1)
            pool.wait_ge(zeroed, 1)
            pool.affine_select(out=ident[:], in_=ident[:], compare_op=ALU.not_equal, fill=1.0, base=0,
                               pattern=[[-1, P]], channel_multiplier=1).then_inc(ident_ready, 1)
            pool.memset(ones[:], 1.0).then_inc(zeroed, 1)
            pool.iota(iota_i[:, 0, :], pattern=[[1, E]], base=0, channel_multiplier=0).then_inc(route_consts, 1)
            pool.iota(iota_i[:, 1, :], pattern=[[REGION, E]], base=0, channel_multiplier=0).then_inc(route_consts, 1)
            pool.iota(tile_n[:], pattern=[[1, MAX_TILES]], base=0, channel_multiplier=0).then_inc(route_consts, 1)
            pool.wait_ge(zeroed, 2)
            pool.affine_select(out=tri[:], in_=ones[:], compare_op=ALU.is_gt, fill=0.0, base=0,
                               pattern=[[1, P]], channel_multiplier=-1).then_inc(route_consts, 1)
            pool.wait_ge(xn_stored, 64)

            def gather(t, u):
                wait_alone(pool, idx_ready, t + 1)
                wait_alone(pool, y_ps, t + 1)
                for k in range(K):
                    pool.indirect_dma_start(nbr[:, u, k, :], None, xn_rows,
                                            bass.IndirectOffsetOnAxis(ap=idx[:, u, k:k + 1], axis=0)).then_inc(gathered[u], 16)
            with pool.Fori(0, NG) as g:
                for u in range(GT):
                    gather(g * GT + u, u)
            pool.wait_ge(rounds_known, 1)
            with pool.Fori(0, NT) as t:
                r = pool.value_load(sched[0:1, 0, bass.ds(t, 1)], min_val=0, max_val=N // K)
                before = pool.value_load(sched[0:1, 1, bass.ds(t, 1)], min_val=0, max_val=NT * N // K)
                with pool.If(r > 0):
                    with pool.Fori(0, r) as i:
                        wait_alone(pool, more_idx, before + i + 1)
                        for k in range(K):
                            pool.indirect_dma_start(nbr[:, 0, k, :], None, xn_rows,
                                                    bass.IndirectOffsetOnAxis(ap=idx[:, 0, k:k + 1], axis=0)).then_inc(more_rows, 16)

            def scatter(g, b, half):
                wait_alone(pool, pos_ready, g + 1)
                for c in range(2):
                    for u in range(GT):
                        pool.indirect_dma_start(expert_in, bass.IndirectOffsetOnAxis(ap=pos[:, b, c, u:u + 1], axis=0),
                                                xg[:, b, u, :], None).then_inc(scattered[b], 16)
                pool.wait_ge(scattered[b], half * (32 * GT) + 32 * GT)
                pool.sem_inc(xg_free, 1)
            with pool.Fori(0, NG // 2) as g:
                scatter(g * 2, 0, g)
                scatter(g * 2 + 1, 1, g)

            def split_weights(e, b):
                wait_alone(pool, w_split, e * 2 + 2)
                pool.dma_start(w1_raw[:], W1[bass.ds(e, 1)].rearrange("a (k p) h -> p (a k) h", p=P)).then_inc(w_raw, 16)
                pool.dma_start(w2_raw[:], W2[bass.ds(e, 1)].rearrange("a (k p) c -> p (a k) c", p=P)).then_inc(w_raw, 16)
                wait_alone(pool, w_used, e + 1)
                wait_alone(pool, w_raw, e * 32 + 32)
                pool.tensor_copy(w1_hi[:, b], w1_raw[:]).then_inc(w_hi, 1)
                pool.tensor_copy(w2_hi[:, b], w2_raw[:]).then_inc(w_hi, 1)
                wait_alone(pool, w_hi, e * 2 + 2)
                pool.tensor_tensor(w1_lo[:, b], w1_raw[:], w1_hi[:, b].bitcast(F32), ALU.subtract).then_inc(w_split, 1)
                pool.tensor_tensor(w2_lo[:, b], w2_raw[:], w2_hi[:, b].bitcast(F32), ALU.subtract).then_inc(w_split, 1)
            pool.wait_ge(planned, 1)
            pool.sem_inc(w_split, 2)
            with pool.Fori(0, E // 2) as e:
                split_weights(e * 2, 0)
                split_weights(e * 2 + 1, 1)
            def fetch(g, b):
                wait_alone(pool, gpos_ready, g + 1)
                for u in range(GT):
                    wait_alone(pool, mixed, g * GT + u + 1)
                    for c in range(2):
                        pool.indirect_dma_start(e_rows[:, u, c, :], None, expert_out,
                                                bass.IndirectOffsetOnAxis(ap=gpos[:, b, c, u:u + 1], axis=0)).then_inc(results[u], 16)
            total = pool.value_load(plan[0:1, 3, 0:1], min_val=E, max_val=MAX_TILES)
            wait_alone(pool, yo_stored, total * 16 + 16)
            pool.wait_ge(rest_known, 1)
            with pool.Fori(0, NG // 2) as g:
                fetch(g * 2, 0)
                fetch(g * 2 + 1, 1)

        @block.vector
        def _(dve):
            dve.sem_inc(codes_used, 2)
            dve.sem_inc(sm_ready, 2)
            dve.memset(half16[:], 0.5).then_inc(half_ready, 1)
            dve.wait_ge(ident_ready, 1)
            dve.tensor_copy(ident16[:], ident[:]).then_inc(cast16, 1)
            dve.wait_ge(counted, 1)
            dve.tensor_copy(code_u[:], code_i[:]).then_inc(cast16, 1)
            dve.wait_ge(cast16, 2)
            dve.tensor_tensor(codediag[:], ident16[:].unsqueeze(1).to_broadcast([P, NT, P]),
                              code_u[:].bitcast(F16).unsqueeze(2).to_broadcast([P, NT, P]), ALU.mult).then_inc(codediag_ready, 1)
            for t in range(NT):
                if t % XL == 0:
                    dve.wait_ge(x_loaded[t // XL], 16)
                dve.bn_stats(stats[:, t % 2, :], x_all[:, t, :]).then_inc(ln_step, 1)
                dve.wait_ge(ln_step, 2 * t + 1)
                dve.bn_aggr(mv[:, t, :], stats[:, t % 2, :]).then_inc(ln_step, 1)
            dve.wait_ge(ln_step, 2 * NT)
            nstep = [2 * NT]

            def chain(ins):
                nstep[0] += 1
                ins.then_inc(ln_step, 1)
                dve.wait_ge(ln_step, nstep[0])
            chain(dve.tensor_scalar(nr[:, 0], mv[:, :, 1], EPS, None, ALU.add))
            dve.wait_ge(rstd_sqrt, 1)
            chain(dve.reciprocal(rstd[:], rstd[:]))
            chain(dve.tensor_tensor(nr[:, 1], rstd[:], rstd[:], ALU.mult))
            chain(dve.tensor_tensor(nr[:, 1], nr[:, 1], nr[:, 0], ALU.mult))
            chain(dve.tensor_scalar(nr[:, 1], nr[:, 1], -0.5, 1.5, ALU.mult, ALU.add))
            chain(dve.tensor_tensor(rstd[:], rstd[:], nr[:, 1], ALU.mult))
            for t in range(NT):
                dve.tensor_scalar(row_all[:, t, :], x_all[:, t, :], mv[:, t, 0:1], rstd[:, t:t + 1],
                                  ALU.subtract, ALU.mult).then_inc(xn_ready, 1)

            def shift(g):
                if not isinstance(g, int):
                    dve.wait_ge(deg_ps, g)
                dve.wait_ge(adj_loaded, g * 16 + 16)
                dve.tensor_scalar(adj_f8[:].bitcast(U32), adj_raw[:].bitcast(U32), 6, None,
                                  ALU.logical_shift_left).then_inc(adj_shifted, 1)

            FOUND = 3

            def extract(t, u):
                b = u % 2
                for q in range(NQ):
                    wait_alone(dve, codes_ready, t * NQ + q + 1)
                    dve.max(best[:, q * K:(q + 1) * K], codes[:, q % 2, :]).then_inc(codes_used, 1)
                wait_alone(dve, codes_used, t * NQ + NQ + 2)
                dve.max(top[:, b, :], best[:]).then_inc(found, 1)
                dve.wait_ge(found, t * FOUND + 1)
                bits = top[:, b, :].bitcast(U16)
                dve.tensor_scalar(idx[:, u, :], bits, float(CODE0), float(CODE0), ALU.max, ALU.subtract).then_inc(idx_ready, 1)
                dve.tensor_scalar(valid[:, b, :], bits, float(CODE0), None, ALU.is_ge).then_inc(found, 1)
                dve.wait_ge(found, t * FOUND + 2)
                dve.tensor_scalar(neg[:, b, :], valid[:, b, :], -NEG, NEG, ALU.mult, ALU.add).then_inc(found, 1)

            SCORED = K + 2

            def score(t, u, g):
                b = u % 2
                dve.wait_ge(gathered[u], g * (K * 16) + K * 16)
                dve.wait_ge(q_ready, t + 1)
                for k in range(K):
                    dve.tensor_tensor_reduce(out=prod[:, k, :], in0=q_sb[:, b, :], in1=nbr[:, u, k, :], scale=1.0, scalar=0.0,
                                             op0=ALU.mult, op1=ALU.add, accum_out=s[:, b, k:k + 1]).then_inc(scored, 1)
                dve.wait_ge(scored, t * SCORED + K)
                dve.tensor_tensor(sv[:], s[:, b, :], valid[:, b, :], ALU.mult).then_inc(scored, 1)
                dve.wait_ge(scored, t * SCORED + K + 1)
                dve.tensor_tensor(sm[:, b, :], sv[:], neg[:, b, :], ALU.add).then_inc(scored, 1)
                dve.wait_ge(scored, t * SCORED + K + 2)
                dve.tensor_reduce(ml[:, b, 0:1], sm[:, b, :], AX.X, ALU.max, negate=True).then_inc(sm_ready, 1)

            shift(0)
            extract(0, 0)
            with dve.Fori(0, NG - 1) as g:
                for u in range(GT):
                    extract(g * GT + u + 1, (u + 1) % GT)
                    if u == GT - 2:
                        shift(g + 1)
                    score(g * GT + u, u, g)
            for u in range(GT):
                t = NT - GT + u
                if t + 1 < NT:
                    extract(t + 1, u + 1)
                score(t, u, NG - 1)

            plan_n = [0]

            def planning(ins):
                plan_n[0] += 1
                ins.then_inc(plan_step, 1)
                dve.wait_ge(plan_step, plan_n[0])
            dve.wait_ge(deg_T, 1)
            dve.tensor_reduce(rounds_f[:, 0:1], psT[0:NT, 0:P], AX.X, ALU.max).then_inc(deg_max, 1)
            dve.wait_ge(deg_row, 1)
            planning(dve.tensor_scalar(rounds_i[:, 0], psT[0:1, P:P + NT], float(K - 1), None, ALU.add))
            planning(dve.tensor_scalar(rounds_i[:, 1], rounds_i[:, 0], K.bit_length() - 1, None, ALU.logical_shift_right))
            r_f = rounds_row
            planning(dve.tensor_copy(r_f[:, 0], rounds_i[:, 1]))
            planning(dve.tensor_scalar(r_f[:, 1], r_f[:, 0], 1.0, None, ALU.is_gt))
            planning(dve.tensor_tensor(r_f[:, 2], r_f[:, 0], r_f[:, 1], ALU.mult))
            planning(dve.memset(r_f[:, 3], 1.0))
            planning(dve.tensor_tensor_scan(r_f[:, 4], r_f[:, 3], r_f[:, 2], 0.0, ALU.mult, ALU.add))
            planning(dve.tensor_tensor(r_f[:, 5], r_f[:, 4], r_f[:, 2], ALU.subtract))
            planning(dve.tensor_copy(sched[:, 0], r_f[:, 2]))
            dve.tensor_copy(sched[:, 1], r_f[:, 5]).then_inc(rounds_known, 1)

            MORE = 3 * NQ + 15

            def more_round(n):
                k = [0]

                def then(ins):
                    k[0] += 1
                    ins.then_inc(more_step, 1)
                    wait_alone(dve, more_step, n * MORE + k[0])
                wait_alone(dve, more_adj, n * 16 + 16)
                dve.tensor_scalar(adj_f8[:, :, 0:P].bitcast(U32), adj_raw[:, :, 0:P].bitcast(U32), 6, None,
                                  ALU.logical_shift_left).then_inc(more_shift, 1)
                flat = prod[:].rearrange("p k c -> p (k c)")
                all_q, below = flat[:, 0:QW], flat[:, QW:2 * QW]
                for q in range(NQ):
                    wait_alone(dve, more_codes, n * NQ + q + 1)
                    then(dve.tensor_copy(all_q, codes[:, q % 2, :]))
                    then(dve.scalar_tensor_tensor(below, all_q, run[:, 5:6], all_q, ALU.is_lt, ALU.mult))
                    then(dve.max(best[:, q * K:(q + 1) * K], below))
                then(dve.max(top[:, 0, :], best[:]))
                bits = top[:, 0, :].bitcast(U16)
                dve.tensor_scalar(idx[:, 0, :], bits, float(CODE0), float(CODE0), ALU.max, ALU.subtract).then_inc(more_idx, 1)
                then(dve.tensor_copy(run[:, 5:6], top[:, 0, K - 1:K]))
                then(dve.tensor_scalar(valid[:, 0, :], bits, float(CODE0), None, ALU.is_ge))
                then(dve.tensor_scalar(neg[:, 0, :], valid[:, 0, :], -NEG, NEG, ALU.mult, ALU.add))
                wait_alone(dve, more_rows, n * (16 * K) + 16 * K)
                wait_alone(dve, more_q, n + 1)
                for j in range(K):
                    ins = dve.tensor_tensor_reduce(out=prod[:, j, :], in0=q_sb[:, 0, :], in1=nbr[:, 0, j, :], scale=1.0, scalar=0.0,
                                                   op0=ALU.mult, op1=ALU.add, accum_out=s[:, 0, j:j + 1])
                then(ins)
                then(dve.tensor_tensor(sv[:], s[:, 0, :], valid[:, 0, :], ALU.mult))
                then(dve.tensor_tensor(sm[:, 0, :], sv[:], neg[:, 0, :], ALU.add))
                then(dve.tensor_reduce(run[:, 6:7], sm[:, 0, :], AX.X, ALU.max))
                then(dve.tensor_tensor(run[:, 7:8], run[:, 6:7], run[:, 0:1], ALU.max))
                then(dve.tensor_scalar(run[:, 2:3], run[:, 7:8], -1.0, None, ALU.mult))
                dve.drain().then_inc(more_m, 1)
                wait_alone(dve, more_p, n * 2 + 2)
                then(dve.tensor_copy(run[:, 0:1], run[:, 7:8]))
                then(dve.scalar_tensor_tensor(run[:, 1:2], run[:, 1:2], run[:, 4:5], run[:, 3:4], ALU.mult, ALU.add))
                wait_alone(dve, more_y, n + 1)
                then(dve.scalar_tensor_tensor(run_y, run_y, run[:, 4:5], psY[:, 0:C], ALU.mult, ALU.add))
                then(dve.drain())
                then(dve.drain())
                dve.drain().then_inc(more_free, 1)
                assert k[0] == MORE, k[0]

            dve.sem_inc(more_free, 1)
            dve.wait_ge(rounds_known, 1)
            with dve.Fori(0, NT) as t:
                r = dve.value_load(sched[0:1, 0, bass.ds(t, 1)], min_val=0, max_val=N // K)
                before = dve.value_load(sched[0:1, 1, bass.ds(t, 1)], min_val=0, max_val=NT * N // K)
                with dve.If(r > 0):
                    dve.memset(run[:, 0:1], NEG)
                    dve.memset(run[:, 1:2], 0.0)
                    dve.memset(run[:, 5:6], 65536.0)
                    dve.memset(run_y, 0.0)
                    dve.drain()
                    with dve.Fori(0, r) as i:
                        more_round(before + i)
                    dve.tensor_copy(y_all[:, bass.ds(t, 1), :].rearrange("p a c -> p (a c)"), run_y)
                    dve.tensor_copy(ml_all[:, bass.ds(t, 1), 1:2].rearrange("p a c -> p (a c)"), run[:, 1:2])
                    dve.drain()

            rl_n = [0]

            def link(ins):
                rl_n[0] += 1
                ins.then_inc(rl_step, 1)
                dve.wait_ge(rl_step, rl_n[0])
            dve.sem_inc(x2_ready, 2)
            dve.sem_inc(xg_free, 2)
            dve.sem_inc(lg_ready, 1)
            dve.wait_ge(route_consts, 4)
            dve.wait_ge(y_used, NT + 1)
            link(dve.memset(zero_rows[:], 0.0))
            link(dve.tensor_copy(iota_f[:], iota_i[:]))
            link(dve.tensor_copy(row0[:, GT, :], iota_f[:, 1, :]))
            link(dve.tensor_scalar(rl[:, 0], ml_all[:, :, 1], 1e-30, None, ALU.max))
            link(dve.reciprocal(rl[:, 1], rl[:, 0]))
            link(dve.tensor_scalar(rl[:, 2], deg_all[:], 1.0, None, ALU.min))
            link(dve.tensor_tensor(rl[:, 0], rl[:, 1], rl[:, 2], ALU.mult))

            ROUTE = 5 * GT + 15

            def row(a, t):
                return a[:, bass.ds(t, 1), :].rearrange("p a c -> p (a c)")

            def route(g, b):
                k = [0]

                def step(ins):
                    k[0] += 1
                    ins.then_inc(ln2_step, 1)
                    wait_alone(dve, ln2_step, g * ROUTE + k[0])
                for u in range(GT):
                    t = g * GT + u
                    wait_alone(dve, yT_ps, t + 1)
                    dve.tensor_scalar(yt[:, u % 2, :], row(y_all, t), rl[:, 0, bass.ds(t, 1)], None, ALU.mult).then_inc(yt_ready, 1)
                for u in range(GT):
                    t = g * GT + u
                    dve.wait_ge(proj_ps, t + 1 + 2)
                    dve.tensor_tensor(row(x_all, t), row(x_all, t), psPr[:, u % 2, 0:C], ALU.add).then_inc(x2_ready, 1)
                    wait_alone(dve, x2_ready, t + 1 + 2)
                    step(dve.bn_stats(st2[:, u, :], row(x_all, t)))
                for u in range(GT):
                    step(dve.bn_aggr(mv2[:, u, :], st2[:, u, :]))
                dve.tensor_scalar(rs2[:, 0], mv2[:, :, 1], EPS, None, ALU.add).then_inc(var_ready, 1)
                dve.wait_ge(std_ready, g + 1)
                step(dve.reciprocal(rs2[:, 2], rs2[:, 1]))
                step(dve.tensor_tensor(rs2[:, 3], rs2[:, 2], rs2[:, 2], ALU.mult))
                step(dve.tensor_tensor(rs2[:, 3], rs2[:, 3], rs2[:, 0], ALU.mult))
                step(dve.tensor_scalar(rs2[:, 3], rs2[:, 3], -0.5, 1.5, ALU.mult, ALU.add))
                step(dve.tensor_tensor(rs2[:, 2], rs2[:, 2], rs2[:, 3], ALU.mult))
                wait_alone(dve, xg_free, g + 1)
                for u in range(GT):
                    t = g * GT + u
                    dve.tensor_scalar(xg[:, b, u, :], row(x_all, t), mv2[:, u, 0:1], rs2[:, 2, u:u + 1],
                                      ALU.subtract, ALU.mult).then_inc(xg_ready, 1)
                wait_alone(dve, lg_done, g * GT + GT + 2)
                dve.tensor_copy(lg[:].rearrange("p u e -> p (u e)"), psL[:, 0:GT * E]).then_inc(lg_ready, 1)
                wait_alone(dve, lg_ready, g + 1 + 1)
                for u in range(GT):
                    step(dve.max(m8[:, u, :], lg[:, u, :]))
                for u in range(GT):
                    step(dve.max_index(i8[:, u, :], m8[:, u, :], lg[:, u, :]))
                step(dve.tensor_copy(ef[:], i8[:, :, 0:2]))
                for c in range(2):
                    step(dve.tensor_tensor(oh[:, c], iota_f[:, 0, :].unsqueeze(1).to_broadcast([P, GT, E]),
                                           ef[:, :, c:c + 1].to_broadcast([P, GT, E]), ALU.is_equal))
                dve.tensor_tensor(oh[:, 2], oh[:, 0], oh[:, 1], ALU.add).then_inc(oh_ready, 1)
                dve.wait_ge(rank_ps, g + 1)
                step(dve.tensor_copy(row0[:, 0, :], row0[:, GT, :]))
                for u in range(GT):
                    step(dve.tensor_tensor(row0[:, u + 1, :], row0[:, u, :], psR[:, 1, u * E:(u + 1) * E], ALU.add))
                step(dve.tensor_tensor(z[:, 0], row0[:, 0:GT, :], psR[:, 0].rearrange("p (u e) -> p u e", e=E), ALU.add))
                for c in range(2):
                    step(dve.tensor_tensor(z[:, 1 + c], oh[:, c], z[:, 0], ALU.mult))
                step(dve.tensor_reduce(posf[:], z[:, 1:3], AX.X, ALU.add))
                dve.tensor_copy(pos[:, b], posf[:]).then_inc(pos_ready, 1)
                step(dve.tensor_copy(pos_all[:, :, bass.ds(g * GT, GT)], posf[:]))
                step(dve.tensor_tensor(d_all[:, bass.ds(g * GT, GT)], m8[:, :, 1], m8[:, :, 0], ALU.subtract))
                assert k[0] == ROUTE, k[0]
            with dve.Fori(0, NG // 2) as g:
                route(g * 2, 0)
                route(g * 2 + 1, 1)

            link(dve.tensor_tensor(plan_f[:, 0], row0[:, GT, :], iota_f[:, 1, :], ALU.subtract))
            link(dve.tensor_scalar(plan_i[:, 0], plan_f[:, 0], float(T - 1), None, ALU.add))
            link(dve.tensor_scalar(plan_i[:, 1], plan_i[:, 0], T.bit_length() - 1, None, ALU.logical_shift_right))
            link(dve.tensor_copy(plan_f[:, 1], plan_i[:, 1]))
            link(dve.tensor_scalar(plan_f[:, 2], plan_f[:, 1], 1.0, None, ALU.max))
            link(dve.tensor_tensor_scan(plan_f[:, 3], ones[:, 0:E], plan_f[:, 2], 0.0, ALU.mult, ALU.add))
            link(dve.tensor_tensor(plan_f[:, 0], plan_f[:, 3], plan_f[:, 2], ALU.subtract))
            link(dve.tensor_copy(plan[:, 0], plan_f[0:1, 2]))
            link(dve.tensor_copy(plan[:, 1], plan_f[0:1, 0]))
            link(dve.tensor_copy(plan[:, 2], row0[0:1, GT, :]))
            link(dve.tensor_copy(plan[:, 3], plan_f[0:1, 3, E - 1:E].to_broadcast([1, E])))
            link(dve.tensor_scalar(plan[:, 4], plan[:, 3], -1.0, float(MAX_TILES + 1), ALU.mult, ALU.add))
            link(dve.tensor_scalar(plan_f[:, 4], plan_f[:, 2], -float(T), float(REGION), ALU.mult, ALU.add))
            link(dve.tensor_copy(tile_f[:, 0], tile_n[:]))
            link(dve.tensor_scalar(tile_f[:, 1], tile_f[:, 0], float(T), None, ALU.mult))
            for e in range(1, E):
                link(dve.tensor_scalar(tile_f[:, 2], tile_f[:, 0], plan_f[0:1, 0, e:e + 1], plan_f[0:1, 4, e - 1:e], ALU.is_ge, ALU.mult))
                link(dve.tensor_tensor(tile_f[:, 1], tile_f[:, 1], tile_f[:, 2], ALU.add))
            link(dve.tensor_copy(out_f[:, 0], pos_all[:]))
            link(dve.tensor_copy(out_f[:, 1], pos_all[:]))
            for e in range(1, E):
                link(dve.tensor_scalar(out_s[:], out_f[:, 0], iota_f[:, 1, e:e + 1], plan_f[:, 4, e - 1:e], ALU.is_ge, ALU.mult))
                link(dve.tensor_tensor(out_f[:, 1], out_f[:, 1], out_s[:], ALU.subtract))
            link(dve.tensor_copy(pos_all[:], out_f[:, 1]))
            dve.tensor_copy(tile_rows[:], tile_f[:, 1]).then_inc(planned, 1)
            dve.wait_ge(d_exp, 1)
            link(dve.tensor_scalar(gates[:, 2], gates[:, 1], 1.0, None, ALU.add))
            link(dve.reciprocal(gates[:, 0], gates[:, 2]))
            link(dve.tensor_tensor(gates[:, 1], gates[:, 1], gates[:, 0], ALU.mult))

            dve.sem_inc(yo_ready, TS)
            dve.sem_inc(yo_stored, 16)
            dve.sem_inc(hl_ready, HC)
            dve.wait_ge(planned, 1)
            dve.wait_ge(b2_loaded, 16)

            def tiles(e):
                count = dve.value_load(plan[0:1, 0, bass.ds(e, 1)], min_val=1, max_val=N // T)
                before = dve.value_load(plan[0:1, 1, bass.ds(e, 1)], min_val=0, max_val=MAX_TILES)
                with dve.Fori(0, count) as i:
                    n = before + i
                    dve.wait_ge(xh_ready, n + 1)
                    dve.tensor_tensor(x_lo[:].rearrange("p k t -> p (k t)"), psX[:], x_hi[:].bitcast(F32).rearrange("p k t -> p (k t)"),
                                      ALU.subtract).then_inc(xl_ready, 1)
                    for hc in range(HC):
                        dve.wait_ge(hf_ready, n * HC + hc + 1 + 4)
                        dve.tensor_copy(h_hi[:, hc, :], h_f[:, hc, :]).then_inc(hh_ready, 1)
                        dve.wait_ge(hh_ready, n * HC + hc + 1)
                        dve.tensor_tensor(h_lo[:, hc, :], h_f[:, hc, :], h_hi[:, hc, :].bitcast(F32), ALU.subtract).then_inc(hl_ready, 1)
                    wait_alone(dve, yo_stored, n * 16 + 16)
                    for q in range(TS):
                        dve.wait_ge(e_ps, n * TS + q + 1)
                        dve.tensor_tensor(y_out[:, q, :], psE[:, q, 0:C], row(b2_rows, e), ALU.add).then_inc(yo_ready, 1)
            with dve.Fori(0, E) as e:
                tiles(e)

            dve.sem_inc(mixed, GT)

            def place(g, b):
                dve.tensor_copy(gpos[:, b], pos_all[:, :, bass.ds(g * GT, GT)]).then_inc(gpos_ready, 1)

            def mix(g, b):
                for u in range(GT):
                    t = g * GT + u
                    wait_alone(dve, results[u], g * 32 + 32)
                    dve.scalar_tensor_tensor(row(x_all, t), e_rows[:, u, 0, :], gates[:, 0, bass.ds(t, 1)], row(x_all, t),
                                             ALU.mult, ALU.add).then_inc(mix_step, 1)
                    wait_alone(dve, mix_step, t + 1)
                    dve.scalar_tensor_tensor(row(x_all, t), e_rows[:, u, 1, :], gates[:, 1, bass.ds(t, 1)], row(x_all, t),
                                             ALU.mult, ALU.add).then_inc(mixed, 1)
            place(0, 0)
            with dve.Fori(0, NG // 2 - 1) as g:
                place(g * 2 + 1, 1)
                mix(g * 2, 0)
                place(g * 2 + 2, 0)
                mix(g * 2 + 1, 1)
            place(NG - 1, 1)
            mix(NG - 2, 0)
            mix(NG - 1, 1)

        @block.tensor
        def _(pe):
            pe.sem_inc(y_ps, GT)
            pe.wait_ge(w_loaded, 80)
            pe.wait_ge(ident_ready, 1)
            for m in range(CC):
                for k in range(CC):
                    last = pe.matmul(psQ[:, m * C:(m + 1) * C], wraw[:, 0, k, m * P:(m + 1) * P], wraw[:, 1, k, :],
                                     start=(k == 0), stop=(k == CC - 1))
            last.then_inc(w_t, 1)
            for m in range(CC):
                for k in range(CC):
                    pe.transpose(psT[:, m * C + k * P:m * C + (k + 1) * P], wraw[:, 2, k, m * P:(m + 1) * P], ident[:])
            pe.transpose(psY[:, 0:E * HC], b1raw[:], ident[0:E * HC, 0:E * HC]).then_inc(w_t, 1)
            pe.wait_ge(half_ready, 1)
            pe.wait_ge(codediag_ready, 1)
            pe.wait_ge(w_sb, 3)

            def code(t, g, u, half):
                if u == 0 and half == 0:
                    wait_alone(pe, adj_shifted, g + 1)
                for q in range(half * NQ // 2, (half + 1) * NQ // 2):
                    wait_alone(pe, codes_used, t * NQ + q + 1)
                    for j in range(QW // P):
                        blk = q * (QW // P) + j
                        last = pe.matmul(codes[:, q % 2, j * P:(j + 1) * P], adj_f8[:].bitcast(F8)[:, blk, u * P:(u + 1) * P],
                                         codediag[:, blk, :], start=True, stop=True)
                    last.then_inc(codes_ready, 1)

            def degree(g, u):
                if u == 0 and not (isinstance(g, int) and g == 0):
                    wait_alone(pe, deg_copied, g)
                for blk in range(NT):
                    last = pe.matmul(psD[:, u:u + 1], adj_f8[:].bitcast(F8)[:, blk, u * P:(u + 1) * P], half16[:],
                                     start=(blk == 0), stop=(blk == NT - 1))
                if u == GT - 1:
                    last.then_inc(deg_ps, 1)

            def query(t):
                pe.wait_ge(xt_ready, t + 1)
                for k in range(CC):
                    last = pe.transpose(psT[:, k * P:(k + 1) * P], xt[:, k * P:(k + 1) * P], ident[:])
                last.then_inc(xT_ps, 1)
                pe.wait_ge(xT_ready, t + 1)
                if not isinstance(t, int) or t > 0:
                    pe.wait_ge(q_ready, t)
                for k in range(CC):
                    last = pe.matmul(psQ[:, 0:C], xT[:, k, :], wqk[:, k, :], start=(k == 0), stop=(k == CC - 1))
                last.then_inc(q_ps, 1)

            def weigh(t, u):
                for k in range(K):
                    pe.wait_ge(diag_ready, t * K + k + 1)
                    if k == 0:
                        pe.wait_ge(y_used, t + 1)
                    last = pe.matmul(psY[:, 0:C], diag[:, u % 2, k, :], nbr[:, u, k, :], start=(k == 0), stop=(k == K - 1))
                last.then_inc(y_ps, 1)

            code(0, 0, 0, 0)
            code(0, 0, 0, 1)
            degree(0, 0)
            code(1, 0, 1, 0)
            query(0)
            with pe.Fori(0, NG - 1) as g:
                for u in range(GT):
                    t = g * GT + u
                    code(t + 1, g + (u + 1) // GT, (u + 1) % GT, 1)
                    degree(g + (u + 1) // GT, (u + 1) % GT)
                    code(t + 2, g + (u + 2) // GT, (u + 2) % GT, 0)
                    query(t + 1)
                    weigh(t, u)
            for u in range(GT):
                t = NT - GT + u
                if t + 1 < NT:
                    code(t + 1, NG - 1, u + 1, 1)
                    degree(NG - 1, u + 1)
                    if t + 2 < NT:
                        code(t + 2, NG - 1, u + 2, 0)
                    query(t + 1)
                weigh(t, u)

            pe.wait_ge(y_used, NT + 1)
            pe.transpose(psT[0:NT, 0:P], deg_all[:], ident[:]).then_inc(deg_T, 1)
            pe.wait_ge(deg_max, 1)
            pe.transpose(psT[0:1, P:P + NT], rounds_f[:, 0:1], ident[0:NT, 0:NT]).then_inc(deg_row, 1)

            def more_round(n):
                wait_alone(pe, more_shift, n + 1)
                for q in range(NQ):
                    if q < 2:
                        wait_alone(pe, more_free, n + 1)
                    else:
                        wait_alone(pe, more_step, n * (3 * NQ + 15) + 3 * (q - 2) + 1)
                    for j in range(QW // P):
                        blk = q * (QW // P) + j
                        last = pe.matmul(codes[:, q % 2, j * P:(j + 1) * P], adj_f8[:].bitcast(F8)[:, blk, 0:P],
                                         codediag[:, blk, :], start=True, stop=True)
                    last.then_inc(more_codes, 1)
                wait_alone(pe, more_xt, n + 1)
                for k in range(CC):
                    last = pe.transpose(psT[:, k * P:(k + 1) * P], xt[:, k * P:(k + 1) * P], ident[:])
                last.then_inc(more_xTps, 1)
                wait_alone(pe, more_xT, n + 1)
                for k in range(CC):
                    last = pe.matmul(psQ[:, 0:C], xT[:, k, :], wqk[:, k, :], start=(k == 0), stop=(k == CC - 1))
                last.then_inc(more_qps, 1)
                wait_alone(pe, more_diag, n * K + K)
                for k in range(K):
                    last = pe.matmul(psY[:, 0:C], diag[:, 0, k, :], nbr[:, 0, k, :], start=(k == 0), stop=(k == K - 1))
                last.then_inc(more_y, 1)

            pe.wait_ge(rounds_known, 1)
            with pe.Fori(0, NT) as t:
                r = pe.value_load(sched[0:1, 0, bass.ds(t, 1)], min_val=0, max_val=N // K)
                before = pe.value_load(sched[0:1, 1, bass.ds(t, 1)], min_val=0, max_val=NT * N // K)
                with pe.If(r > 0):
                    with pe.Fori(0, r) as i:
                        more_round(before + i)

            pe.sem_inc(yT_ps, 2)
            pe.sem_inc(proj_ps, 2)
            pe.sem_inc(lg_done, 2)

            def route(g, b):
                def transposed(t, u):
                    pe.wait_ge(yt_ready, t + 1)
                    for k in range(CC):
                        last = pe.transpose(psYT[:, u % 2, k * P:(k + 1) * P], yt[:, u % 2, k * P:(k + 1) * P], ident[:])
                    last.then_inc(yT_ps, 1)

                def projected(t, u):
                    pe.wait_ge(yT_ready, t + 1)
                    wait_alone(pe, x2_ready, t + 1)
                    for k in range(CC):
                        last = pe.matmul(psPr[:, u % 2, 0:C], yT[:, u % 2, k * P:(k + 1) * P], wvT[:, k, :],
                                         start=(k == 0), stop=(k == CC - 1))
                    last.then_inc(proj_ps, 1)
                transposed(g * GT, 0)
                for u in range(GT):
                    if u + 1 < GT:
                        transposed(g * GT + u + 1, u + 1)
                    projected(g * GT + u, u)

                def rows_transposed(t, u):
                    pe.wait_ge(xg_ready, t + 1)
                    for k in range(CC):
                        last = pe.transpose(psXT[:, u % 2, k * P:(k + 1) * P], xg[:, b, u, k * P:(k + 1) * P], ident[:])
                    last.then_inc(xg_ps, 1)
                rows_transposed(g * GT, 0)
                for u in range(GT):
                    t = g * GT + u
                    if u + 1 < GT:
                        rows_transposed(t + 1, u + 1)
                    pe.wait_ge(xgT_ready, t + 1)
                    if u == 0:
                        wait_alone(pe, lg_ready, g + 1)
                    for k in range(CC):
                        last = pe.matmul(psL[:, u * E:(u + 1) * E], xgT[:, u % 2, k * P:(k + 1) * P], wr[:, k, :],
                                         start=(k == 0), stop=(k == CC - 1))
                    last.then_inc(lg_done, 1)
                pe.wait_ge(oh_ready, g + 1)
                both = oh[:, 2].rearrange("p u e -> p (u e)")
                pe.matmul(psR[:, 0], tri[:], both, start=True, stop=True)
                pe.matmul(psR[:, 1], ones[:], both, start=True, stop=True).then_inc(rank_ps, 1)
            pe.wait_ge(route_consts, 4)
            with pe.Fori(0, NG // 2) as g:
                route(g * 2, 0)
                route(g * 2 + 1, 1)

            pe.sem_inc(w_used, 2)
            pe.sem_inc(x_ps, 1)
            pe.wait_ge(planned, 1)
            LAG = 3

            def tiles(e, b):
                wait_alone(pe, w_split, e * 2 + 2 + 2)
                count = pe.value_load(plan[0:1, 0, bass.ds(e, 1)], min_val=1, max_val=N // T)
                before = pe.value_load(plan[0:1, 1, bass.ds(e, 1)], min_val=0, max_val=MAX_TILES)
                with pe.Fori(0, count) as i:
                    n = before + i
                    wait_alone(pe, xin_loaded, n * 16 + 16)
                    for q in range(TS):
                        for k in range(CC):
                            last = pe.transpose(psX[:, k * T + q * P:k * T + (q + 1) * P], x_in[:, q, k * P:(k + 1) * P], ident[:])
                    last.then_inc(x_ps, 1)
                    wait_alone(pe, xl_ready, n + 1)

                    def first(hc):
                        wait_alone(pe, hf_ready, n * HC + hc + 1)
                        m = slice(hc * P, (hc + 1) * P)
                        for k in range(CC):
                            pe.matmul(psH[:, hc % 4, 0:T], w1_hi[:, b, k, m], x_hi[:, k, :], start=(k == 0), stop=False)
                            pe.matmul(psH[:, hc % 4, 0:T], w1_hi[:, b, k, m], x_lo[:, k, :], start=False, stop=False)
                            last = pe.matmul(psH[:, hc % 4, 0:T], w1_lo[:, b, k, m], x_hi[:, k, :], start=False, stop=(k == CC - 1))
                        last.then_inc(h_ps, 1)

                    def second(hc):
                        wait_alone(pe, hl_ready, n * HC + hc + 1 + HC)
                        if hc == 0:
                            wait_alone(pe, yo_ready, n * TS + TS)
                        for q in range(TS):
                            m = slice(q * P, (q + 1) * P)
                            pe.matmul(psE[:, q, 0:C], h_hi[:, hc, m], w2_hi[:, b, hc, :], start=(hc == 0), stop=False)
                            pe.matmul(psE[:, q, 0:C], h_hi[:, hc, m], w2_lo[:, b, hc, :], start=False, stop=False)
                            last = pe.matmul(psE[:, q, 0:C], h_lo[:, hc, m], w2_hi[:, b, hc, :], start=False, stop=(hc == HC - 1))
                            if hc == HC - 1:
                                last.then_inc(e_ps, 1)
                    for hc in range(HC + LAG):
                        if hc < HC:
                            first(hc)
                        if hc >= LAG:
                            second(hc - LAG)
                pe.drain().then_inc(w_used, 1)
            with pe.Fori(0, E // 2) as e:
                tiles(e * 2, 0)
                tiles(e * 2 + 1, 1)

        @block.scalar
        def _(act):
            act.sem_inc(y_used, 1)
            act.wait_ge(ln_step, 2 * NT + 1)
            act.activation(rstd[:], nr[:, 0], ACT.Sqrt).then_inc(rstd_sqrt, 1)
            act.wait_ge(w_t, 2)
            act.copy(wqk[:].rearrange("p k c -> p (k c)"), psQ[:]).then_inc(w_sb, 1)
            act.copy(wvT[:].rearrange("p k c -> p (k c)"), psT[:]).then_inc(w_sb, 1)
            act.copy(b1T[:], psY[:, 0:E * HC]).then_inc(w_sb, 1)

            def query(t, b):
                act.copy(xt[:], row_all[:, bass.ds(t, 1), :].rearrange("p a c -> p (a c)")).then_inc(xt_ready, 1)
                act.wait_ge(xT_ps, t + 1)
                act.copy(xT[:].rearrange("p k c -> p (k c)"), psT[:, 0:C]).then_inc(xT_ready, 1)
                act.wait_ge(q_ps, t + 1)
                act.wait_ge(sm_ready, t + 1)
                act.copy(q_sb[:, b, :], psQ[:, 0:C]).then_inc(q_ready, 1)

            def weigh(t, b):
                act.wait_ge(sm_ready, t + 1 + 2)
                act.activation(p[:, b, :], sm[:, b, :], ACT.Exp, bias=ml[:, b, 0:1], accum_out=ml[:, b, 1:2]).then_inc(p_ready, 1)
                act.wait_ge(p_ready, t + 1)
                for k in range(K):
                    act.activation(diag[:, b, k, :], ident[:], ACT.Copy, scale=p[:, b, k:k + 1]).then_inc(diag_ready, 1)
                act.copy(ml_all[:, bass.ds(t, 1), :].rearrange("p a c -> p (a c)"), ml[:, b, :])
                act.wait_ge(y_ps, t + 1 + GT)
                act.copy(y_all[:, bass.ds(t, 1), :].rearrange("p a c -> p (a c)"), psY[:, 0:C]).then_inc(y_used, 1)

            def degrees(g):
                act.wait_ge(deg_ps, g + 1)
                act.copy(deg_all[:, bass.ds(g * GT, GT)], psD[:, 0:GT]).then_inc(deg_copied, 1)

            act.wait_ge(xn_ready, NT)
            query(0, 0)
            with act.Fori(0, NG - 1) as g:
                for u in range(GT):
                    query(g * GT + u + 1, (u + 1) % 2)
                    if u == GT - 2:
                        degrees(g)
                    weigh(g * GT + u, u % 2)
            for u in range(GT):
                t = NT - GT + u
                if t + 1 < NT:
                    query(t + 1, (t + 1) % 2)
                if u == GT - 2:
                    degrees(NG - 1)
                weigh(t, t % 2)

            def more_round(t, n):
                wait_alone(act, more_free, n + 1)
                act.copy(xt[:], row_all[:, bass.ds(t, 1), :].rearrange("p a c -> p (a c)")).then_inc(more_xt, 1)
                wait_alone(act, more_xTps, n + 1)
                act.copy(xT[:].rearrange("p k c -> p (k c)"), psT[:, 0:C]).then_inc(more_xT, 1)
                wait_alone(act, more_qps, n + 1)
                act.copy(q_sb[:, 0, :], psQ[:, 0:C]).then_inc(more_q, 1)
                wait_alone(act, more_m, n + 1)
                act.activation(p[:, 0, :], sm[:, 0, :], ACT.Exp, bias=run[:, 2:3], accum_out=run[:, 3:4]).then_inc(more_p, 1)
                act.activation(run[:, 4:5], run[:, 0:1], ACT.Exp, bias=run[:, 2:3]).then_inc(more_p, 1)
                wait_alone(act, more_p, n * 2 + 2)
                for k in range(K):
                    act.activation(diag[:, 0, k, :], ident[:], ACT.Copy, scale=p[:, 0, k:k + 1]).then_inc(more_diag, 1)
            act.wait_ge(rounds_known, 1)
            with act.Fori(0, NT) as t:
                r = act.value_load(sched[0:1, 0, bass.ds(t, 1)], min_val=0, max_val=N // K)
                before = act.value_load(sched[0:1, 1, bass.ds(t, 1)], min_val=0, max_val=NT * N // K)
                with act.If(r > 0):
                    with act.Fori(0, r) as i:
                        more_round(t, before + i)

            def route(g):
                for u in range(GT):
                    t = g * GT + u
                    act.wait_ge(yT_ps, t + 1 + 2)
                    wait_alone(act, proj_ps, t + 1)
                    act.copy(yT[:, u % 2, :], psYT[:, u % 2, 0:C]).then_inc(yT_ready, 1)
                act.wait_ge(var_ready, g + 1)
                act.activation(rs2[:, 1], rs2[:, 0], ACT.Sqrt).then_inc(std_ready, 1)
                for u in range(GT):
                    t = g * GT + u
                    act.wait_ge(xg_ps, t + 1)
                    wait_alone(act, lg_done, t + 1)
                    act.copy(xgT[:, u % 2, :], psXT[:, u % 2, 0:C]).then_inc(xgT_ready, 1)
            with act.Fori(0, NG) as g:
                route(g)
            act.wait_ge(planned, 1)
            act.activation(gates[:, 1], d_all[:], ACT.Exp).then_inc(d_exp, 1)

            act.sem_inc(hf_ready, 4)

            def tiles(e, b):
                act.copy(b1e[:, b, :], b1T[:, bass.ds(e * HC, HC)]).then_inc(b1_moved, 1)
                wait_alone(act, b1_moved, e + 1)
                count = act.value_load(plan[0:1, 0, bass.ds(e, 1)], min_val=1, max_val=N // T)
                before = act.value_load(plan[0:1, 1, bass.ds(e, 1)], min_val=0, max_val=MAX_TILES)
                with act.Fori(0, count) as i:
                    n = before + i
                    act.wait_ge(x_ps, n + 1 + 1)
                    act.copy(x_hi[:].rearrange("p k t -> p (k t)"), psX[:]).then_inc(xh_ready, 1)
                    for hc in range(HC):
                        wait_alone(act, hl_ready, n * HC + hc + 1)
                        act.wait_ge(h_ps, n * HC + hc + 1)
                        act.activation(h_f[:, hc, :], psH[:, hc % 4, 0:T], ACT.Relu, bias=b1e[:, b, hc:hc + 1]).then_inc(hf_ready, 1)
            with act.Fori(0, E // 2) as e:
                tiles(e * 2, 0)
                tiles(e * 2 + 1, 1)
    return nc


_INS = ["x", "adj", "L0_gnn_Wq", "L0_gnn_Wk", "L0_gnn_Wv", "L0_ffn_W_router", "L0_ffn_W1", "L0_ffn_b1", "L0_ffn_W2", "L0_ffn_b2"]


def kernel(**inputs):
    import concourse.bacc as bacc
    from concourse.bass_utils import run_bass_kernel_spmd

    nc = bacc.Bacc("TRN2", target_bir_lowering=False, num_devices=1)
    arrays, args = {}, []
    for name in _INS:
        a = np.ascontiguousarray(inputs[name])
        arrays[f"in_{name}"] = a
        args.append(nc.dram_tensor(f"in_{name}", a.shape, mybir.dt.from_np(a.dtype), kind="ExternalInput").ap())
    out = nc.dram_tensor("out", (N, C), F32, kind="ExternalOutput").ap()
    attention_and_experts(nc, *args, out)
    r = run_bass_kernel_spmd(nc, [arrays], core_ids=[0])
    return r.results[0]["out"]
```

```python
from contextlib import ExitStack

import numpy as np

import concourse.bass as bass
from concourse import mybir

F32 = mybir.dt.float32
F32R = mybir.dt.float32r
F16 = mybir.dt.float16
F8 = mybir.dt.float8e4
U8 = mybir.dt.uint8
U16 = mybir.dt.uint16
U32 = mybir.dt.uint32
I32 = mybir.dt.int32
ALU = mybir.AluOpType
ACT = mybir.ActivationFunctionType
AX = mybir.AxisListType

P = 128
N = 4096
C = 256
E = 8
H = 1024
EPS = 1e-5
NEG = -1e30
NT = N // P
CC = C // P
HC = H // P
GT = 4
NG = NT // GT
K = 8
QW = 1024
NQ = N // QW
CODE0 = 0x4000
T = 256
TS = T // P
MAX_TILES = 2 * N // T + E
REGION = N + T


def attention_and_experts(nc, x, adj, Wq, Wk, Wv, Wr, W1, b1, W2, b2, out):
    ctx = ExitStack()

    def sb(name, shape, dt, stack=ctx):
        return stack.enter_context(nc.sbuf_tensor(name, shape, dt))

    def ps(name, shape, dt, stack=ctx):
        return stack.enter_context(nc.psum_tensor(name, shape, dt))

    def sem(name):
        return ctx.enter_context(nc.semaphore(name))

    with ctx:
        xn_rows = nc.dram_tensor("xn_rows", (N, C), F32).ap()
        expert_in = nc.dram_tensor("expert_in", (E * REGION, C), F32).ap()
        expert_out = nc.dram_tensor("expert_out", ((MAX_TILES + 1) * T, C), F32).ap()

        x_all = sb("x_all", [P, NT, C], F32)
        ident = sb("ident", [P, P], F32)
        stats = sb("stats", [P, 4, 6], F32)
        mv = sb("mv", [P, NT, 2], F32)
        rstd = sb("rstd", [P, NT], F32)
        nr = sb("nr", [P, 2, NT], F32)
        shift_by = sb("shift_by", [P, NT], F32)
        wvT = sb("wvT", [P, CC, C], F32)
        wr = sb("wr", [P, CC, E], F32)
        b1T = sb("b1T", [P, E * HC], F32)
        b1e = sb("b1e", [P, 2, HC], F32)
        zero_rows = sb("zero_rows", [P, 1, C], F32)
        tri = sb("tri", [P, P], F32)
        ones = sb("ones", [P, P], F32)
        iota_i = sb("iota_i", [P, 2, E], I32)
        iota_f = sb("iota_f", [P, 2, E], F32)
        rl = sb("rl", [P, 3, NT], F32)
        row_end = sb("row_end", [P, E], F32)
        pos_all = sb("pos_all", [P, 2, NT], U32)
        d_all = sb("d_all", [P, NT], F32)
        gates = sb("gates", [P, 3, NT], F32)
        gpos = sb("gpos", [P, 2, 2, GT], U32)
        plan_f = sb("plan_f", [P, 5, E], F32)
        tile_f = sb("tile_f", [1, 3, MAX_TILES], F32)
        tile_n = sb("tile_n", [1, MAX_TILES], I32)
        tile_rows = sb("tile_rows", [1, MAX_TILES], I32)
        plan_i = sb("plan_i", [P, 2, E], I32)
        plan = sb("plan", [1, 5, E], I32)

        sums = ExitStack()
        z_all = sb("z_all", [P, NT, C], F32, sums)
        ml_all = sb("ml_all", [P, NT, 2], F32, sums)
        deg_all = sb("deg_all", [P, NT], F32, sums)
        att = ExitStack()
        row_all = sb("row_all", [P, NT, C], F32, att)
        adj_raw = sb("adj_raw", [P, NT, GT * P], U8, att)
        adj_f8 = sb("adj_f8", [P, NT, GT * P], U8, att)
        codediag = sb("codediag", [P, NT, P], F16, att)
        half16 = sb("half16", [P, 1], F16, att)
        code_i = sb("code_i", [P, NT], I32, att)
        code_u = sb("code_u", [P, NT], U16, att)
        wqk = sb("wqk", [P, CC, C], F32, att)
        b1raw = sb("b1raw", [E * HC, P], F32, att)
        xt = sb("xt", [P, C], F32, att)
        xT = sb("xT", [P, CC, P], F32, att)
        q_sb = sb("q_sb", [P, 2, C], F32, att)
        best = sb("best", [P, NQ * K], F16, att)
        top = sb("top", [P, 2, K], F16, att)
        idx = sb("idx", [P, GT, K], U32, att)
        valid = sb("valid", [P, GT, K], F32, att)
        neg = sb("neg", [P, GT, K], F32, att)
        nbr = sb("nbr", [P, GT, K, C], F32, att)
        wraw = nbr[:, GT - 1, 0:3 * CC, :].rearrange("p (n k) c -> p n k c", n=3)
        yT_sb = sb("yT_sb", [P, CC, P], F32, att)
        prod = sb("prod", [P, K, C], F32, att)
        s = sb("s", [P, 2, K], F32, att)
        sv = sb("sv", [P, K], F32, att)
        sm = sb("sm", [P, 2, K], F32, att)
        ml = sb("ml", [P, 2, 2], F32, att)
        p = sb("p", [P, 2, K], F32, att)
        diag = sb("diag", [P, 2, K, P], F32, att)

        rounds_f = sb("rounds_f", [NT, 2], F32, att)
        ident16 = sb("ident16", [P, P], F16, att)
        rounds_row = sb("rounds_row", [1, 6, NT], F32, att)
        rounds_i = sb("rounds_i", [1, 2, NT], I32, att)
        list_f = sb("list_f", [1, 3, NT], F32, att)
        sched = sb("sched", [1, 4, NT], I32, att)
        run = sb("run", [P, 8], F32, att)
        run_y = diag[:, 1, 0:CC, :].rearrange("p k c -> p (k c)")

        attp = ExitStack()
        codes = ps("codes", [P, 2, QW], F32, attp)
        psT = ps("psT", [P, 512], F32, attp)
        psQ = ps("psQ", [P, 512], F32, attp)
        psY = ps("psY", [P, 512], F32, attp)
        psD = ps("psD", [P, 512], F32, attp)
        attp.close()
        att.close()

        st2 = sb("st2", [P, GT, 6], F32, sums)
        mv2 = sb("mv2", [P, GT, 2], F32, sums)
        xg = sb("xg", [P, 2, GT, C], F32, sums)
        xgT = sb("xgT", [P, 2, C], F32, sums)
        lg = sb("lg", [P, 2, NT, E], F32, sums)
        m12 = sb("m12", [P, 2, NT], F32, sums)
        e12 = sb("e12", [P, NT], F32, sums)
        cand = sb("cand", [P, NT, E], F32, sums)
        oh = sb("oh", [P, 3, NT, E], F32, sums)
        same_e = sb("same_e", [P, E, NT], F32, sums)
        cnt = sb("cnt", [P, 3, E, NT], F32, sums)
        z = sb("z", [P, 2, NT, E], F32, sums)
        posf = sb("posf", [P, 2, NT], F32, sums)
        out_f = sb("out_f", [P, 2, 2, NT], F32, sums)
        out_s = sb("out_s", [P, 2, NT], F32, sums)
        pos = sb("pos", [P, 2, 2, GT], U32, sums)
        midp = ExitStack()
        psXT = ps("psXT", [P, 2, 512], F32, midp)
        psL = ps("psL", [P, 512], F32, midp)
        psR = ps("psR", [P, 2, NT * E], F32, midp)
        midp.close()

        ffn = ExitStack()
        w1_raw = sb("w1_raw", [P, CC, H], F32, ffn)
        w2_raw = sb("w2_raw", [P, HC, C], F32, ffn)
        w1_hi = sb("w1_hi", [P, 2, CC, H], F32R, ffn)
        w1_lo = sb("w1_lo", [P, 2, CC, H], F32R, ffn)
        w2_hi = sb("w2_hi", [P, 2, HC, C], F32R, ffn)
        w2_lo = sb("w2_lo", [P, 2, HC, C], F32R, ffn)
        x_in = sb("x_in", [P, TS, C], F32, ffn)
        x_hi = sb("x_hi", [P, CC, T], F32R, ffn)
        x_lo = sb("x_lo", [P, CC, T], F32R, ffn)
        h_f = z_all[:].rearrange("p t c -> p (t c)")[:, 0:HC * T].rearrange("p (k t) -> p k t", t=T)
        b2_rows = z_all[:].rearrange("p t c -> p (t c)")[:, HC * T:HC * T + E * C].rearrange("p (e c) -> p e c", c=C)
        h_hi = sb("h_hi", [P, HC, T], F32R, ffn)
        h_lo = sb("h_lo", [P, HC, T], F32R, ffn)
        y_out = sb("y_out", [P, TS, C], F32, ffn)
        e_rows = xg[:].rearrange("p c u f -> p u c f")
        ffnp = ExitStack()
        psX = ps("psX", [P, 512], F32, ffnp)
        psH = ps("psH", [P, 4, 512], F32, ffnp)
        psE = ps("psE", [P, TS, 512], F32, ffnp)
        ffnp.close()
        ffn.close()
        sums.close()

        x_loaded = [sem(f"x_loaded{i}") for i in range(4)]
        w_loaded = sem("w_loaded")
        adj_loaded = sem("adj_loaded")
        xn_stored = sem("xn_stored")
        gathered = [sem(f"gathered{i}") for i in range(GT)]
        passed = {e.engine: sem(f"passed_{n}") for n, e in (("pe", nc.tensor), ("dve", nc.vector), ("pool", nc.gpsimd), ("sp", nc.sync), ("act", nc.scalar))}
        zeroed = sem("zeroed")
        counted = sem("counted")
        ident_ready = sem("ident_ready")
        cast16 = sem("cast16")
        half_ready = sem("half_ready")
        codediag_ready = sem("codediag_ready")
        ln_step = sem("ln_step")
        rstd_sqrt = sem("rstd_sqrt")
        xn_ready = sem("xn_ready")
        w_t = sem("w_t")
        w_sb = sem("w_sb")
        adj_shifted = sem("adj_shifted")
        codes_ready = sem("codes_ready")
        codes_used = sem("codes_used")
        xt_ready = sem("xt_ready")
        xT_ps = sem("xT_ps")
        xT_ready = sem("xT_ready")
        q_ps = sem("q_ps")
        q_ready = sem("q_ready")
        found = sem("found")
        idx_ready = sem("idx_ready")
        scored = sem("scored")
        sm_ready = sem("sm_ready")
        p_ready = sem("p_ready")
        diag_ready = sem("diag_ready")
        y_ps = sem("y_ps")
        y_used = sem("y_used")
        z_ps = sem("z_ps")
        z_copied = sem("z_copied")
        deg_copied = sem("deg_copied")
        out_stored = sem("out_stored")
        deg_T = sem("deg_T"); deg_max = sem("deg_max"); deg_row = sem("deg_row")
        plan_step = sem("plan_step"); rounds_known = sem("rounds_known")
        more_free = sem("more_free"); more_adj = sem("more_adj"); more_shift = sem("more_shift")
        more_codes = sem("more_codes"); more_used = sem("more_used"); more_idx = sem("more_idx")
        more_rows = sem("more_rows"); more_xt = sem("more_xt"); more_xTps = sem("more_xTps")
        more_xT = sem("more_xT"); more_qps = sem("more_qps"); more_q = sem("more_q")
        more_m = sem("more_m"); more_p = sem("more_p"); more_diag = sem("more_diag")
        more_y = sem("more_y"); more_yr = sem("more_yr"); more_yps = sem("more_yps"); more_yT = sem("more_yT"); more_z = sem("more_z"); more_step = sem("more_step"); more_done = sem("more_done")
        route_consts = sem("route_consts"); rl_step = sem("rl_step")
        attention_done = sem("attention_done")
        x2_ready = sem("x2_ready"); ln2_step = sem("ln2_step"); route_step = sem("route_step")
        var_ready = sem("var_ready"); std_ready = sem("std_ready"); norm_ready = sem("norm_ready")
        xg_ready = sem("xg_ready"); xg_ps = sem("xg_ps"); xgT_ready = sem("xgT_ready")
        lg_done = sem("lg_done"); lg_ready = sem("lg_ready"); oh_ready = sem("oh_ready")
        rank_ps = sem("rank_ps"); placed = sem("placed"); xs_ready = sem("xs_ready")
        scattered = [sem("scattered0"), sem("scattered1")]
        planned = sem("planned"); tails_zeroed = sem("tails_zeroed"); d_exp = sem("d_exp")
        rest_zeroed = sem("rest_zeroed"); rest_known = sem("rest_known")
        b2_loaded = sem("b2_loaded"); x_ps = sem("x_ps"); b1_moved = sem("b1_moved")
        w_raw = sem("w_raw"); w_hi = sem("w_hi"); w_split = sem("w_split"); w_used = sem("w_used")
        xin_loaded = sem("xin_loaded"); xin_used = sem("xin_used"); xh_ready = sem("xh_ready"); xl_ready = sem("xl_ready")
        h_ps = sem("h_ps"); hf_ready = sem("hf_ready"); hh_ready = sem("hh_ready"); hl_ready = sem("hl_ready")
        e_ps = sem("e_ps"); yo_ready = sem("yo_ready"); yo_stored = sem("yo_stored")
        results = [sem(f"results{i}") for i in range(4)]
        gpos_ready = sem("gpos_ready"); mixed = sem("mixed"); mix_step = sem("mix_step")

        x_t = x.rearrange("(t p) c -> p t c", p=P)
        out_t = out.rearrange("(t p) c -> p t c", p=P)
        adj_u8 = adj.rearrange("(b p) i -> p b i", p=P)
        XL = NT // 4

        def wait_alone(eng, what, value):
            eng.wait_ge(what, value)
            if not isinstance(value, int):
                eng.sem_inc(passed[eng.engine], 1)

        block = ctx.enter_context(nc.Block())

        @block.sync
        def _(sp):
            for i in range(4):
                sp.dma_start(x_all[:, i * XL:(i + 1) * XL, :], x_t[:, i * XL:(i + 1) * XL, :]).then_inc(x_loaded[i], 16)
                if i == 0:
                    for n, w in enumerate((Wq, Wk, Wv)):
                        sp.dma_start(wraw[:, n], w.rearrange("(k p) c -> p k c", p=P)).then_inc(w_loaded, 16)
                    sp.dma_start(wr[:], Wr.rearrange("(k p) e -> p k e", p=P)).then_inc(w_loaded, 16)
                    sp.dma_start(b1raw[:], b1.rearrange("e (k h) -> (e k) h", h=P)).then_inc(w_loaded, 16)
                    sp.dma_start(adj_raw[:], adj_u8[:, :, 0:GT * P]).then_inc(adj_loaded, 16)
            for i in range(4):
                sp.wait_ge(xn_ready, (i + 1) * XL)
                sp.dma_start(xn_rows.rearrange("(t p) c -> p t c", p=P)[:, i * XL:(i + 1) * XL, :],
                             row_all[:, i * XL:(i + 1) * XL, :]).then_inc(xn_stored, 16)
            with sp.Fori(1, NG) as g:
                wait_alone(sp, adj_shifted, g * 2)
                sp.dma_start(adj_raw[:], adj_u8[:, :, bass.ds(g * (GT * P), GT * P)]).then_inc(adj_loaded, 16)
            sp.wait_ge(rounds_known, 1)
            listed = sp.value_load(sched[0:1, 3, 0:1], min_val=0, max_val=NT)
            with sp.If(listed > 0):
                with sp.Fori(0, listed) as m:
                    t = sp.value_load(sched[0:1, 0, bass.ds(m, 1)], min_val=0, max_val=NT - 1)
                    r = sp.value_load(sched[0:1, 1, bass.ds(m, 1)], min_val=1, max_val=N // K)
                    before = sp.value_load(sched[0:1, 2, bass.ds(m, 1)], min_val=0, max_val=NT * N // K)
                    with sp.Fori(0, r) as i:
                        wait_alone(sp, more_free, before + i + 1)
                        sp.dma_start(adj_raw[:, :, 0:P], adj_u8[:, :, bass.ds(t * P, P)]).then_inc(more_adj, 16)
            sp.wait_ge(norm_ready, 2)
            sp.dma_start(b2_rows.rearrange("p e c -> p (e c)"), b2.rearrange("(a e) c -> a (e c)", a=1).to_broadcast([P, E * C])).then_inc(b2_loaded, 16)
            sp.wait_ge(planned, 1)
            for e in range(E):
                end = sp.value_load(plan[0:1, 2, e:e + 1], min_val=0, max_val=E * REGION - T)
                sp.dma_start(expert_in[bass.ds(end, T), :].rearrange("(s p) c -> p s c", p=P), zero_rows[:].to_broadcast([P, TS, C])).then_inc(tails_zeroed, 16)
            sp.wait_ge(tails_zeroed, E * 16)
            for b in range(2):
                sp.wait_ge(scattered[b], 16 * 2 * GT * (NG // 2))

            def tile_row(n):
                return sp.value_load(tile_rows[0:1, bass.ds(n, 1)], min_val=0, max_val=E * REGION - T)

            def load_tile(n, r):
                wait_alone(sp, x_ps, n + 1)
                sp.dma_start(x_in[:], expert_in[bass.ds(r, T), :].rearrange("(s p) c -> p s c", p=P)).then_inc(xin_loaded, 16)

            def store_tile(n):
                wait_alone(sp, yo_ready, n * TS + TS + TS)
                sp.dma_start(expert_out[bass.ds(n * T, T), :].rearrange("(s p) c -> p s c", p=P), y_out[:]).then_inc(yo_stored, 16)
            total = sp.value_load(plan[0:1, 3, 0:1], min_val=E, max_val=MAX_TILES)
            with sp.Fori(total, MAX_TILES + 1) as n:
                sp.dma_start(expert_out[bass.ds(n * T, T), :].rearrange("(s p) c -> p s c", p=P),
                             zero_rows[:].to_broadcast([P, TS, C])).then_inc(rest_zeroed, 16)
            load_tile(0, 0)
            with sp.Fori(1, total) as n:
                load_tile(n, tile_row(n))
                store_tile(n - 1)
            load_tile(total, 0)
            store_tile(total - 1)
            rest = sp.value_load(plan[0:1, 4, 0:1], min_val=1, max_val=MAX_TILES + 1)
            wait_alone(sp, rest_zeroed, rest * 16)
            sp.sem_inc(rest_known, 1)
            with sp.Fori(0, NG) as g:
                wait_alone(sp, mixed, g * GT + GT + GT)
                sp.dma_start(out_t[:, bass.ds(g * GT, GT), :], x_all[:, bass.ds(g * GT, GT), :]).then_inc(out_stored, 16)
            sp.wait_ge(out_stored, 16 * NG)

        @block.gpsimd
        def _(pool):
            pool.memset(ident[:], 0.0).then_inc(zeroed, 1)
            pool.iota(code_i[:], pattern=[[P, NT]], base=CODE0 - 0x400, channel_multiplier=1).then_inc(counted, 1)
            pool.wait_ge(zeroed, 1)
            pool.affine_select(out=ident[:], in_=ident[:], compare_op=ALU.not_equal, fill=1.0, base=0,
                               pattern=[[-1, P]], channel_multiplier=1).then_inc(ident_ready, 1)
            pool.memset(ones[:], 1.0).then_inc(zeroed, 1)
            pool.iota(iota_i[:, 0, :], pattern=[[1, E]], base=0, channel_multiplier=0).then_inc(route_consts, 1)
            pool.iota(iota_i[:, 1, :], pattern=[[REGION, E]], base=0, channel_multiplier=0).then_inc(route_consts, 1)
            pool.iota(tile_n[:], pattern=[[1, MAX_TILES]], base=0, channel_multiplier=0).then_inc(route_consts, 1)
            pool.wait_ge(zeroed, 2)
            pool.affine_select(out=tri[:], in_=ones[:], compare_op=ALU.is_gt, fill=0.0, base=0,
                               pattern=[[1, P]], channel_multiplier=-1).then_inc(route_consts, 1)
            pool.wait_ge(xn_stored, 64)

            def gather(t, u):
                wait_alone(pool, idx_ready, t + 1)
                wait_alone(pool, y_ps, t + 1)
                for k in range(K):
                    pool.indirect_dma_start(nbr[:, u, k, :], None, xn_rows,
                                            bass.IndirectOffsetOnAxis(ap=idx[:, u, k:k + 1], axis=0)).then_inc(gathered[u], 16)
            with pool.Fori(0, NG) as g:
                for u in range(GT):
                    gather(g * GT + u, u)
            pool.wait_ge(rounds_known, 1)
            listed = pool.value_load(sched[0:1, 3, 0:1], min_val=0, max_val=NT)
            with pool.If(listed > 0):
                with pool.Fori(0, listed) as m:
                    t = pool.value_load(sched[0:1, 0, bass.ds(m, 1)], min_val=0, max_val=NT - 1)
                    r = pool.value_load(sched[0:1, 1, bass.ds(m, 1)], min_val=1, max_val=N // K)
                    before = pool.value_load(sched[0:1, 2, bass.ds(m, 1)], min_val=0, max_val=NT * N // K)
                    with pool.Fori(0, r) as i:
                        wait_alone(pool, more_idx, before + i + 1)
                        for k in range(K):
                            pool.indirect_dma_start(nbr[:, 0, k, :], None, xn_rows,
                                                    bass.IndirectOffsetOnAxis(ap=idx[:, 0, k:k + 1], axis=0)).then_inc(more_rows, 16)

            def split_weights(e, b):
                wait_alone(pool, w_split, e * 2 + 2)
                pool.dma_start(w1_raw[:], W1[bass.ds(e, 1)].rearrange("a (k p) h -> p (a k) h", p=P)).then_inc(w_raw, 16)
                pool.dma_start(w2_raw[:], W2[bass.ds(e, 1)].rearrange("a (k p) c -> p (a k) c", p=P)).then_inc(w_raw, 16)
                wait_alone(pool, w_used, e + 1)
                wait_alone(pool, w_raw, e * 32 + 32)
                pool.tensor_copy(w1_hi[:, b], w1_raw[:]).then_inc(w_hi, 1)
                pool.tensor_copy(w2_hi[:, b], w2_raw[:]).then_inc(w_hi, 1)
                wait_alone(pool, w_hi, e * 2 + 2)
                pool.tensor_tensor(w1_lo[:, b], w1_raw[:], w1_hi[:, b].bitcast(F32), ALU.subtract).then_inc(w_split, 1)
                pool.tensor_tensor(w2_lo[:, b], w2_raw[:], w2_hi[:, b].bitcast(F32), ALU.subtract).then_inc(w_split, 1)
            pool.wait_ge(attention_done, 1)
            pool.sem_inc(w_split, 2)
            split_weights(0, 0)

            def scatter(g, b):
                wait_alone(pool, placed, g + 1)
                wait_alone(pool, xs_ready, g * GT + GT)
                for c in range(2):
                    for u in range(GT):
                        pool.indirect_dma_start(expert_in, bass.IndirectOffsetOnAxis(ap=pos[:, b, c, u:u + 1], axis=0),
                                                xg[:, b, u, :], None).then_inc(scattered[b], 16)
            with pool.Fori(0, NG // 2) as i:
                scatter(i * 2, 0)
                scatter(i * 2 + 1, 1)
            split_weights(1, 1)
            with pool.Fori(1, E // 2) as e:
                split_weights(e * 2, 0)
                split_weights(e * 2 + 1, 1)
            def fetch(g, b):
                wait_alone(pool, gpos_ready, g + 1)
                for u in range(GT):
                    wait_alone(pool, mixed, g * GT + u + 1)
                    for c in range(2):
                        pool.indirect_dma_start(e_rows[:, u, c, :], None, expert_out,
                                                bass.IndirectOffsetOnAxis(ap=gpos[:, b, c, u:u + 1], axis=0)).then_inc(results[u], 16)
            total = pool.value_load(plan[0:1, 3, 0:1], min_val=E, max_val=MAX_TILES)
            wait_alone(pool, yo_stored, total * 16 + 16)
            pool.wait_ge(rest_known, 1)
            with pool.Fori(0, NG // 2) as g:
                fetch(g * 2, 0)
                fetch(g * 2 + 1, 1)

        @block.vector
        def _(dve):
            dve.sem_inc(codes_used, 2)
            dve.sem_inc(sm_ready, 2)
            dve.memset(half16[:], 0.5).then_inc(half_ready, 1)
            dve.wait_ge(ident_ready, 1)
            dve.tensor_copy(ident16[:], ident[:]).then_inc(cast16, 1)
            dve.wait_ge(counted, 1)
            dve.tensor_copy(code_u[:], code_i[:]).then_inc(cast16, 1)
            dve.wait_ge(cast16, 2)
            dve.tensor_tensor(codediag[:], ident16[:].unsqueeze(1).to_broadcast([P, NT, P]),
                              code_u[:].bitcast(F16).unsqueeze(2).to_broadcast([P, NT, P]), ALU.mult).then_inc(codediag_ready, 1)
            for t in range(NT):
                if t % XL == 0:
                    dve.wait_ge(x_loaded[t // XL], 16)
                if t >= 4:
                    dve.wait_ge(ln_step, 2 * t - 4)
                dve.bn_stats(stats[:, t % 4, :], x_all[:, t, :]).then_inc(ln_step, 1)
                if t >= 1:
                    dve.wait_ge(ln_step, max(2 * t - 2, 1))
                    dve.bn_aggr(mv[:, t - 1, :], stats[:, (t - 1) % 4, :]).then_inc(ln_step, 1)
            dve.wait_ge(ln_step, 2 * NT - 1)
            dve.bn_aggr(mv[:, NT - 1, :], stats[:, (NT - 1) % 4, :]).then_inc(ln_step, 1)
            dve.wait_ge(ln_step, 2 * NT)
            nstep = [2 * NT]

            def chain(ins):
                nstep[0] += 1
                ins.then_inc(ln_step, 1)
                dve.wait_ge(ln_step, nstep[0])
            chain(dve.tensor_scalar(nr[:, 0], mv[:, :, 1], EPS, None, ALU.add))
            dve.wait_ge(rstd_sqrt, 1)
            chain(dve.reciprocal(rstd[:], rstd[:]))
            chain(dve.tensor_tensor(nr[:, 1], rstd[:], rstd[:], ALU.mult))
            chain(dve.tensor_tensor(nr[:, 1], nr[:, 1], nr[:, 0], ALU.mult))
            chain(dve.tensor_scalar(nr[:, 1], nr[:, 1], -0.5, 1.5, ALU.mult, ALU.add))
            chain(dve.tensor_tensor(rstd[:], rstd[:], nr[:, 1], ALU.mult))
            for t in range(NT):
                dve.tensor_scalar(row_all[:, t, :], x_all[:, t, :], mv[:, t, 0:1], rstd[:, t:t + 1],
                                  ALU.subtract, ALU.mult).then_inc(xn_ready, 1)

            def shift(g, h):
                wait_alone(dve, adj_loaded, g * 16 + 16)
                cols = slice(h * 2 * P, (h + 1) * 2 * P)
                dve.tensor_scalar(adj_f8[:, :, cols].bitcast(U32), adj_raw[:, :, cols].bitcast(U32), 6, None,
                                  ALU.logical_shift_left).then_inc(adj_shifted, 1)

            FOUND = 3

            def extract(t, u):
                b, v = u % 2, u
                for q in range(NQ):
                    wait_alone(dve, codes_ready, t * NQ + q + 1)
                    dve.max(best[:, q * K:(q + 1) * K], codes[:, q % 2, :]).then_inc(codes_used, 1)
                wait_alone(dve, codes_used, t * NQ + NQ + 2)
                dve.max(top[:, b, :], best[:]).then_inc(found, 1)
                dve.wait_ge(found, t * FOUND + 1)
                bits = top[:, b, :].bitcast(U16)
                dve.tensor_scalar(idx[:, u, :], bits, float(CODE0), float(CODE0), ALU.max, ALU.subtract).then_inc(idx_ready, 1)
                dve.tensor_scalar(valid[:, v, :], bits, float(CODE0), None, ALU.is_ge).then_inc(found, 1)
                dve.wait_ge(found, t * FOUND + 2)
                dve.tensor_scalar(neg[:, v, :], valid[:, v, :], -NEG, NEG, ALU.mult, ALU.add).then_inc(found, 1)

            SCORED = K + 2

            def score(t, u, g):
                b = u % 2
                dve.wait_ge(gathered[u], g * (K * 16) + K * 16)
                dve.wait_ge(q_ready, t + 1)
                for k in range(K):
                    dve.tensor_tensor_reduce(out=prod[:, k, :], in0=q_sb[:, b, :], in1=nbr[:, u, k, :], scale=1.0, scalar=0.0,
                                             op0=ALU.mult, op1=ALU.add, accum_out=s[:, b, k:k + 1]).then_inc(scored, 1)
                dve.wait_ge(scored, t * SCORED + K)
                dve.tensor_tensor(sv[:], s[:, b, :], valid[:, u, :], ALU.mult).then_inc(scored, 1)
                dve.wait_ge(scored, t * SCORED + K + 1)
                dve.tensor_tensor(sm[:, b, :], sv[:], neg[:, u, :], ALU.add).then_inc(scored, 1)
                dve.wait_ge(scored, t * SCORED + K + 2)
                dve.tensor_reduce(ml[:, b, 0:1], sm[:, b, :], AX.X, ALU.max, negate=True).then_inc(sm_ready, 1)

            shift(0, 0)
            shift(0, 1)
            extract(0, 0)
            extract(1, 1)
            with dve.Fori(0, NG - 1) as g:
                for u in range(GT):
                    extract(g * GT + u + 2, (u + 2) % GT)
                    if u % 2 == 0:
                        shift(g + 1, u // 2)
                    score(g * GT + u, u, g)
            for u in range(GT):
                t = NT - GT + u
                if t + 2 < NT:
                    extract(t + 2, u + 2)
                score(t, u, NG - 1)

            plan_n = [0]

            def planning(ins):
                plan_n[0] += 1
                ins.then_inc(plan_step, 1)
                dve.wait_ge(plan_step, plan_n[0])
            dve.wait_ge(route_consts, 4)
            dve.wait_ge(deg_T, 1)
            dve.tensor_reduce(rounds_f[:, 0:1], psT[0:NT, 0:P], AX.X, ALU.max).then_inc(deg_max, 1)
            dve.wait_ge(deg_row, 1)
            planning(dve.tensor_scalar(rounds_i[:, 0], psT[0:1, P:P + NT], float(K - 1), None, ALU.add))
            planning(dve.tensor_scalar(rounds_i[:, 1], rounds_i[:, 0], K.bit_length() - 1, None, ALU.logical_shift_right))
            r_f = rounds_row
            planning(dve.tensor_copy(r_f[:, 0], rounds_i[:, 1]))
            planning(dve.tensor_scalar(r_f[:, 1], r_f[:, 0], 1.0, None, ALU.is_gt))
            planning(dve.tensor_tensor(r_f[:, 2], r_f[:, 0], r_f[:, 1], ALU.mult))
            planning(dve.memset(r_f[:, 3], 1.0))
            planning(dve.tensor_tensor_scan(r_f[:, 4], r_f[:, 3], r_f[:, 2], 0.0, ALU.mult, ALU.add))
            planning(dve.tensor_tensor(r_f[:, 5], r_f[:, 4], r_f[:, 2], ALU.subtract))
            flat = prod[0:1].rearrange("p k c -> p (k c)")
            place = flat[:, 0:NT * NT].rearrange("p (i t) -> p i t", t=NT)
            picked = flat[:, NT * NT:2 * NT * NT].rearrange("p (i t) -> p i t", t=NT)
            planning(dve.tensor_copy(list_f[:, 0], tile_n[:, 0:NT]))
            planning(dve.tensor_tensor_scan(list_f[:, 1], r_f[:, 3], r_f[:, 1], 0.0, ALU.mult, ALU.add))
            planning(dve.tensor_copy(sched[:, 3], list_f[:, 1, NT - 1:NT].to_broadcast([1, NT])))
            planning(dve.tensor_tensor(list_f[:, 1], list_f[:, 1], r_f[:, 1], ALU.subtract))
            planning(dve.tensor_tensor(place, list_f[:, 0].unsqueeze(2).to_broadcast([1, NT, NT]),
                                       list_f[:, 1].unsqueeze(1).to_broadcast([1, NT, NT]), ALU.is_equal))
            planning(dve.tensor_tensor(place, place, r_f[:, 1].unsqueeze(1).to_broadcast([1, NT, NT]), ALU.mult))
            for n, values in enumerate((list_f[:, 0], r_f[:, 2], r_f[:, 5])):
                planning(dve.tensor_tensor(picked, place, values.unsqueeze(1).to_broadcast([1, NT, NT]), ALU.mult))
                planning(dve.tensor_reduce(list_f[:, 2], picked, AX.X, ALU.add))
                planning(dve.tensor_copy(sched[:, n], list_f[:, 2]))
            dve.drain().then_inc(rounds_known, 1)

            MORE = 3 * NQ + 17

            def more_round(t, n):
                k = [0]

                def then(ins):
                    k[0] += 1
                    ins.then_inc(more_step, 1)
                    wait_alone(dve, more_step, n * MORE + k[0])
                wait_alone(dve, more_adj, n * 16 + 16)
                dve.tensor_scalar(adj_f8[:, :, 0:P].bitcast(U32), adj_raw[:, :, 0:P].bitcast(U32), 6, None,
                                  ALU.logical_shift_left).then_inc(more_shift, 1)
                flat = prod[:].rearrange("p k c -> p (k c)")
                all_q, below = flat[:, 0:QW], flat[:, QW:2 * QW]
                for q in range(NQ):
                    wait_alone(dve, more_codes, n * NQ + q + 1)
                    then(dve.tensor_copy(all_q, codes[:, q % 2, :]))
                    then(dve.scalar_tensor_tensor(below, all_q, run[:, 5:6], all_q, ALU.is_lt, ALU.mult))
                    then(dve.max(best[:, q * K:(q + 1) * K], below))
                then(dve.max(top[:, 0, :], best[:]))
                bits = top[:, 0, :].bitcast(U16)
                dve.tensor_scalar(idx[:, 0, :], bits, float(CODE0), float(CODE0), ALU.max, ALU.subtract).then_inc(more_idx, 1)
                then(dve.tensor_copy(run[:, 5:6], top[:, 0, K - 1:K]))
                then(dve.tensor_scalar(valid[:, 0, :], bits, float(CODE0), None, ALU.is_ge))
                then(dve.tensor_scalar(neg[:, 0, :], valid[:, 0, :], -NEG, NEG, ALU.mult, ALU.add))
                wait_alone(dve, more_rows, n * (16 * K) + 16 * K)
                wait_alone(dve, more_q, n + 1)
                for j in range(K):
                    ins = dve.tensor_tensor_reduce(out=prod[:, j, :], in0=q_sb[:, 0, :], in1=nbr[:, 0, j, :], scale=1.0, scalar=0.0,
                                                   op0=ALU.mult, op1=ALU.add, accum_out=s[:, 0, j:j + 1])
                then(ins)
                then(dve.tensor_tensor(sv[:], s[:, 0, :], valid[:, 0, :], ALU.mult))
                then(dve.tensor_tensor(sm[:, 0, :], sv[:], neg[:, 0, :], ALU.add))
                then(dve.tensor_reduce(run[:, 6:7], sm[:, 0, :], AX.X, ALU.max))
                then(dve.tensor_tensor(run[:, 7:8], run[:, 6:7], run[:, 0:1], ALU.max))
                then(dve.tensor_scalar(run[:, 2:3], run[:, 7:8], -1.0, None, ALU.mult))
                dve.drain().then_inc(more_m, 1)
                wait_alone(dve, more_p, n * 2 + 2)
                then(dve.tensor_copy(run[:, 0:1], run[:, 7:8]))
                then(dve.scalar_tensor_tensor(run[:, 1:2], run[:, 1:2], run[:, 4:5], run[:, 3:4], ALU.mult, ALU.add))
                wait_alone(dve, more_y, n + 1)
                then(dve.scalar_tensor_tensor(run_y, run_y, run[:, 4:5], psY[:, 0:C], ALU.mult, ALU.add))
                then(dve.drain())
                then(dve.drain())
                dve.drain().then_inc(more_yr, 1)
                wait_alone(dve, more_z, n + 1)
                then(dve.tensor_copy(z_all[:, bass.ds(t, 1), :].rearrange("p a c -> p (a c)"), psQ[:, C:2 * C]))
                then(dve.tensor_copy(ml_all[:, bass.ds(t, 1), 1:2].rearrange("p a c -> p (a c)"), run[:, 1:2]))
                dve.drain().then_inc(more_free, 1)
                assert k[0] == MORE, k[0]

            dve.sem_inc(more_free, 1)
            dve.wait_ge(rounds_known, 1)
            listed = dve.value_load(sched[0:1, 3, 0:1], min_val=0, max_val=NT)
            with dve.If(listed > 0):
                with dve.Fori(0, listed) as m:
                    t = dve.value_load(sched[0:1, 0, bass.ds(m, 1)], min_val=0, max_val=NT - 1)
                    r = dve.value_load(sched[0:1, 1, bass.ds(m, 1)], min_val=1, max_val=N // K)
                    before = dve.value_load(sched[0:1, 2, bass.ds(m, 1)], min_val=0, max_val=NT * N // K)
                    dve.memset(run[:, 0:1], NEG)
                    dve.memset(run[:, 1:2], 0.0)
                    dve.memset(run[:, 5:6], 65536.0)
                    dve.memset(run_y, 0.0)
                    dve.drain()
                    with dve.Fori(0, r) as i:
                        more_round(t, before + i)

            rl_n = [0]

            def link(ins):
                rl_n[0] += 1
                ins.then_inc(rl_step, 1)
                dve.wait_ge(rl_step, rl_n[0])

            def row(a, t):
                return a[:, bass.ds(t, 1), :].rearrange("p a c -> p (a c)")
            dve.wait_ge(z_copied, NT)
            dve.drain().then_inc(attention_done, 1)
            link(dve.memset(zero_rows[:], 0.0))
            link(dve.tensor_copy(iota_f[:], iota_i[:]))
            link(dve.memset(same_e[:], 1.0))
            link(dve.memset(same_e[:, :, 0:1], 0.0))
            link(dve.tensor_scalar(rl[:, 0], ml_all[:, :, 1], 1e-30, None, ALU.max))
            link(dve.reciprocal(rl[:, 1], rl[:, 0]))
            link(dve.tensor_scalar(rl[:, 2], deg_all[:], 1.0, None, ALU.min))
            link(dve.tensor_tensor(rl[:, 0], rl[:, 1], rl[:, 2], ALU.mult))

            def add_and_measure(g):
                for u in range(GT):
                    t = g * GT + u
                    dve.scalar_tensor_tensor(row(x_all, t), row(z_all, t), rl[:, 0, bass.ds(t, 1)], row(x_all, t),
                                             ALU.mult, ALU.add).then_inc(x2_ready, 1)
                for u in range(GT):
                    wait_alone(dve, x2_ready, g * GT + u + 1)
                    dve.bn_stats(st2[:, u, :], row(x_all, g * GT + u)).then_inc(ln2_step, 1)
                for u in range(GT):
                    wait_alone(dve, ln2_step, g * (2 * GT + 1) + u + 1)
                    dve.bn_aggr(mv2[:, u, :], st2[:, u, :]).then_inc(ln2_step, 1)
                wait_alone(dve, ln2_step, g * (2 * GT + 1) + 2 * GT)
                dve.tensor_copy(mv[:, bass.ds(g * GT, GT), :], mv2[:]).then_inc(ln2_step, 1)
                wait_alone(dve, ln2_step, g * (2 * GT + 1) + 2 * GT + 1)

            for half in range(2):
                w = slice(half * NT // 2, (half + 1) * NT // 2)
                with dve.Fori(half * NG // 2, (half + 1) * NG // 2) as g:
                    add_and_measure(g)
                dve.tensor_scalar(nr[:, 0, w], mv[:, w, 1], EPS, None, ALU.add).then_inc(var_ready, 1)
                dve.wait_ge(std_ready, half + 1)
                link(dve.reciprocal(rstd[:, w], rstd[:, w]))
                link(dve.tensor_tensor(nr[:, 1, w], rstd[:, w], rstd[:, w], ALU.mult))
                link(dve.tensor_tensor(nr[:, 1, w], nr[:, 1, w], nr[:, 0, w], ALU.mult))
                link(dve.tensor_scalar(nr[:, 1, w], nr[:, 1, w], -0.5, 1.5, ALU.mult, ALU.add))
                link(dve.tensor_tensor(rstd[:, w], rstd[:, w], nr[:, 1, w], ALU.mult))
                link(dve.tensor_tensor(nr[:, 1, w], mv[:, w, 0], rstd[:, w], ALU.mult))
                dve.tensor_scalar(shift_by[:, w], nr[:, 1, w], -1.0, None, ALU.mult).then_inc(norm_ready, 1)

            def by_expert(a):
                return a.unsqueeze(1).to_broadcast([P, NT, E])

            def by_token(a):
                return a.unsqueeze(2).to_broadcast([P, NT, E])
            dve.wait_ge(lg_ready, NG + 1)
            for c in range(2):
                link(dve.tensor_reduce(m12[:, c], lg[:, c], AX.X, ALU.max))
                link(dve.tensor_tensor(cand[:], lg[:, c], by_token(m12[:, c]), ALU.is_equal))
                link(dve.scalar_tensor_tensor(cand[:], cand[:], -float(E), by_expert(iota_f[:, 0]), ALU.mult, ALU.add))
                link(dve.tensor_reduce(e12[:], cand[:], AX.X, ALU.min))
                link(dve.tensor_tensor(oh[:, c], cand[:], by_token(e12[:]), ALU.is_equal))
                if c == 0:
                    link(dve.scalar_tensor_tensor(lg[:, 1], oh[:, 0], NEG, lg[:, 0], ALU.mult, ALU.add))
            dve.tensor_tensor(oh[:, 2], oh[:, 0], oh[:, 1], ALU.add).then_inc(oh_ready, 1)
            link(dve.tensor_tensor(d_all[:], m12[:, 1], m12[:, 0], ALU.subtract))
            dve.wait_ge(rank_ps, 1)
            link(dve.tensor_copy(cnt[:, 0], psR[:, 1].rearrange("p (t e) -> p e t", e=E)))
            link(dve.tensor_tensor_scan(cnt[:, 1].rearrange("p e t -> p (e t)"), same_e[:].rearrange("p e t -> p (e t)"),
                                        cnt[:, 0].rearrange("p e t -> p (e t)"), 0.0, ALU.mult, ALU.add))
            link(dve.tensor_tensor(row_end[:], cnt[:, 1, :, NT - 1], iota_f[:, 1], ALU.add))
            link(dve.tensor_tensor(cnt[:, 2], cnt[:, 1], cnt[:, 0], ALU.subtract))
            link(dve.tensor_tensor(cand[:], cnt[:, 2].rearrange("p e t -> p t e"), psR[:, 0].rearrange("p (t e) -> p t e", e=E), ALU.add))
            link(dve.tensor_tensor(cand[:], cand[:], by_expert(iota_f[:, 1]), ALU.add))
            for c in range(2):
                link(dve.tensor_tensor(z[:, c], oh[:, c], cand[:], ALU.mult))
            link(dve.tensor_reduce(posf[:], z[:], AX.X, ALU.add))

            def place_rows(g, i, b):
                if not isinstance(i, int):
                    wait_alone(dve, scattered[b], i * (32 * GT))
                dve.tensor_copy(pos[:, b], posf[:, :, bass.ds(g * GT, GT)]).then_inc(placed, 1)
            place_rows(0, 0, 0)
            place_rows(1, 0, 1)

            link(dve.tensor_tensor(plan_f[:, 0], row_end[:], iota_f[:, 1, :], ALU.subtract))
            link(dve.tensor_scalar(plan_i[:, 0], plan_f[:, 0], float(T - 1), None, ALU.add))
            link(dve.tensor_scalar(plan_i[:, 1], plan_i[:, 0], T.bit_length() - 1, None, ALU.logical_shift_right))
            link(dve.tensor_copy(plan_f[:, 1], plan_i[:, 1]))
            link(dve.tensor_scalar(plan_f[:, 2], plan_f[:, 1], 1.0, None, ALU.max))
            link(dve.tensor_tensor_scan(plan_f[:, 3], ones[:, 0:E], plan_f[:, 2], 0.0, ALU.mult, ALU.add))
            link(dve.tensor_tensor(plan_f[:, 0], plan_f[:, 3], plan_f[:, 2], ALU.subtract))
            link(dve.tensor_copy(plan[:, 0], plan_f[0:1, 2]))
            link(dve.tensor_copy(plan[:, 1], plan_f[0:1, 0]))
            link(dve.tensor_copy(plan[:, 2], row_end[0:1, :]))
            link(dve.tensor_copy(plan[:, 3], plan_f[0:1, 3, E - 1:E].to_broadcast([1, E])))
            link(dve.tensor_scalar(plan[:, 4], plan[:, 3], -1.0, float(MAX_TILES + 1), ALU.mult, ALU.add))
            link(dve.tensor_scalar(plan_f[:, 4], plan_f[:, 2], -float(T), float(REGION), ALU.mult, ALU.add))
            link(dve.tensor_copy(tile_f[:, 0], tile_n[:]))
            link(dve.tensor_scalar(tile_f[:, 1], tile_f[:, 0], float(T), None, ALU.mult))
            for e in range(1, E):
                link(dve.tensor_scalar(tile_f[:, 2], tile_f[:, 0], plan_f[0:1, 0, e:e + 1], plan_f[0:1, 4, e - 1:e], ALU.is_ge, ALU.mult))
                link(dve.tensor_tensor(tile_f[:, 1], tile_f[:, 1], tile_f[:, 2], ALU.add))
            link(dve.tensor_copy(out_f[:, 0], posf[:]))
            link(dve.tensor_copy(out_f[:, 1], posf[:]))
            for e in range(1, E):
                link(dve.tensor_scalar(out_s[:], out_f[:, 0], iota_f[:, 1, e:e + 1], plan_f[:, 4, e - 1:e], ALU.is_ge, ALU.mult))
                link(dve.tensor_tensor(out_f[:, 1], out_f[:, 1], out_s[:], ALU.subtract))
            link(dve.tensor_copy(pos_all[:], out_f[:, 1]))
            dve.tensor_copy(tile_rows[:], tile_f[:, 1]).then_inc(planned, 1)
            with dve.Fori(1, NG // 2) as i:
                place_rows(i * 2, i, 0)
                place_rows(i * 2 + 1, i, 1)
            dve.wait_ge(d_exp, 1)
            link(dve.tensor_scalar(gates[:, 2], gates[:, 1], 1.0, None, ALU.add))
            link(dve.reciprocal(gates[:, 0], gates[:, 2]))
            link(dve.tensor_tensor(gates[:, 1], gates[:, 1], gates[:, 0], ALU.mult))

            dve.sem_inc(yo_ready, TS)
            dve.sem_inc(yo_stored, 16)
            dve.sem_inc(hl_ready, HC)
            dve.wait_ge(planned, 1)
            dve.wait_ge(b2_loaded, 16)

            def rest_of_x(n):
                dve.wait_ge(xh_ready, n + 1)
                dve.tensor_tensor(x_lo[:].rearrange("p k t -> p (k t)"), psX[:], x_hi[:].bitcast(F32).rearrange("p k t -> p (k t)"),
                                  ALU.subtract).then_inc(xl_ready, 1)

            def tiles(e):
                count = dve.value_load(plan[0:1, 0, bass.ds(e, 1)], min_val=1, max_val=N // T)
                before = dve.value_load(plan[0:1, 1, bass.ds(e, 1)], min_val=0, max_val=MAX_TILES)
                with dve.Fori(0, count) as i:
                    n = before + i
                    for hc in range(HC):
                        dve.wait_ge(hf_ready, n * HC + hc + 1 + 4)
                        dve.tensor_copy(h_hi[:, hc, :], h_f[:, hc, :]).then_inc(hh_ready, 1)
                        dve.wait_ge(hh_ready, n * HC + hc + 1)
                        dve.tensor_tensor(h_lo[:, hc, :], h_f[:, hc, :], h_hi[:, hc, :].bitcast(F32), ALU.subtract).then_inc(hl_ready, 1)
                    rest_of_x(n + 1)
                    wait_alone(dve, yo_stored, n * 16 + 16)
                    for q in range(TS):
                        dve.wait_ge(e_ps, n * TS + q + 1)
                        dve.tensor_tensor(y_out[:, q, :], psE[:, q, 0:C], row(b2_rows, e), ALU.add).then_inc(yo_ready, 1)
            rest_of_x(0)
            with dve.Fori(0, E) as e:
                tiles(e)

            dve.sem_inc(mixed, GT)

            def place(g, b):
                dve.tensor_copy(gpos[:, b], pos_all[:, :, bass.ds(g * GT, GT)]).then_inc(gpos_ready, 1)

            def mix(g, b):
                for u in range(GT):
                    t = g * GT + u
                    wait_alone(dve, results[u], g * 32 + 32)
                    dve.scalar_tensor_tensor(row(x_all, t), e_rows[:, u, 0, :], gates[:, 0, bass.ds(t, 1)], row(x_all, t),
                                             ALU.mult, ALU.add).then_inc(mix_step, 1)
                    wait_alone(dve, mix_step, t + 1)
                    dve.scalar_tensor_tensor(row(x_all, t), e_rows[:, u, 1, :], gates[:, 1, bass.ds(t, 1)], row(x_all, t),
                                             ALU.mult, ALU.add).then_inc(mixed, 1)
            place(0, 0)
            with dve.Fori(0, NG // 2 - 1) as g:
                place(g * 2 + 1, 1)
                mix(g * 2, 0)
                place(g * 2 + 2, 0)
                mix(g * 2 + 1, 1)
            place(NG - 1, 1)
            mix(NG - 2, 0)
            mix(NG - 1, 1)

        @block.tensor
        def _(pe):
            pe.wait_ge(w_loaded, 80)
            pe.wait_ge(ident_ready, 1)
            for m in range(CC):
                for k in range(CC):
                    last = pe.matmul(psQ[:, m * C:(m + 1) * C], wraw[:, 0, k, m * P:(m + 1) * P], wraw[:, 1, k, :],
                                     start=(k == 0), stop=(k == CC - 1))
            last.then_inc(w_t, 1)
            for m in range(CC):
                for k in range(CC):
                    pe.transpose(psT[:, m * C + k * P:m * C + (k + 1) * P], wraw[:, 2, k, m * P:(m + 1) * P], ident[:])
            pe.transpose(psY[:, 0:E * HC], b1raw[:], ident[0:E * HC, 0:E * HC]).then_inc(w_t, 1)
            pe.wait_ge(half_ready, 1)
            pe.wait_ge(codediag_ready, 1)
            pe.wait_ge(w_sb, 3)
            pe.sem_inc(y_ps, GT)

            def code(t, u, half):
                for q in range(half * NQ // 2, (half + 1) * NQ // 2):
                    wait_alone(pe, codes_used, t * NQ + q + 1)
                    for j in range(QW // P):
                        blk = q * (QW // P) + j
                        last = pe.matmul(codes[:, q % 2, j * P:(j + 1) * P], adj_f8[:].bitcast(F8)[:, blk, u * P:(u + 1) * P],
                                         codediag[:, blk, :], start=True, stop=True)
                    last.then_inc(codes_ready, 1)

            def degree(g, u, column):
                if u % 2 == 0:
                    wait_alone(pe, adj_shifted, g * 2 + u // 2 + 1)
                for blk in range(NT):
                    pe.matmul(psT[:, column:column + 1], adj_f8[:].bitcast(F8)[:, blk, u * P:(u + 1) * P], half16[:],
                              start=(blk == 0), stop=(blk == NT - 1))

            def query(t):
                pe.wait_ge(xt_ready, t + 1)
                if not isinstance(t, int) or t > 0:
                    pe.wait_ge(deg_copied, t if not isinstance(t, int) else min(t, NT - 2))
                for k in range(CC):
                    last = pe.transpose(psT[:, k * P:(k + 1) * P], xt[:, k * P:(k + 1) * P], ident[:])
                last.then_inc(xT_ps, 1)
                pe.wait_ge(xT_ready, t + 1)
                if not isinstance(t, int) or t > 0:
                    pe.wait_ge(q_ready, t)
                if not isinstance(t, int) or t > 2:
                    pe.wait_ge(z_copied, t - 2)
                for k in range(CC):
                    last = pe.matmul(psQ[:, 0:C], xT[:, k, :], wqk[:, k, :], start=(k == 0), stop=(k == CC - 1))
                last.then_inc(q_ps, 1)

            def weigh(t, u):
                pe.wait_ge(diag_ready, t * K + K)
                if not isinstance(t, int) or t > 0:
                    pe.wait_ge(y_used, t)
                for c in range(CC):
                    for k in range(K):
                        last = pe.matmul(psY[:, c * P:(c + 1) * P], nbr[:, u, k, c * P:(c + 1) * P], diag[:, u % 2, k, :],
                                         start=(k == 0), stop=(k == K - 1))
                last.then_inc(y_ps, 1)

            def project(t, queries):
                pe.wait_ge(y_used, t + 1)
                pe.wait_ge(q_ready, queries)
                if not isinstance(t, int) or t > 0:
                    pe.wait_ge(z_copied, t)
                for k in range(CC):
                    last = pe.matmul(psQ[:, C:2 * C], yT_sb[:, k, :], wvT[:, k, :], start=(k == 0), stop=(k == CC - 1))
                last.then_inc(z_ps, 1)

            def step(t, u, g):
                first, over = isinstance(t, int) and t < GT, isinstance(t, int) and t >= NT - GT
                if not (over and t + 2 >= NT):
                    code(t + 2, (u + 2) % GT, 1)
                if not (over and t + 3 >= NT):
                    wait_alone(pe, deg_copied, t + 1)
                    degree(g + (u + 3) // GT, (u + 3) % GT, C)
                if not (first and t < 2):
                    project(t - 2, t + 1)
                if not (first and t < 1):
                    weigh(t - 1, (u - 1) % GT)
                if not (over and t + 3 >= NT):
                    code(t + 3, (u + 3) % GT, 0)
                if not (over and t + 1 >= NT):
                    query(t + 1)
            for t in range(3):
                degree(0, t, C + t)
            for t in range(2):
                code(t, t, 0)
                code(t, t, 1)
            code(2, 2, 0)
            query(0)
            for u in range(GT):
                step(u, u, 0)
            with pe.Fori(0, NG - 2) as i:
                for u in range(GT):
                    step(i * GT + (GT + u), u, i + 1)
            for u in range(GT):
                step(NT - GT + u, u, NG - 1)
            project(NT - 2, NT)
            weigh(NT - 1, GT - 1)
            project(NT - 1, NT)

            pe.wait_ge(z_copied, NT)
            pe.transpose(psT[0:NT, 0:P], deg_all[:], ident[:]).then_inc(deg_T, 1)
            pe.wait_ge(deg_max, 1)
            pe.transpose(psT[0:1, P:P + NT], rounds_f[:, 0:1], ident[0:NT, 0:NT]).then_inc(deg_row, 1)

            def more_round(n):
                wait_alone(pe, more_shift, n + 1)
                for q in range(NQ):
                    if q < 2:
                        wait_alone(pe, more_free, n + 1)
                    else:
                        wait_alone(pe, more_step, n * (3 * NQ + 17) + 3 * (q - 2) + 1)
                    for j in range(QW // P):
                        blk = q * (QW // P) + j
                        last = pe.matmul(codes[:, q % 2, j * P:(j + 1) * P], adj_f8[:].bitcast(F8)[:, blk, 0:P],
                                         codediag[:, blk, :], start=True, stop=True)
                    last.then_inc(more_codes, 1)
                wait_alone(pe, more_xt, n + 1)
                for k in range(CC):
                    last = pe.transpose(psT[:, k * P:(k + 1) * P], xt[:, k * P:(k + 1) * P], ident[:])
                last.then_inc(more_xTps, 1)
                wait_alone(pe, more_xT, n + 1)
                for k in range(CC):
                    last = pe.matmul(psQ[:, 0:C], xT[:, k, :], wqk[:, k, :], start=(k == 0), stop=(k == CC - 1))
                last.then_inc(more_qps, 1)
                wait_alone(pe, more_diag, n * K + K)
                for k in range(K):
                    last = pe.matmul(psY[:, 0:C], diag[:, 0, k, :], nbr[:, 0, k, :], start=(k == 0), stop=(k == K - 1))
                last.then_inc(more_y, 1)
                wait_alone(pe, more_yr, n + 1)
                for k in range(CC):
                    last = pe.transpose(psT[:, k * P:(k + 1) * P], run_y[:, k * P:(k + 1) * P], ident[:])
                last.then_inc(more_yps, 1)
                wait_alone(pe, more_yT, n + 1)
                for k in range(CC):
                    last = pe.matmul(psQ[:, C:2 * C], yT_sb[:, k, :], wvT[:, k, :], start=(k == 0), stop=(k == CC - 1))
                last.then_inc(more_z, 1)

            pe.wait_ge(rounds_known, 1)
            listed = pe.value_load(sched[0:1, 3, 0:1], min_val=0, max_val=NT)
            with pe.If(listed > 0):
                with pe.Fori(0, listed) as m:
                    t = pe.value_load(sched[0:1, 0, bass.ds(m, 1)], min_val=0, max_val=NT - 1)
                    r = pe.value_load(sched[0:1, 1, bass.ds(m, 1)], min_val=1, max_val=N // K)
                    before = pe.value_load(sched[0:1, 2, bass.ds(m, 1)], min_val=0, max_val=NT * N // K)
                    with pe.Fori(0, r) as i:
                        more_round(before + i)

            pe.sem_inc(xg_ps, GT)
            pe.sem_inc(lg_done, 2)

            def rows_transposed(t, u):
                wait_alone(pe, xg_ready, t + 1)
                for k in range(CC):
                    last = pe.transpose(psXT[:, u % 2, k * P:(k + 1) * P], xg[:, 0, u, k * P:(k + 1) * P], ident[:])
                last.then_inc(xg_ps, 1)

            with pe.Fori(0, NG) as g:
                rows_transposed(g * GT, 0)
                for u in range(GT):
                    t = g * GT + u
                    if u + 1 < GT:
                        rows_transposed(t + 1, u + 1)
                    pe.wait_ge(xgT_ready, t + 1)
                    if u == 0:
                        wait_alone(pe, lg_ready, g + 1)
                    for k in range(CC):
                        last = pe.matmul(psL[:, u * E:(u + 1) * E], xgT[:, u % 2, k * P:(k + 1) * P], wr[:, k, :],
                                         start=(k == 0), stop=(k == CC - 1))
                    last.then_inc(lg_done, 1)
            pe.wait_ge(route_consts, 4)
            pe.wait_ge(oh_ready, 1)
            both = oh[:, 2].rearrange("p t e -> p (t e)")
            pe.matmul(psR[:, 0], tri[:], both, start=True, stop=True)
            pe.matmul(psR[:, 1], ones[:], both, start=True, stop=True).then_inc(rank_ps, 1)

            pe.sem_inc(w_used, 2)
            pe.sem_inc(x_ps, 1)
            pe.wait_ge(planned, 1)
            LAG = 3

            def rows_turned(n):
                wait_alone(pe, xin_loaded, n * 16 + 16)
                if not isinstance(n, int):
                    wait_alone(pe, xl_ready, n)
                for q in range(TS):
                    for k in range(CC):
                        last = pe.transpose(psX[:, k * T + q * P:k * T + (q + 1) * P], x_in[:, q, k * P:(k + 1) * P], ident[:])
                last.then_inc(x_ps, 1)
            rows_turned(0)

            def tiles(e, b):
                wait_alone(pe, w_split, e * 2 + 2 + 2)
                count = pe.value_load(plan[0:1, 0, bass.ds(e, 1)], min_val=1, max_val=N // T)
                before = pe.value_load(plan[0:1, 1, bass.ds(e, 1)], min_val=0, max_val=MAX_TILES)
                with pe.Fori(0, count) as i:
                    n = before + i
                    wait_alone(pe, xl_ready, n + 1)

                    def first(hc):
                        wait_alone(pe, hf_ready, n * HC + hc + 1)
                        m = slice(hc * P, (hc + 1) * P)
                        for k in range(CC):
                            pe.matmul(psH[:, hc % 4, 0:T], w1_hi[:, b, k, m], x_hi[:, k, :], start=(k == 0), stop=False)
                            pe.matmul(psH[:, hc % 4, 0:T], w1_hi[:, b, k, m], x_lo[:, k, :], start=False, stop=False)
                            last = pe.matmul(psH[:, hc % 4, 0:T], w1_lo[:, b, k, m], x_hi[:, k, :], start=False, stop=(k == CC - 1))
                        last.then_inc(h_ps, 1)

                    def second(hc):
                        wait_alone(pe, hl_ready, n * HC + hc + 1 + HC)
                        if hc == 0:
                            wait_alone(pe, yo_ready, n * TS + TS)
                        for q in range(TS):
                            m = slice(q * P, (q + 1) * P)
                            pe.matmul(psE[:, q, 0:C], h_hi[:, hc, m], w2_hi[:, b, hc, :], start=(hc == 0), stop=False)
                            pe.matmul(psE[:, q, 0:C], h_hi[:, hc, m], w2_lo[:, b, hc, :], start=False, stop=False)
                            last = pe.matmul(psE[:, q, 0:C], h_lo[:, hc, m], w2_hi[:, b, hc, :], start=False, stop=(hc == HC - 1))
                            if hc == HC - 1:
                                last.then_inc(e_ps, 1)
                    for hc in range(HC + LAG):
                        if hc < HC:
                            first(hc)
                        if hc == HC:
                            rows_turned(n + 1)
                        if hc >= LAG:
                            second(hc - LAG)
                pe.drain().then_inc(w_used, 1)
            with pe.Fori(0, E // 2) as e:
                tiles(e * 2, 0)
                tiles(e * 2 + 1, 1)

        @block.scalar
        def _(act):
            act.wait_ge(ln_step, 2 * NT + 1)
            act.activation(rstd[:], nr[:, 0], ACT.Sqrt).then_inc(rstd_sqrt, 1)
            act.wait_ge(w_t, 2)
            act.copy(wqk[:].rearrange("p k c -> p (k c)"), psQ[:]).then_inc(w_sb, 1)
            act.copy(wvT[:].rearrange("p k c -> p (k c)"), psT[:]).then_inc(w_sb, 1)
            act.copy(b1T[:], psY[:, 0:E * HC]).then_inc(w_sb, 1)

            def tile(a, t):
                return a[:, bass.ds(t, 1), :].rearrange("p a c -> p (a c)")

            def step(t, u):
                first, over = isinstance(t, int) and t < GT, isinstance(t, int) and t >= NT - GT
                b = u % 2
                query = not (over and t + 1 >= NT)
                if query:
                    act.copy(xt[:], tile(row_all, t + 1)).then_inc(xt_ready, 1)
                if not (first and t < 2):
                    act.wait_ge(z_ps, t - 1)
                    act.copy(tile(z_all, t - 2), psQ[:, C:2 * C]).then_inc(z_copied, 1)
                if not (first and t < 1):
                    act.wait_ge(y_ps, t + GT)
                    act.copy(yT_sb[:].rearrange("p k c -> p (k c)"), psY[:, 0:C]).then_inc(y_used, 1)
                if query:
                    queries(t + 1, (u + 1) % 2, 0 if over and t + 3 >= NT else 1)
                act.wait_ge(sm_ready, t + 1 + 2)
                act.activation(p[:, b, :], sm[:, b, :], ACT.Exp, bias=ml[:, b, 0:1], accum_out=ml[:, b, 1:2]).then_inc(p_ready, 1)
                act.wait_ge(p_ready, t + 1)
                for k in range(K):
                    act.activation(diag[:, b, k, :], ident[:], ACT.Copy, scale=p[:, b, k:k + 1]).then_inc(diag_ready, 1)
                act.copy(tile(ml_all, t), ml[:, b, :])

            def queries(t, b, degrees):
                act.wait_ge(xT_ps, t + 1)
                act.copy(xT[:].rearrange("p k c -> p (k c)"), psT[:, 0:C]).then_inc(xT_ready, 1)
                if degrees == 1:
                    act.copy(deg_all[:, bass.ds(t + 2, 1)], psT[:, C:C + 1]).then_inc(deg_copied, 1)
                elif degrees > 1:
                    act.copy(deg_all[:, 0:degrees], psT[:, C:C + degrees]).then_inc(deg_copied, 1)
                act.wait_ge(q_ps, t + 1)
                act.wait_ge(sm_ready, t + 1)
                act.copy(q_sb[:, b, :], psQ[:, 0:C]).then_inc(q_ready, 1)

            act.wait_ge(xn_ready, NT)
            act.copy(xt[:], row_all[:, 0, :]).then_inc(xt_ready, 1)
            queries(0, 0, 3)
            for u in range(GT):
                step(u, u)
            with act.Fori(0, NG - 2) as i:
                for u in range(GT):
                    step(i * GT + (GT + u), u)
            for u in range(GT):
                step(NT - GT + u, u)
            act.wait_ge(z_ps, NT - 1)
            act.copy(z_all[:, NT - 2, :], psQ[:, C:2 * C]).then_inc(z_copied, 1)
            act.wait_ge(y_ps, NT + GT)
            act.copy(yT_sb[:].rearrange("p k c -> p (k c)"), psY[:, 0:C]).then_inc(y_used, 1)
            act.wait_ge(z_ps, NT)
            act.copy(z_all[:, NT - 1, :], psQ[:, C:2 * C]).then_inc(z_copied, 1)

            def more_round(t, n):
                wait_alone(act, more_free, n + 1)
                act.copy(xt[:], row_all[:, bass.ds(t, 1), :].rearrange("p a c -> p (a c)")).then_inc(more_xt, 1)
                wait_alone(act, more_xTps, n + 1)
                act.copy(xT[:].rearrange("p k c -> p (k c)"), psT[:, 0:C]).then_inc(more_xT, 1)
                wait_alone(act, more_qps, n + 1)
                act.copy(q_sb[:, 0, :], psQ[:, 0:C]).then_inc(more_q, 1)
                wait_alone(act, more_m, n + 1)
                act.activation(p[:, 0, :], sm[:, 0, :], ACT.Exp, bias=run[:, 2:3], accum_out=run[:, 3:4]).then_inc(more_p, 1)
                act.activation(run[:, 4:5], run[:, 0:1], ACT.Exp, bias=run[:, 2:3]).then_inc(more_p, 1)
                wait_alone(act, more_p, n * 2 + 2)
                for k in range(K):
                    act.activation(diag[:, 0, k, :], ident[:], ACT.Copy, scale=p[:, 0, k:k + 1]).then_inc(more_diag, 1)
                wait_alone(act, more_yps, n + 1)
                act.copy(yT_sb[:].rearrange("p k c -> p (k c)"), psT[:, 0:C]).then_inc(more_yT, 1)
            act.wait_ge(rounds_known, 1)
            listed = act.value_load(sched[0:1, 3, 0:1], min_val=0, max_val=NT)
            with act.If(listed > 0):
                with act.Fori(0, listed) as m:
                    t = act.value_load(sched[0:1, 0, bass.ds(m, 1)], min_val=0, max_val=NT - 1)
                    r = act.value_load(sched[0:1, 1, bass.ds(m, 1)], min_val=1, max_val=N // K)
                    before = act.value_load(sched[0:1, 2, bass.ds(m, 1)], min_val=0, max_val=NT * N // K)
                    with act.Fori(0, r) as i:
                        more_round(t, before + i)

            act.sem_inc(lg_ready, 1)
            act.wait_ge(attention_done, 1)

            def normalise(t, b, u, what):
                act.activation(xg[:, b, u, :], tile(x_all, t), ACT.Identity, bias=shift_by[:, bass.ds(t, 1)],
                               scale=rstd[:, bass.ds(t, 1)]).then_inc(what, 1)

            def turned(t, u):
                wait_alone(act, lg_done, t + 1)
                act.wait_ge(xg_ps, t + 1 + GT)
                act.copy(xgT[:, u % 2, :], psXT[:, u % 2, 0:C]).then_inc(xgT_ready, 1)
            for half in range(2):
                w = slice(half * NT // 2, (half + 1) * NT // 2)
                act.wait_ge(var_ready, half + 1)
                act.activation(rstd[:, w], nr[:, 0, w], ACT.Sqrt).then_inc(std_ready, 1)
                act.wait_ge(norm_ready, half + 1)
                with act.Fori(half * NG // 2, (half + 1) * NG // 2) as g:
                    for u in range(GT + 1):
                        if u < GT:
                            wait_alone(act, xg_ps, g * GT + u + 1)
                            normalise(g * GT + u, 0, u, xg_ready)
                        if u >= 1:
                            turned(g * GT + u - 1, u - 1)
                    act.wait_ge(lg_done, g * GT + GT + 2)
                    act.copy(lg[:, 0, bass.ds(g * GT, GT), :].rearrange("p t e -> p (t e)"), psL[:, 0:GT * E]).then_inc(lg_ready, 1)
            for b in range(2):
                for u in range(GT):
                    normalise(b * GT + u, b, u, xs_ready)
            with act.Fori(1, NG // 2) as i:
                for b in range(2):
                    wait_alone(act, scattered[b], i * (32 * GT))
                    for u in range(GT):
                        normalise(i * (2 * GT) + (b * GT + u), b, u, xs_ready)
            act.wait_ge(planned, 1)
            act.activation(gates[:, 1], d_all[:], ACT.Exp).then_inc(d_exp, 1)

            act.sem_inc(hf_ready, 4)

            def part_of_x(n):
                act.wait_ge(x_ps, n + 1 + 1)
                act.copy(x_hi[:].rearrange("p k t -> p (k t)"), psX[:]).then_inc(xh_ready, 1)
            part_of_x(0)

            def tiles(e, b):
                act.copy(b1e[:, b, :], b1T[:, bass.ds(e * HC, HC)]).then_inc(b1_moved, 1)
                wait_alone(act, b1_moved, e + 1)
                count = act.value_load(plan[0:1, 0, bass.ds(e, 1)], min_val=1, max_val=N // T)
                before = act.value_load(plan[0:1, 1, bass.ds(e, 1)], min_val=0, max_val=MAX_TILES)
                with act.Fori(0, count) as i:
                    n = before + i
                    for hc in range(HC):
                        wait_alone(act, hl_ready, n * HC + hc + 1)
                        act.wait_ge(h_ps, n * HC + hc + 1)
                        act.activation(h_f[:, hc, :], psH[:, hc % 4, 0:T], ACT.Relu, bias=b1e[:, b, hc:hc + 1]).then_inc(hf_ready, 1)
                    part_of_x(n + 1)
            with act.Fori(0, E // 2) as e:
                tiles(e * 2, 0)
                tiles(e * 2 + 1, 1)
    return nc


_INS = ["x", "adj", "L0_gnn_Wq", "L0_gnn_Wk", "L0_gnn_Wv", "L0_ffn_W_router", "L0_ffn_W1", "L0_ffn_b1", "L0_ffn_W2", "L0_ffn_b2"]


def kernel(**inputs):
    import concourse.bacc as bacc
    from concourse.bass_utils import run_bass_kernel_spmd

    nc = bacc.Bacc("TRN2", target_bir_lowering=False, num_devices=1)
    arrays, args = {}, []
    for name in _INS:
        a = np.ascontiguousarray(inputs[name])
        arrays[f"in_{name}"] = a
        args.append(nc.dram_tensor(f"in_{name}", a.shape, mybir.dt.from_np(a.dtype), kind="ExternalInput").ap())
    out = nc.dram_tensor("out", (N, C), F32, kind="ExternalOutput").ap()
    attention_and_experts(nc, *args, out)
    r = run_bass_kernel_spmd(nc, [arrays], core_ids=[0])
    return r.results[0]["out"]
```

```python
from contextlib import ExitStack

import numpy as np

import concourse.bass as bass
from concourse import mybir

F32 = mybir.dt.float32
F32R = mybir.dt.float32r
F16 = mybir.dt.float16
F8 = mybir.dt.float8e4
U8 = mybir.dt.uint8
U16 = mybir.dt.uint16
U32 = mybir.dt.uint32
I32 = mybir.dt.int32
ALU = mybir.AluOpType
ACT = mybir.ActivationFunctionType
AX = mybir.AxisListType

P = 128
N = 4096
C = 256
E = 8
H = 1024
EPS = 1e-5
NEG = -1e30
NT = N // P
CC = C // P
HC = H // P
QT = 8
GT = 4
NG = NT // GT
K = 8
QW = 1024
NQ = N // QW
CODE0 = 0x4000
T = 256
TS = T // P
MAX_TILES = 2 * N // T + E
REGION = N + T


def attention_and_experts(nc, x, adj, Wq, Wk, Wv, Wr, W1, b1, W2, b2, out):
    ctx = ExitStack()

    def sb(name, shape, dt, stack=ctx):
        return stack.enter_context(nc.sbuf_tensor(name, shape, dt))

    def ps(name, shape, dt, stack=ctx):
        return stack.enter_context(nc.psum_tensor(name, shape, dt))

    def sem(name):
        return ctx.enter_context(nc.semaphore(name))

    with ctx:
        xn_rows = nc.dram_tensor("xn_rows", (N, C), F32).ap()
        expert_in = nc.dram_tensor("expert_in", (E * REGION, C), F32).ap()
        early_out = nc.dram_tensor("early_out", ((MAX_TILES + 1) * T, C), F32).ap()
        expert_out = nc.dram_tensor("expert_out", ((MAX_TILES + 1) * T, C), F32).ap()

        x_all = sb("x_all", [P, NT, C], F32)
        ident = sb("ident", [P, P], F32)
        stats = sb("stats", [P, 4, 6], F32)
        mv = sb("mv", [P, NT, 2], F32)
        rstd = sb("rstd", [P, NT], F32)
        less_mean = sb("less_mean", [P, NT], F32)
        nr = sb("nr", [P, 2, NT], F32)
        wvT = sb("wvT", [P, CC, C], F32)
        wr = sb("wr", [P, CC, E], F32)
        b1T = sb("b1T", [P, E * HC], F32)
        b1e = sb("b1e", [P, 2, HC], F32)
        same_e = sb("same_e", [P, E, QT], F32)
        zero_rows = sb("zero_rows", [P, 1, C], F32)
        tri = sb("tri", [P, P], F32)
        ones = sb("ones", [P, P], F32)
        iota_i = sb("iota_i", [P, 2, E], I32)
        iota_f = sb("iota_f", [P, 2, E], F32)
        rl = sb("rl", [P, 3, NT], F32)
        row_end = sb("row_end", [P, 2, E], F32)
        pos_all = sb("pos_all", [P, 2, NT], U32)
        d_all = sb("d_all", [P, NT], F32)
        gates = sb("gates", [P, 3, NT], F32)
        mix_by = sb("mix_by", [P, 2, NT], F32)
        swap = sb("swap", [P, 4, NT], F32)
        gpos = sb("gpos", [P, 2, GT], U32)
        plan_f = sb("plan_f", [P, 9, E], F32)
        tile_f = sb("tile_f", [1, 3, MAX_TILES], F32)
        tile_n = sb("tile_n", [1, MAX_TILES], I32)
        tile_rows = sb("tile_rows", [1, MAX_TILES], I32)
        plan_i = sb("plan_i", [P, 2, E], I32)
        plan = sb("plan", [1, 7, E], I32)

        sums = ExitStack()
        z_all = sb("z_all", [P, NT, C], F32, sums)
        ml_all = sb("ml_all", [P, NT, 2], F32, sums)
        deg_all = sb("deg_all", [P, NT], F32, sums)
        last_all = sb("last_all", [P, NT], F32, sums)
        att = ExitStack()
        row_all = sb("row_all", [P, NT, C], F32, att)
        adj_raw = sb("adj_raw", [P, NT, GT * P], U8, att)
        adj_f8 = sb("adj_f8", [P, NT, GT * P], U8, att)
        codediag = sb("codediag", [P, NT, P], F16, att)
        half16 = sb("half16", [P, 1], F16, att)
        code_i = sb("code_i", [P, NT], I32, att)
        code_u = sb("code_u", [P, NT], U16, att)
        wqk = sb("wqk", [P, CC, C], F32, att)
        b1raw = sb("b1raw", [E * HC, P], F32, att)
        xt = sb("xt", [P, C], F32, att)
        xT = sb("xT", [P, CC, P], F32, att)
        q_sb = sb("q_sb", [P, 2, C], F32, att)
        best = sb("best", [P, NQ * K], F16, att)
        top = sb("top", [P, 2, K], F16, att)
        idx = sb("idx", [P, GT, K], U32, att)
        off = sb("off", [P, GT, K], F32, att)
        nbr = sb("nbr", [P, GT, K, C], F32, att)
        wraw = nbr[:, GT - 1, 0:3 * CC, :].rearrange("p (n k) c -> p n k c", n=3)
        yT_sb = sb("yT_sb", [P, CC, P], F32, att)
        prod = sb("prod", [P, K, C], F32, att)
        s = sb("s", [P, 2, K], F32, att)
        sm = sb("sm", [P, 2, K], F32, att)
        ml = sb("ml", [P, 2, 2], F32, att)
        p = sb("p", [P, 2, K], F32, att)
        diag = sb("diag", [P, 2, K, P], F32, att)
        rounds_f = sb("rounds_f", [NT, 2], F32, att)
        ident16 = sb("ident16", [P, P], F16, att)
        rounds_row = sb("rounds_row", [1, 6, NT], F32, att)
        rounds_i = sb("rounds_i", [1, 2, NT], I32, att)
        list_f = sb("list_f", [1, 3, NT], F32, att)
        sched = sb("sched", [1, 4, NT], I32, att)
        run = sb("run", [P, 8], F32, att)

        attp = ExitStack()
        codes = ps("codes", [P, 2, QW], F32, attp)
        psT = ps("psT", [P, 512], F32, attp)
        psQ = ps("psQ", [P, 512], F32, attp)
        psY = ps("psY", [P, 512], F32, attp)
        attp.close()
        att.close()

        st2 = sb("st2", [P, QT, 6], F32, sums)
        mv2 = sb("mv2", [P, 2, QT, 2], F32, sums)
        rs2 = sb("rs2", [P, 2, 5, QT], F32, sums)
        xg = sb("xg", [P, 2, QT, C], F32, sums)
        xgT = sb("xgT", [P, 2, C], F32, sums)
        lg = sb("lg", [P, 2, QT, E], F32, sums)
        m12 = sb("m12", [P, 2, QT], F32, sums)
        e12 = sb("e12", [P, QT], F32, sums)
        cand = sb("cand", [P, QT, E], F32, sums)
        oh = sb("oh", [P, 3, QT, E], F32, sums)
        cnt = sb("cnt", [P, 3, E, QT], F32, sums)
        z = sb("z", [P, 2, QT, E], F32, sums)
        posq = sb("posq", [P, 2, QT], F32, sums)
        posf = sb("posf", [P, 2, NT], F32, sums)
        out_f = sb("out_f", [P, 2, 2, NT], F32, sums)
        out_s = sb("out_s", [P, 2, NT], F32, sums)
        pos = sb("pos", [P, 2, 2, QT], U32, sums)
        midp = ExitStack()
        psXT = ps("psXT", [P, 2, 512], F32, midp)
        psL = ps("psL", [P, 512], F32, midp)
        psR = ps("psR", [P, 2, QT * E], F32, midp)
        midp.close()

        ffn = ExitStack()
        w1_raw = sb("w1_raw", [P, CC, H], F32, ffn)
        w2_raw = sb("w2_raw", [P, HC, C], F32, ffn)
        w1_hi = sb("w1_hi", [P, 2, CC, H], F32R, ffn)
        w1_lo = sb("w1_lo", [P, 2, CC, H], F32R, ffn)
        w2_hi = sb("w2_hi", [P, 2, HC, C], F32R, ffn)
        w2_lo = sb("w2_lo", [P, 2, HC, C], F32R, ffn)
        x_in = sb("x_in", [P, TS, C], F32, ffn)
        x_hi = sb("x_hi", [P, CC, T], F32R, ffn)
        x_lo = sb("x_lo", [P, CC, T], F32R, ffn)
        h_f = z_all[:].rearrange("p t c -> p (t c)")[:, 0:HC * T].rearrange("p (k t) -> p k t", t=T)
        b2_rows = z_all[:].rearrange("p t c -> p (t c)")[:, HC * T:HC * T + E * C].rearrange("p (e c) -> p e c", c=C)
        h_hi = sb("h_hi", [P, HC, T], F32R, ffn)
        h_lo = sb("h_lo", [P, HC, T], F32R, ffn)
        y_out = sb("y_out", [P, TS, C], F32, ffn)
        e_rows = xg[:, 0, 0:GT, :]
        lower = [a for rows in (z_all[:, NT // 2:NT, :], w1_raw[:].rearrange("p k (j c) -> p (k j) c", c=C), w2_raw[:])
                 for a in (rows[:, t, :] for t in range(rows.shape[1]))]
        ffnp = ExitStack()
        psX = ps("psX", [P, 512], F32, ffnp)
        psH = ps("psH", [P, 4, 512], F32, ffnp)
        psE = ps("psE", [P, TS, 512], F32, ffnp)
        ffnp.close()
        ffn.close()
        sums.close()

        x_loaded = [sem(f"x_loaded{i}") for i in range(4)]
        w_loaded = sem("w_loaded")
        adj_loaded = sem("adj_loaded")
        xn_stored = sem("xn_stored")
        gathered = [sem(f"gathered{i}") for i in range(GT)]
        passed = {e.engine: sem(f"passed_{n}") for n, e in (("pe", nc.tensor), ("dve", nc.vector), ("pool", nc.gpsimd), ("sp", nc.sync), ("act", nc.scalar))}
        zeroed = sem("zeroed")
        counted = sem("counted")
        ident_ready = sem("ident_ready")
        cast16 = sem("cast16")
        half_ready = sem("half_ready")
        codediag_ready = sem("codediag_ready")
        ln_step = sem("ln_step")
        rstd_sqrt = sem("rstd_sqrt")
        last_ready = sem("last_ready")
        var1_ready = sem("var1_ready"); ln_ready = sem("ln_ready")
        xn_ready = sem("xn_ready")
        w_t = sem("w_t")
        w_sb = sem("w_sb")
        adj_shifted = sem("adj_shifted")
        codes_ready = sem("codes_ready")
        codes_used = sem("codes_used")
        xt_ready = sem("xt_ready")
        xT_ps = sem("xT_ps")
        xT_ready = sem("xT_ready")
        q_ps = sem("q_ps")
        q_ready = sem("q_ready")
        found = sem("found")
        idx_ready = sem("idx_ready")
        scored = sem("scored")
        sm_ready = sem("sm_ready")
        p_ready = sem("p_ready")
        diag_ready = sem("diag_ready")
        y_ps = sem("y_ps")
        y_used = sem("y_used")
        z_ps = sem("z_ps")
        z_copied = sem("z_copied")
        deg_copied = sem("deg_copied")
        out_stored = sem("out_stored")
        deg_T = sem("deg_T"); deg_max = sem("deg_max"); deg_row = sem("deg_row")
        plan_step = sem("plan_step"); rounds_known = sem("rounds_known")
        more_free = sem("more_free"); more_adj = sem("more_adj"); more_shift = sem("more_shift")
        more_codes = sem("more_codes"); more_copied = sem("more_copied"); more_idx = sem("more_idx")
        more_rows = sem("more_rows"); more_xt = sem("more_xt"); more_xTps = sem("more_xTps")
        more_xT = sem("more_xT"); more_qps = sem("more_qps"); more_q = sem("more_q")
        more_m = sem("more_m"); more_p = sem("more_p"); more_diag = sem("more_diag")
        more_yps = sem("more_yps"); more_yT = sem("more_yT"); more_z = sem("more_z"); more_step = sem("more_step")
        route_consts = sem("route_consts"); consts_step = sem("consts_step"); rl_step = sem("rl_step")
        attention_done = sem("attention_done")
        x2_ready = sem("x2_ready"); ln2_step = sem("ln2_step"); route_step = sem("route_step")
        var_ready = sem("var_ready"); std_ready = sem("std_ready"); norm_ready = sem("norm_ready")
        xg_ready = sem("xg_ready"); xg_ps = sem("xg_ps"); xgT_ready = sem("xgT_ready")
        lg_done = sem("lg_done"); lg_ready = sem("lg_ready"); oh_ready = sem("oh_ready")
        rank_ps = sem("rank_ps"); placed = sem("placed"); xg_free = sem("xg_free"); mv_ready = sem("mv_ready")
        scattered = [sem("scattered0"), sem("scattered1")]
        ends_known = sem("ends_known"); planned = sem("planned"); tails_zeroed = sem("tails_zeroed"); d_exp = sem("d_exp")
        rest_zeroed = sem("rest_zeroed"); early_stored = sem("early_stored")
        b2_loaded = sem("b2_loaded"); x_ps = sem("x_ps"); b1_moved = sem("b1_moved")
        w_raw = [sem("w1_raw_loaded"), sem("w2_raw_loaded")]; w_hi = sem("w_hi"); w_split = sem("w_split"); w_used = sem("w_used")
        xin_loaded = sem("xin_loaded"); xh_ready = sem("xh_ready"); xl_ready = sem("xl_ready")
        h_ps = sem("h_ps"); hf_ready = sem("hf_ready"); hh_ready = sem("hh_ready"); hl_ready = sem("hl_ready")
        e_ps = sem("e_ps"); yo_ready = sem("yo_ready"); yo_stored = sem("yo_stored")
        results = [sem(f"results{i}") for i in range(4)]
        gpos_ready = sem("gpos_ready"); lower_fetched = sem("lower_fetched"); mixed = sem("mixed"); mix_step = sem("mix_step")

        x_t = x.rearrange("(t p) c -> p t c", p=P)
        out_t = out.rearrange("(t p) c -> p t c", p=P)
        adj_u8 = adj.rearrange("(b p) i -> p b i", p=P)
        XL = NT // 4

        def wait_alone(eng, what, value):
            eng.wait_ge(what, value)
            if not isinstance(value, int):
                eng.sem_inc(passed[eng.engine], 1)

        MORE = 2 * NQ + 12
        quarter = [prod[:].rearrange("p k c -> p (k c)")[:, i * QW:(i + 1) * QW] for i in range(2)]

        block = ctx.enter_context(nc.Block())

        @block.sync
        def _(sp):
            for i in range(4):
                sp.dma_start(x_all[:, i * XL:(i + 1) * XL, :], x_t[:, i * XL:(i + 1) * XL, :]).then_inc(x_loaded[i], 16)
                if i == 0:
                    for n, w in enumerate((Wq, Wk, Wv)):
                        sp.dma_start(wraw[:, n], w.rearrange("(k p) c -> p k c", p=P)).then_inc(w_loaded, 16)
                    sp.dma_start(wr[:], Wr.rearrange("(k p) e -> p k e", p=P)).then_inc(w_loaded, 16)
                    sp.dma_start(b1raw[:], b1.rearrange("e (k h) -> (e k) h", h=P)).then_inc(w_loaded, 16)
            sp.dma_start(adj_raw[:], adj_u8[:, :, 0:GT * P]).then_inc(adj_loaded, 16)
            for i in range(4):
                if i < 3:
                    sp.wait_ge(xn_ready, (i + 1) * XL)
                else:
                    sp.wait_ge(last_ready, XL)
                sp.dma_start(xn_rows.rearrange("(t p) c -> p t c", p=P)[:, i * XL:(i + 1) * XL, :],
                             row_all[:, i * XL:(i + 1) * XL, :]).then_inc(xn_stored, 16)
            sp.wait_ge(xn_stored, 64)
            with sp.Fori(1, NG) as g:
                wait_alone(sp, adj_shifted, g * 2)
                sp.dma_start(adj_raw[:], adj_u8[:, :, bass.ds(g * (GT * P), GT * P)]).then_inc(adj_loaded, 16)
            sp.wait_ge(rounds_known, 1)
            listed = sp.value_load(sched[0:1, 3, 0:1], min_val=0, max_val=NT)
            with sp.If(listed > 0):
                with sp.Fori(0, listed) as m:
                    t = sp.value_load(sched[0:1, 0, bass.ds(m, 1)], min_val=0, max_val=NT - 1)
                    r = sp.value_load(sched[0:1, 1, bass.ds(t, 1)], min_val=1, max_val=N // K)
                    before = sp.value_load(sched[0:1, 2, bass.ds(t, 1)], min_val=0, max_val=NT * N // K)
                    with sp.Fori(0, r) as i:
                        wait_alone(sp, more_free, before + i + 1)
                        sp.dma_start(adj_raw[:, :, 0:P], adj_u8[:, :, bass.ds(t * P, P)]).then_inc(more_adj, 16)
            sp.sem_inc(xg_free, 2)
            for b in range(2):
                sp.wait_ge(scattered[b], 32 * QT)
                sp.sem_inc(xg_free, 1)
            sp.wait_ge(norm_ready, NT // QT)
            sp.dma_start(b2_rows.rearrange("p e c -> p (e c)"), b2.rearrange("(a e) c -> a (e c)", a=1).to_broadcast([P, E * C])).then_inc(b2_loaded, 16)
            sp.wait_ge(ends_known, 1)
            for e in range(E):
                end = sp.value_load(plan[0:1, 2, e:e + 1], min_val=0, max_val=E * REGION - T)
                sp.dma_start(expert_in[bass.ds(end, T), :].rearrange("(s p) c -> p s c", p=P), zero_rows[:].to_broadcast([P, TS, C])).then_inc(tails_zeroed, 16)
            def tile_row(n):
                return sp.value_load(tile_rows[0:1, bass.ds(n, 1)], min_val=0, max_val=E * REGION - T)

            def load_tile(n, r):
                wait_alone(sp, x_ps, n + 1)
                sp.dma_start(x_in[:], expert_in[bass.ds(r, T), :].rearrange("(s p) c -> p s c", p=P)).then_inc(xin_loaded, 16)

            def rows_of(table, n):
                return table[bass.ds(n * T, T), :].rearrange("(s p) c -> p s c", p=P)

            def store_tile(n, early):
                wait_alone(sp, yo_ready, n * TS + TS + TS)
                sp.dma_start(rows_of(expert_out, n), y_out[:]).then_inc(yo_stored, 16)
                if early:
                    sp.dma_start(rows_of(early_out, n), y_out[:]).then_inc(early_stored, 16)
            sp.wait_ge(planned, 1)
            total = sp.value_load(plan[0:1, 3, 0:1], min_val=E, max_val=MAX_TILES)
            early = sp.value_load(plan[0:1, 1, E - 1:E], min_val=E - 1, max_val=MAX_TILES - 1)
            of_last = sp.value_load(plan[0:1, 0, E - 1:E], min_val=1, max_val=N // T)
            sp.wait_ge(tails_zeroed, E * 16)
            for b in range(2):
                sp.wait_ge(scattered[b], 32 * QT * (NT // QT // 2))
            load_tile(0, 0)
            with sp.Fori(total, MAX_TILES + 1) as n:
                sp.dma_start(rows_of(expert_out, n), zero_rows[:].to_broadcast([P, TS, C])).then_inc(rest_zeroed, 16)
            with sp.Fori(early, MAX_TILES + 1) as n:
                sp.dma_start(rows_of(early_out, n), zero_rows[:].to_broadcast([P, TS, C])).then_inc(rest_zeroed, 16)
            with sp.Fori(1, early + 1) as n:
                load_tile(n, tile_row(n))
                store_tile(n - 1, True)
            with sp.If(of_last > 1):
                with sp.Fori(early + 1, total) as n:
                    load_tile(n, tile_row(n))
                    store_tile(n - 1, False)
            load_tile(total, 0)
            store_tile(total - 1, False)
            with sp.Fori(0, NG) as g:
                wait_alone(sp, mixed, g * GT + GT + GT)
                sp.dma_start(out_t[:, bass.ds(g * GT, GT), :], x_all[:, bass.ds(g * GT, GT), :]).then_inc(out_stored, 16)
            sp.wait_ge(out_stored, 16 * NG)

        @block.gpsimd
        def _(pool):
            pool.memset(ident[:], 0.0).then_inc(zeroed, 1)
            pool.iota(code_i[:], pattern=[[P, NT]], base=CODE0 - 0x400, channel_multiplier=1).then_inc(counted, 1)
            pool.wait_ge(zeroed, 1)
            pool.affine_select(out=ident[:], in_=ident[:], compare_op=ALU.not_equal, fill=1.0, base=0,
                               pattern=[[-1, P]], channel_multiplier=1).then_inc(ident_ready, 1)
            pool.memset(ones[:], 1.0).then_inc(zeroed, 1)
            pool.iota(iota_i[:, 0, :], pattern=[[1, E]], base=0, channel_multiplier=0).then_inc(route_consts, 1)
            pool.iota(iota_i[:, 1, :], pattern=[[REGION, E]], base=0, channel_multiplier=0).then_inc(route_consts, 1)
            pool.iota(tile_n[:], pattern=[[1, MAX_TILES]], base=0, channel_multiplier=0).then_inc(route_consts, 1)
            pool.wait_ge(zeroed, 2)
            pool.affine_select(out=tri[:], in_=ones[:], compare_op=ALU.is_gt, fill=0.0, base=0,
                               pattern=[[1, P]], channel_multiplier=-1).then_inc(route_consts, 1)
            pool.wait_ge(cast16, 2)
            pool.tensor_tensor(codediag[:], ident16[:].unsqueeze(1).to_broadcast([P, NT, P]),
                              code_u[:].bitcast(F16).unsqueeze(2).to_broadcast([P, NT, P]), ALU.mult).then_inc(codediag_ready, 1)
            pool.wait_ge(xn_stored, 64)

            def gather(t, u):
                wait_alone(pool, idx_ready, t + 1)
                wait_alone(pool, y_ps, t + 1)
                for k in range(K):
                    pool.indirect_dma_start(nbr[:, u, k, :], None, xn_rows,
                                            bass.IndirectOffsetOnAxis(ap=idx[:, u, k:k + 1], axis=0)).then_inc(gathered[u], 16)
            with pool.Fori(0, NG) as g:
                for u in range(GT):
                    gather(g * GT + u, u)
            pool.wait_ge(rounds_known, 1)
            listed = pool.value_load(sched[0:1, 3, 0:1], min_val=0, max_val=NT)
            with pool.If(listed > 0):
                with pool.Fori(0, listed) as m:
                    t = pool.value_load(sched[0:1, 0, bass.ds(m, 1)], min_val=0, max_val=NT - 1)
                    r = pool.value_load(sched[0:1, 1, bass.ds(t, 1)], min_val=1, max_val=N // K)
                    before = pool.value_load(sched[0:1, 2, bass.ds(t, 1)], min_val=0, max_val=NT * N // K)
                    with pool.Fori(0, r) as i:
                        wait_alone(pool, more_idx, before + i + 1)
                        for k in range(K):
                            pool.indirect_dma_start(nbr[:, 0, k, :], None, xn_rows,
                                                    bass.IndirectOffsetOnAxis(ap=idx[:, 0, k:k + 1], axis=0)).then_inc(more_rows, 16)

            matrices = ((W1, w1_raw, w1_hi, w1_lo), (W2, w2_raw, w2_hi, w2_lo))

            def load_weights(e, m):
                wait_alone(pool, w_split, e * 2 + m + 1)
                pool.dma_start(matrices[m][1][:], matrices[m][0][bass.ds(e, 1)].rearrange("a (k p) h -> p (a k) h", p=P)).then_inc(w_raw[m], 16)

            def high_part(e, b, m):
                wait_alone(pool, w_raw[m], e * 16 + 16)
                pool.tensor_copy(matrices[m][2][:, b], matrices[m][1][:]).then_inc(w_hi, 1)

            def low_part(e, b, m):
                wait_alone(pool, w_hi, e * 2 + m + 1)
                pool.tensor_tensor(matrices[m][3][:, b], matrices[m][1][:], matrices[m][2][:, b].bitcast(F32), ALU.subtract).then_inc(w_split, 1)

            def split_weights(e, b, more=True):
                wait_alone(pool, w_used, e + 1)
                for m in range(2):
                    high_part(e, b, m)
                    low_part(e, b, m)
                    if more:
                        load_weights(e + 1, m)
            pool.wait_ge(attention_done, 1)
            pool.sem_inc(w_split, 2)
            pool.wait_ge(w_used, 1)
            load_weights(0, 0)
            load_weights(0, 1)
            high_part(0, 0, 0)
            low_part(0, 0, 0)
            load_weights(1, 0)
            high_part(0, 0, 1)

            def scatter(q, b):
                wait_alone(pool, placed, q + 1)
                wait_alone(pool, xg_ready, q * QT + QT)
                for c in range(2):
                    for u in range(QT):
                        pool.indirect_dma_start(expert_in, bass.IndirectOffsetOnAxis(ap=pos[:, b, c, u:u + 1], axis=0),
                                                xg[:, b, u, :], None).then_inc(scattered[b], 16)
            with pool.Fori(0, NT // QT // 2) as i:
                scatter(i * 2, 0)
                scatter(i * 2 + 1, 1)
            low_part(0, 0, 1)
            load_weights(1, 1)
            split_weights(1, 1)
            with pool.Fori(1, E // 2 - 1) as i:
                split_weights(i * 2, 0)
                split_weights(i * 2 + 1, 1)
            split_weights(E - 2, 0)
            split_weights(E - 1, 1, False)
            total = pool.value_load(plan[0:1, 3, 0:1], min_val=E, max_val=MAX_TILES)
            early = pool.value_load(plan[0:1, 1, E - 1:E], min_val=E - 1, max_val=MAX_TILES - 1)
            rest = pool.value_load(plan[0:1, 4, 0:1], min_val=1, max_val=2 * MAX_TILES + 2)
            wait_alone(pool, rest_zeroed, rest * 16)
            wait_alone(pool, early_stored, early * 16)
            wait_alone(pool, w_split, E * 2 + 2)
            for t in range(NT):
                pool.indirect_dma_start(lower[t], None, early_out,
                                        bass.IndirectOffsetOnAxis(ap=pos_all[:, 0, t:t + 1], axis=0)).then_inc(lower_fetched, 16)

            def fetch(g, b):
                wait_alone(pool, gpos_ready, g + 1)
                for u in range(GT):
                    wait_alone(pool, mixed, g * GT + u + 1)
                    pool.indirect_dma_start(e_rows[:, u, :], None, expert_out,
                                            bass.IndirectOffsetOnAxis(ap=gpos[:, b, u:u + 1], axis=0)).then_inc(results[u], 16)
            wait_alone(pool, yo_stored, total * 16 + 16)
            with pool.Fori(0, NG // 2) as g:
                fetch(g * 2, 0)
                fetch(g * 2 + 1, 1)

        @block.vector
        def _(dve):
            dve.sem_inc(codes_used, 2)
            dve.sem_inc(sm_ready, 2)
            dve.memset(half16[:], 0.5).then_inc(half_ready, 1)
            dve.wait_ge(ident_ready, 1)
            dve.tensor_copy(ident16[:], ident[:]).then_inc(cast16, 1)
            dve.wait_ge(counted, 1)
            dve.tensor_copy(code_u[:], code_i[:]).then_inc(cast16, 1)
            dve.memset(zero_rows[:], 0.0).then_inc(consts_step, 1)
            dve.memset(same_e[:], 1.0).then_inc(consts_step, 1)
            dve.wait_ge(consts_step, 2)
            dve.memset(same_e[:, :, 0:1], 0.0).then_inc(consts_step, 1)
            dve.wait_ge(route_consts, 4)
            dve.tensor_copy(iota_f[:], iota_i[:]).then_inc(consts_step, 1)
            nstep = [0]

            def chain(ins, wait=True):
                nstep[0] += 1
                ins.then_inc(ln_step, 1)
                if wait:
                    dve.wait_ge(ln_step, nstep[0])

            def deviation(i):
                w = slice(i * XL, (i + 1) * XL)
                dve.wait_ge(rstd_sqrt, i + 1)
                chain(dve.reciprocal(rstd[:, w], rstd[:, w]))
                chain(dve.tensor_tensor(nr[:, 1, w], rstd[:, w], rstd[:, w], ALU.mult))
                chain(dve.tensor_tensor(nr[:, 1, w], nr[:, 1, w], nr[:, 0, w], ALU.mult))
                chain(dve.tensor_scalar(nr[:, 1, w], nr[:, 1, w], -0.5, 1.5, ALU.mult, ALU.add))
                chain(dve.tensor_tensor(rstd[:, w], rstd[:, w], nr[:, 1, w], ALU.mult))
                chain(dve.tensor_tensor(nr[:, 1, w], mv[:, w, 0], rstd[:, w], ALU.mult))
                dve.tensor_scalar(less_mean[:, w], nr[:, 1, w], -1.0, None, ALU.mult).then_inc(ln_ready, 1)

            for i in range(4):
                dve.wait_ge(x_loaded[i], 16)
                for u in range(XL + 1):
                    if u < XL:
                        chain(dve.bn_stats(stats[:, u % 4, :], x_all[:, i * XL + u, :]), wait=False)
                    if u >= 1:
                        dve.wait_ge(ln_step, nstep[0] - (1 if u < XL else 0))
                        chain(dve.bn_aggr(mv[:, i * XL + u - 1, :], stats[:, (u - 1) % 4, :]), wait=False)
                dve.wait_ge(ln_step, nstep[0])
                if i:
                    deviation(i - 1)
                w = slice(i * XL, (i + 1) * XL)
                dve.tensor_scalar(nr[:, 0, w], mv[:, w, 1], EPS, None, ALU.add).then_inc(var1_ready, 1)
            deviation(3)

            def shift(g, h):
                wait_alone(dve, adj_loaded, g * 16 + 16)
                cols = slice(h * 2 * P, (h + 1) * 2 * P)
                dve.tensor_scalar(adj_f8[:, :, cols].bitcast(U32), adj_raw[:, :, cols].bitcast(U32), 6, None,
                                  ALU.logical_shift_left).then_inc(adj_shifted, 1)

            FOUND = 2

            def search(t, u):
                for q in range(NQ):
                    wait_alone(dve, codes_ready, t * NQ + q + 1)
                    dve.max(best[:, q * K:(q + 1) * K], codes[:, q % 2, :]).then_inc(codes_used, 1)
                wait_alone(dve, codes_used, t * NQ + NQ + 2)
                dve.max(top[:, u % 2, :], best[:]).then_inc(found, 1)

            def name(t, u):
                dve.wait_ge(found, t * FOUND + 1)
                bits = top[:, u % 2, :].bitcast(U16)
                dve.tensor_scalar(idx[:, u, :], bits, float(CODE0), float(CODE0), ALU.max, ALU.subtract).then_inc(idx_ready, 1)
                dve.tensor_scalar(off[:, u, :], bits, float(CODE0), -NEG, ALU.is_lt, ALU.mult).then_inc(found, 1)
                dve.tensor_copy(last_all[:, bass.ds(t, 1)], top[:, u % 2, K - 1:K])

            def score(t, u, g, ahead=None):
                b = u % 2
                dve.wait_ge(gathered[u], g * (K * 16) + K * 16)
                dve.wait_ge(q_ready, t + 1)
                for k in range(K):
                    dve.tensor_tensor_reduce(out=prod[:, k, :], in0=q_sb[:, b, :], in1=nbr[:, u, k, :], scale=-1.0, scalar=0.0,
                                             op0=ALU.mult, op1=ALU.add, accum_out=s[:, b, k:k + 1]).then_inc(scored, 1)
                    if k == 0 and ahead:
                        name(*ahead)
                wait_alone(dve, scored, t * K + K)
                dve.tensor_tensor_reduce(out=sm[:, b, :], in0=off[:, u, :], in1=s[:, b, :], scale=1.0, scalar=-10 * NEG,
                                         op0=ALU.add, op1=ALU.min, accum_out=ml[:, b, 0:1]).then_inc(sm_ready, 1)

            def plan_rounds():
                plan_n = [0]

                def planning(ins):
                    plan_n[0] += 1
                    ins.then_inc(plan_step, 1)
                    dve.wait_ge(plan_step, plan_n[0])
                dve.wait_ge(route_consts, 4)
                dve.wait_ge(deg_T, 1)
                dve.tensor_reduce(rounds_f[:, 0:1], psT[0:NT, 0:P], AX.X, ALU.max).then_inc(deg_max, 1)
                dve.wait_ge(deg_row, 1)
                planning(dve.tensor_scalar(rounds_i[:, 0], psT[0:1, P:P + NT], float(K - 1), None, ALU.add))
                planning(dve.tensor_scalar(rounds_i[:, 1], rounds_i[:, 0], K.bit_length() - 1, None, ALU.logical_shift_right))
                r_f = rounds_row
                planning(dve.tensor_copy(r_f[:, 5], rounds_i[:, 1]))
                planning(dve.tensor_scalar(r_f[:, 0], r_f[:, 5], -1.0, None, ALU.add))
                planning(dve.tensor_scalar(r_f[:, 1], r_f[:, 0], 0.0, None, ALU.is_gt))
                planning(dve.tensor_tensor(r_f[:, 2], r_f[:, 0], r_f[:, 1], ALU.mult))
                planning(dve.memset(r_f[:, 3], 1.0))
                planning(dve.tensor_tensor_scan(r_f[:, 4], r_f[:, 3], r_f[:, 2], 0.0, ALU.mult, ALU.add))
                planning(dve.tensor_tensor(r_f[:, 5], r_f[:, 4], r_f[:, 2], ALU.subtract))
                flat = prod[0:1].rearrange("p k c -> p (k c)")
                place = flat[:, 0:NT * NT].rearrange("p (i t) -> p i t", t=NT)
                picked = flat[:, NT * NT:2 * NT * NT].rearrange("p (i t) -> p i t", t=NT)
                planning(dve.tensor_copy(list_f[:, 0], tile_n[:, 0:NT]))
                planning(dve.tensor_tensor_scan(list_f[:, 1], r_f[:, 3], r_f[:, 1], 0.0, ALU.mult, ALU.add))
                planning(dve.tensor_copy(sched[:, 3], list_f[:, 1, NT - 1:NT].to_broadcast([1, NT])))
                planning(dve.tensor_tensor(list_f[:, 1], list_f[:, 1], r_f[:, 1], ALU.mult))
                planning(dve.tensor_scalar(list_f[:, 1], list_f[:, 1], -1.0, None, ALU.add))
                planning(dve.tensor_tensor(place, list_f[:, 0].unsqueeze(2).to_broadcast([1, NT, NT]),
                                           list_f[:, 1].unsqueeze(1).to_broadcast([1, NT, NT]), ALU.is_equal))
                planning(dve.tensor_tensor(picked, place, list_f[:, 0].unsqueeze(1).to_broadcast([1, NT, NT]), ALU.mult))
                planning(dve.tensor_reduce(list_f[:, 2], picked, AX.X, ALU.add))
                planning(dve.tensor_copy(sched[:, 0], list_f[:, 2]))
                planning(dve.tensor_copy(sched[:, 1], r_f[:, 2]))
                planning(dve.tensor_copy(sched[:, 2], r_f[:, 5]))
                dve.drain().then_inc(rounds_known, 1)
                dve.sem_inc(more_free, 1)

            shift(0, 0)
            for t in range(3 * XL, NT):
                dve.tensor_scalar(row_all[:, t, :], x_all[:, t, :], mv[:, t, 0:1], rstd[:, t:t + 1],
                                  ALU.subtract, ALU.mult).then_inc(last_ready, 1)
            shift(0, 1)
            for t in range(2):
                search(t, t)
                name(t, t)
            with dve.Fori(0, NG - 1) as g:
                for u in range(GT):
                    t = g * GT + u
                    search(t + 2, (u + 2) % GT)
                    if u % 2 == 0:
                        shift(g + 1, u // 2)
                    score(t, u, g, (t + 2, (u + 2) % GT))
            for u in range(GT):
                t = NT - GT + u
                if t + 2 < NT:
                    search(t + 2, u + 2)
                if t == NT - 1:
                    plan_rounds()
                score(t, u, NG - 1, (t + 2, u + 2) if t + 2 < NT else None)


            def more_round(t, n):
                k = [0]

                def then(ins):
                    k[0] += 1
                    ins.then_inc(more_step, 1)
                    wait_alone(dve, more_step, n * MORE + k[0])
                wait_alone(dve, more_adj, n * 16 + 16)
                dve.tensor_scalar(adj_f8[:, :, 0:P].bitcast(U32), adj_raw[:, :, 0:P].bitcast(U32), 6, None,
                                  ALU.logical_shift_left).then_inc(more_shift, 1)
                for q in range(NQ):
                    wait_alone(dve, more_copied, n * NQ + q + 1)
                    then(dve.scalar_tensor_tensor(quarter[q % 2], quarter[q % 2], run[:, 5:6], quarter[q % 2], ALU.is_lt, ALU.mult))
                    then(dve.max(best[:, q * K:(q + 1) * K], quarter[q % 2]))
                then(dve.max(top[:, 0, :], best[:]))
                bits = top[:, 0, :].bitcast(U16)
                dve.tensor_scalar(idx[:, 0, :], bits, float(CODE0), float(CODE0), ALU.max, ALU.subtract).then_inc(more_idx, 1)
                then(dve.tensor_copy(run[:, 5:6], top[:, 0, K - 1:K]))
                then(dve.tensor_scalar(off[:, 0, :], bits, float(CODE0), -NEG, ALU.is_lt, ALU.mult))
                wait_alone(dve, more_rows, n * (16 * K) + 16 * K)
                wait_alone(dve, more_q, n + 1)
                for j in range(K):
                    ins = dve.tensor_tensor_reduce(out=prod[:, j, :], in0=q_sb[:, 0, :], in1=nbr[:, 0, j, :], scale=1.0, scalar=0.0,
                                                   op0=ALU.mult, op1=ALU.add, accum_out=s[:, 0, j:j + 1])
                then(ins)
                then(dve.tensor_tensor(sm[:, 0, :], s[:, 0, :], off[:, 0, :], ALU.subtract))
                then(dve.tensor_reduce(run[:, 6:7], sm[:, 0, :], AX.X, ALU.max))
                then(dve.tensor_tensor(run[:, 7:8], run[:, 6:7], run[:, 0:1], ALU.max))
                then(dve.tensor_scalar(run[:, 2:3], run[:, 7:8], -1.0, None, ALU.mult))
                dve.drain().then_inc(more_m, 1)
                wait_alone(dve, more_p, n * 2 + 2)
                then(dve.tensor_copy(run[:, 0:1], run[:, 7:8]))
                then(dve.scalar_tensor_tensor(run[:, 1:2], run[:, 1:2], run[:, 4:5], run[:, 3:4], ALU.mult, ALU.add))
                wait_alone(dve, more_z, n + 1)
                z_t = z_all[:, bass.ds(t, 1), :].rearrange("p a c -> p (a c)")
                then(dve.scalar_tensor_tensor(z_t, z_t, run[:, 4:5], psQ[:, C:2 * C], ALU.mult, ALU.add))
                then(dve.tensor_copy(ml_all[:, bass.ds(t, 1), 1:2].rearrange("p a c -> p (a c)"), run[:, 1:2]))
                dve.drain().then_inc(more_free, 1)
                assert k[0] == MORE, k[0]

            dve.wait_ge(rounds_known, 1)
            listed = dve.value_load(sched[0:1, 3, 0:1], min_val=0, max_val=NT)
            with dve.If(listed > 0):
                with dve.Fori(0, listed) as m:
                    t = dve.value_load(sched[0:1, 0, bass.ds(m, 1)], min_val=0, max_val=NT - 1)
                    r = dve.value_load(sched[0:1, 1, bass.ds(t, 1)], min_val=1, max_val=N // K)
                    before = dve.value_load(sched[0:1, 2, bass.ds(t, 1)], min_val=0, max_val=NT * N // K)
                    dve.tensor_scalar(run[:, 0:1], ml_all[:, bass.ds(t, 1), 0:1].rearrange("p a c -> p (a c)"), -1.0, None, ALU.mult)
                    dve.tensor_copy(run[:, 1:2], ml_all[:, bass.ds(t, 1), 1:2].rearrange("p a c -> p (a c)"))
                    dve.tensor_copy(run[:, 5:6], last_all[:, bass.ds(t, 1)])
                    dve.drain()
                    with dve.Fori(0, r) as i:
                        more_round(t, before + i)

            rl_n = [0]

            def link(ins):
                rl_n[0] += 1
                ins.then_inc(rl_step, 1)
                dve.wait_ge(rl_step, rl_n[0])

            def row(a, t):
                return a[:, bass.ds(t, 1), :].rearrange("p a c -> p (a c)")
            dve.wait_ge(z_copied, NT)
            dve.drain().then_inc(attention_done, 1)
            dve.sem_inc(w_used, 2)
            dve.wait_ge(consts_step, 4)
            link(dve.tensor_scalar(rl[:, 0], ml_all[:, :, 1], 1e-30, None, ALU.max))
            link(dve.reciprocal(rl[:, 1], rl[:, 0]))
            link(dve.tensor_scalar(rl[:, 2], deg_all[:], 1.0, None, ALU.min))
            link(dve.tensor_tensor(rl[:, 0], rl[:, 1], rl[:, 2], ALU.mult))

            link(dve.tensor_copy(row_end[:, 1], iota_f[:, 1]))
            MEASURE, ROUTE = 6, 23

            def measure(q, b):
                for u in range(QT + 2):
                    if u < QT:
                        t = q * QT + u
                        dve.scalar_tensor_tensor(row(x_all, t), row(z_all, t), rl[:, 0, bass.ds(t, 1)], row(x_all, t),
                                                 ALU.mult, ALU.add).then_inc(x2_ready, 1)
                    if 1 <= u <= QT:
                        wait_alone(dve, x2_ready, q * QT + u)
                        dve.bn_stats(st2[:, u - 1, :], row(x_all, q * QT + (u - 1))).then_inc(ln2_step, 1)
                    if u >= 2:
                        wait_alone(dve, ln2_step, q * (QT + MEASURE) + u - 1)
                        dve.bn_aggr(mv2[:, b, u - 2, :], st2[:, u - 2, :]).then_inc(mv_ready, 1)
                k = [QT]

                def step(ins):
                    k[0] += 1
                    ins.then_inc(ln2_step, 1)
                    wait_alone(dve, ln2_step, q * (QT + MEASURE) + k[0])
                wait_alone(dve, mv_ready, q * QT + QT)
                mean, var = mv2[:, b, :, 0], mv2[:, b, :, 1]
                r, r_r, v = rs2[:, b, 0], rs2[:, b, 1], rs2[:, b, 2]
                dve.tensor_scalar(v, var, EPS, None, ALU.add).then_inc(var_ready, 1)
                dve.wait_ge(std_ready, q + 1)
                step(dve.reciprocal(r, r))
                step(dve.tensor_tensor(r_r, r, r, ALU.mult))
                step(dve.tensor_tensor(r_r, r_r, v, ALU.mult))
                step(dve.tensor_scalar(r_r, r_r, -0.5, 1.5, ALU.mult, ALU.add))
                step(dve.tensor_tensor(r, r, r_r, ALU.mult))
                step(dve.tensor_tensor(rs2[:, b, 3], mean, r, ALU.mult))
                dve.tensor_scalar(rs2[:, b, 4], rs2[:, b, 3], -1.0, None, ALU.mult).then_inc(norm_ready, 1)
                assert k[0] == QT + MEASURE

            def by_expert(a):
                return a.unsqueeze(1).to_broadcast([P, QT, E])

            def by_token(a):
                return a.unsqueeze(2).to_broadcast([P, QT, E])

            def route(q, b):
                k = [0]

                def step(ins):
                    k[0] += 1
                    ins.then_inc(route_step, 1)
                    wait_alone(dve, route_step, q * ROUTE + k[0])
                wait_alone(dve, lg_ready, q + 1 + 1)
                for c in range(2):
                    step(dve.tensor_reduce(m12[:, c], lg[:, c], AX.X, ALU.max))
                    step(dve.tensor_tensor(cand[:], lg[:, c], by_token(m12[:, c]), ALU.is_equal))
                    step(dve.scalar_tensor_tensor(cand[:], cand[:], -float(E), by_expert(iota_f[:, 0]), ALU.mult, ALU.add))
                    step(dve.tensor_reduce(e12[:], cand[:], AX.X, ALU.min))
                    step(dve.tensor_tensor(oh[:, c], cand[:], by_token(e12[:]), ALU.is_equal))
                    if c == 0:
                        step(dve.scalar_tensor_tensor(lg[:, 1], oh[:, 0], NEG, lg[:, 0], ALU.mult, ALU.add))
                dve.tensor_tensor(oh[:, 2], oh[:, 0], oh[:, 1], ALU.add).then_inc(oh_ready, 1)
                step(dve.tensor_copy(row_end[:, 0], row_end[:, 1]))
                step(dve.tensor_tensor(d_all[:, bass.ds(q * QT, QT)], m12[:, 1], m12[:, 0], ALU.subtract))
                wait_alone(dve, rank_ps, q + 1)
                step(dve.tensor_copy(cnt[:, 0], psR[:, 1].rearrange("p (t e) -> p e t", e=E)))
                step(dve.tensor_tensor_scan(cnt[:, 1].rearrange("p e t -> p (e t)"), same_e[:].rearrange("p e t -> p (e t)"),
                                            cnt[:, 0].rearrange("p e t -> p (e t)"), 0.0, ALU.mult, ALU.add))
                step(dve.tensor_tensor(row_end[:, 1], cnt[:, 1, :, QT - 1], row_end[:, 0], ALU.add))
                step(dve.tensor_tensor(cnt[:, 2], cnt[:, 1], cnt[:, 0], ALU.subtract))
                step(dve.tensor_tensor(cand[:], cnt[:, 2].rearrange("p e t -> p t e"), psR[:, 0].rearrange("p (t e) -> p t e", e=E), ALU.add))
                step(dve.tensor_tensor(cand[:], cand[:], by_expert(row_end[:, 0]), ALU.add))
                for c in range(2):
                    step(dve.tensor_tensor(z[:, c], oh[:, c], cand[:], ALU.mult))
                step(dve.tensor_reduce(posq[:], z[:], AX.X, ALU.add))
                wait_alone(dve, xg_free, q + 1)
                dve.tensor_copy(pos[:, b], posq[:]).then_inc(placed, 1)
                step(dve.tensor_copy(posf[:, :, bass.ds(q * QT, QT)], posq[:]))
                assert k[0] == ROUTE, k[0]

            measure(0, 0)
            with dve.Fori(0, NT // QT // 2 - 1) as i:
                measure(i * 2 + 1, 1)
                route(i * 2, 0)
                measure(i * 2 + 2, 0)
                route(i * 2 + 1, 1)
            measure(NT // QT - 1, 1)
            route(NT // QT - 2, 0)
            route(NT // QT - 1, 1)

            dve.tensor_copy(plan[:, 2], row_end[0:1, 1]).then_inc(ends_known, 1)
            link(dve.tensor_tensor(plan_f[:, 0], row_end[:, 1], iota_f[:, 1, :], ALU.subtract))
            link(dve.tensor_scalar(plan_i[:, 0], plan_f[:, 0], float(T - 1), None, ALU.add))
            link(dve.tensor_scalar(plan_i[:, 1], plan_i[:, 0], T.bit_length() - 1, None, ALU.logical_shift_right))
            link(dve.tensor_copy(plan_f[:, 1], plan_i[:, 1]))
            link(dve.tensor_scalar(plan_f[:, 2], plan_f[:, 1], 1.0, None, ALU.max))
            link(dve.tensor_tensor_scan(plan_f[:, 3], ones[:, 0:E], plan_f[:, 2], 0.0, ALU.mult, ALU.add))
            link(dve.tensor_tensor(plan_f[:, 0], plan_f[:, 3], plan_f[:, 2], ALU.subtract))
            link(dve.tensor_copy(plan[:, 0], plan_f[0:1, 2]))
            link(dve.tensor_copy(plan[:, 1], plan_f[0:1, 0]))
            link(dve.tensor_copy(plan[:, 3], plan_f[0:1, 3, E - 1:E].to_broadcast([1, E])))
            link(dve.tensor_tensor(plan_f[:, 5, 0:1], plan_f[:, 3, E - 1:E], plan_f[:, 0, E - 1:E], ALU.add))
            link(dve.tensor_scalar(plan[:, 4], plan_f[0:1, 5, 0:1].to_broadcast([1, E]), -1.0, float(2 * MAX_TILES + 2), ALU.mult, ALU.add))
            link(dve.tensor_tensor(plan_f[:, 6], row_end[:, 1], iota_f[:, 1], ALU.subtract))
            link(dve.scalar_tensor_tensor(plan_f[:, 7], plan_f[:, 2], float(T), plan_f[:, 6], ALU.mult, ALU.subtract))
            link(dve.tensor_scalar(plan_f[:, 7], plan_f[:, 7], float(P), None, ALU.is_ge))
            link(dve.tensor_tensor(plan_f[:, 8], plan_f[:, 2], plan_f[:, 7], ALU.subtract))
            link(dve.tensor_scalar(plan_f[:, 8], plan_f[:, 8], 1.0, None, ALU.max))
            link(dve.tensor_tensor(plan_f[:, 7], plan_f[:, 2], plan_f[:, 8], ALU.subtract))
            link(dve.tensor_copy(plan[:, 5], plan_f[0:1, 8]))
            link(dve.tensor_copy(plan[:, 6], plan_f[0:1, 7]))
            link(dve.tensor_scalar(plan_f[:, 4], plan_f[:, 2], -float(T), float(REGION), ALU.mult, ALU.add))
            link(dve.tensor_copy(tile_f[:, 0], tile_n[:]))
            link(dve.tensor_scalar(tile_f[:, 1], tile_f[:, 0], float(T), None, ALU.mult))
            for e in range(1, E):
                link(dve.tensor_scalar(tile_f[:, 2], tile_f[:, 0], plan_f[0:1, 0, e:e + 1], plan_f[0:1, 4, e - 1:e], ALU.is_ge, ALU.mult))
                link(dve.tensor_tensor(tile_f[:, 1], tile_f[:, 1], tile_f[:, 2], ALU.add))
            link(dve.tensor_copy(out_f[:, 0], posf[:]))
            link(dve.tensor_copy(out_f[:, 1], posf[:]))
            for e in range(1, E):
                link(dve.tensor_scalar(out_s[:], out_f[:, 0], iota_f[:, 1, e:e + 1], plan_f[:, 4, e - 1:e], ALU.is_ge, ALU.mult))
                link(dve.tensor_tensor(out_f[:, 1], out_f[:, 1], out_s[:], ALU.subtract))
            link(dve.tensor_tensor(swap[:, 0], out_f[:, 1, 0], out_f[:, 1, 1], ALU.is_gt))
            link(dve.tensor_tensor(pos_all[:, 0], out_f[:, 1, 0], out_f[:, 1, 1], ALU.min))
            link(dve.tensor_tensor(pos_all[:, 1], out_f[:, 1, 0], out_f[:, 1, 1], ALU.max))
            dve.tensor_copy(tile_rows[:], tile_f[:, 1]).then_inc(planned, 1)
            dve.wait_ge(d_exp, 1)
            link(dve.tensor_scalar(gates[:, 2], gates[:, 1], 1.0, None, ALU.add))
            link(dve.reciprocal(gates[:, 0], gates[:, 2]))
            link(dve.tensor_tensor(gates[:, 1], gates[:, 1], gates[:, 0], ALU.mult))
            link(dve.tensor_scalar(swap[:, 1], swap[:, 0], -1.0, 1.0, ALU.mult, ALU.add))
            for c in range(2):
                link(dve.tensor_tensor(swap[:, 2], swap[:, 1], gates[:, c], ALU.mult))
                link(dve.tensor_tensor(swap[:, 3], swap[:, 0], gates[:, 1 - c], ALU.mult))
                link(dve.tensor_tensor(mix_by[:, c], swap[:, 2], swap[:, 3], ALU.add))

            dve.sem_inc(yo_ready, TS)
            dve.sem_inc(yo_stored, 16)
            dve.sem_inc(hl_ready, HC)
            dve.wait_ge(planned, 1)
            dve.wait_ge(b2_loaded, 16)

            def rest_of_x(n):
                dve.wait_ge(xh_ready, n + 1)
                dve.tensor_tensor(x_lo[:].rearrange("p k t -> p (k t)"), psX[:], x_hi[:].bitcast(F32).rearrange("p k t -> p (k t)"),
                                  ALU.subtract).then_inc(xl_ready, 1)

            def tiles(e):
                count = dve.value_load(plan[0:1, 0, bass.ds(e, 1)], min_val=1, max_val=N // T)
                before = dve.value_load(plan[0:1, 1, bass.ds(e, 1)], min_val=0, max_val=MAX_TILES)
                with dve.Fori(0, count) as i:
                    n = before + i
                    for hc in range(HC):
                        dve.wait_ge(hf_ready, n * HC + hc + 1 + 4)
                        dve.tensor_copy(h_hi[:, hc, :], h_f[:, hc, :]).then_inc(hh_ready, 1)
                        dve.wait_ge(hh_ready, n * HC + hc + 1)
                        dve.tensor_tensor(h_lo[:, hc, :], h_f[:, hc, :], h_hi[:, hc, :].bitcast(F32), ALU.subtract).then_inc(hl_ready, 1)
                    rest_of_x(n + 1)
                    wait_alone(dve, yo_stored, n * 16 + 16)
                    for q in range(TS):
                        dve.wait_ge(e_ps, n * TS + q + 1)
                        dve.tensor_tensor(y_out[:, q, :], psE[:, q, 0:C], row(b2_rows, e), ALU.add).then_inc(yo_ready, 1)
                dve.sem_inc(w_used, 1)
            rest_of_x(0)
            with dve.Fori(0, E) as e:
                tiles(e)

            dve.sem_inc(mixed, GT)

            def place(g, b):
                dve.tensor_copy(gpos[:, b], pos_all[:, 1, bass.ds(g * GT, GT)]).then_inc(gpos_ready, 1)

            def mix(g, b, place_of_lower):
                for u in range(GT):
                    t = g * GT + u
                    dve.scalar_tensor_tensor(row(x_all, t), place_of_lower(u), mix_by[:, 0, bass.ds(t, 1)], row(x_all, t),
                                             ALU.mult, ALU.add).then_inc(mix_step, 1)
                    wait_alone(dve, mix_step, t + 1)
                    wait_alone(dve, results[u], g * 16 + 16)
                    dve.scalar_tensor_tensor(row(x_all, t), e_rows[:, u, :], mix_by[:, 1, bass.ds(t, 1)], row(x_all, t),
                                             ALU.mult, ALU.add).then_inc(mixed, 1)
            dve.wait_ge(lower_fetched, 16 * NT)
            place(0, 0)
            first = 0
            for rows in (z_all[:, NT // 2:NT, :], w1_raw[:].rearrange("p k (j c) -> p (k j) c", c=C), w2_raw[:]):
                groups = rows.shape[1] // GT
                with dve.Fori(0, groups // 2) as i:
                    g = i * 2 + first
                    place(g + 1, 1)
                    mix(g, 0, lambda u: row(rows, i * (2 * GT) + u))
                    if first + groups < NG:
                        place(g + 2, 0)
                    mix(g + 1, 1, lambda u: row(rows, i * (2 * GT) + (GT + u)))
                first += groups

        @block.tensor
        def _(pe):
            pe.wait_ge(w_loaded, 80)
            pe.wait_ge(ident_ready, 1)
            for m in range(CC):
                for k in range(CC):
                    last = pe.matmul(psQ[:, m * C:(m + 1) * C], wraw[:, 0, k, m * P:(m + 1) * P], wraw[:, 1, k, :],
                                     start=(k == 0), stop=(k == CC - 1))
            last.then_inc(w_t, 1)
            for m in range(CC):
                for k in range(CC):
                    pe.transpose(psT[:, m * C + k * P:m * C + (k + 1) * P], wraw[:, 2, k, m * P:(m + 1) * P], ident[:])
            pe.transpose(psY[:, 0:E * HC], b1raw[:], ident[0:E * HC, 0:E * HC]).then_inc(w_t, 1)
            pe.wait_ge(half_ready, 1)
            pe.wait_ge(codediag_ready, 1)
            pe.wait_ge(w_sb, 3)
            pe.sem_inc(y_ps, GT)

            def code(t, u, half):
                for q in range(half * NQ // 2, (half + 1) * NQ // 2):
                    wait_alone(pe, codes_used, t * NQ + q + 1)
                    for j in range(QW // P):
                        blk = q * (QW // P) + j
                        last = pe.matmul(codes[:, q % 2, j * P:(j + 1) * P], adj_f8[:].bitcast(F8)[:, blk, u * P:(u + 1) * P],
                                         codediag[:, blk, :], start=True, stop=True)
                    last.then_inc(codes_ready, 1)

            def degree(g, u, column):
                if u % 2 == 0:
                    wait_alone(pe, adj_shifted, g * 2 + u // 2 + 1)
                for blk in range(NT):
                    pe.matmul(psT[:, column:column + 1], adj_f8[:].bitcast(F8)[:, blk, u * P:(u + 1) * P], half16[:],
                              start=(blk == 0), stop=(blk == NT - 1))

            def query(t):
                pe.wait_ge(xt_ready, t + 1)
                if not isinstance(t, int) or t > 0:
                    pe.wait_ge(deg_copied, t if not isinstance(t, int) else min(t, NT - 2))
                for k in range(CC):
                    last = pe.transpose(psT[:, k * P:(k + 1) * P], xt[:, k * P:(k + 1) * P], ident[:])
                last.then_inc(xT_ps, 1)
                pe.wait_ge(xT_ready, t + 1)
                if not isinstance(t, int) or t > 0:
                    pe.wait_ge(q_ready, t)
                if not isinstance(t, int) or t > 2:
                    pe.wait_ge(z_copied, t - 2)
                for k in range(CC):
                    last = pe.matmul(psQ[:, 0:C], xT[:, k, :], wqk[:, k, :], start=(k == 0), stop=(k == CC - 1))
                last.then_inc(q_ps, 1)

            def weigh(t, u):
                if not isinstance(t, int) or t > 0:
                    wait_alone(pe, y_used, t)
                for c in range(CC):
                    for k in range(K):
                        if c == 0:
                            pe.wait_ge(diag_ready, t * K + k + 1)
                        last = pe.matmul(psY[:, c * P:(c + 1) * P], nbr[:, u, k, c * P:(c + 1) * P], diag[:, u % 2, k, :],
                                         start=(k == 0), stop=(k == K - 1))
                last.then_inc(y_ps, 1)

            def project(t, queries):
                pe.wait_ge(y_used, t + 1)
                pe.wait_ge(q_ready, queries)
                if not isinstance(t, int) or t > 0:
                    pe.wait_ge(z_copied, t)
                for k in range(CC):
                    last = pe.matmul(psQ[:, C:2 * C], yT_sb[:, k, :], wvT[:, k, :], start=(k == 0), stop=(k == CC - 1))
                last.then_inc(z_ps, 1)

            def step(t, u, g):
                first, over = isinstance(t, int) and t < GT, isinstance(t, int) and t >= NT - GT
                if not (over and t + 2 >= NT):
                    code(t + 2, (u + 2) % GT, 1)
                if not (over and t + 3 >= NT):
                    wait_alone(pe, deg_copied, t + 1)
                    degree(g + (u + 3) // GT, (u + 3) % GT, C)
                if not (first and t < 2):
                    project(t - 2, t + 1)
                if not (first and t < 1):
                    weigh(t - 1, (u - 1) % GT)
                if not (over and t + 3 >= NT):
                    code(t + 3, (u + 3) % GT, 0)
                if not (over and t + 1 >= NT):
                    query(t + 1)
            for t in range(3):
                degree(0, t, C + t)
            for t in range(2):
                code(t, t, 0)
                code(t, t, 1)
            code(2, 2, 0)
            query(0)
            for u in range(GT):
                step(u, u, 0)
            with pe.Fori(0, NG - 2) as i:
                for u in range(GT):
                    step(i * GT + (GT + u), u, i + 1)
            for u in range(GT - 1):
                step(NT - GT + u, u, NG - 1)
            pe.wait_ge(deg_copied, NT - 2)
            pe.wait_ge(xT_ready, NT)
            pe.transpose(psT[0:NT, 0:P], deg_all[:], ident[:]).then_inc(deg_T, 1)
            pe.wait_ge(deg_max, 1)
            pe.transpose(psT[0:1, P:P + NT], rounds_f[:, 0:1], ident[0:NT, 0:NT]).then_inc(deg_row, 1)
            step(NT - 1, GT - 1, NG - 1)
            project(NT - 2, NT)
            weigh(NT - 1, GT - 1)
            project(NT - 1, NT)

            def more_round(n):
                wait_alone(pe, more_shift, n + 1)
                for q in range(NQ):
                    if q < 2:
                        wait_alone(pe, more_free, n + 1)
                    else:
                        wait_alone(pe, more_copied, n * NQ + q - 1)
                    for j in range(QW // P):
                        blk = q * (QW // P) + j
                        last = pe.matmul(codes[:, q % 2, j * P:(j + 1) * P], adj_f8[:].bitcast(F8)[:, blk, 0:P],
                                         codediag[:, blk, :], start=True, stop=True)
                    last.then_inc(more_codes, 1)
                wait_alone(pe, more_xt, n + 1)
                for k in range(CC):
                    last = pe.transpose(psT[:, k * P:(k + 1) * P], xt[:, k * P:(k + 1) * P], ident[:])
                last.then_inc(more_xTps, 1)
                wait_alone(pe, more_xT, n + 1)
                for k in range(CC):
                    last = pe.matmul(psQ[:, 0:C], xT[:, k, :], wqk[:, k, :], start=(k == 0), stop=(k == CC - 1))
                last.then_inc(more_qps, 1)
                wait_alone(pe, more_diag, n * K + K)
                for c in range(CC):
                    for k in range(K):
                        last = pe.matmul(psY[:, c * P:(c + 1) * P], nbr[:, 0, k, c * P:(c + 1) * P], diag[:, 0, k, :],
                                         start=(k == 0), stop=(k == K - 1))
                last.then_inc(more_yps, 1)
                wait_alone(pe, more_yT, n + 1)
                for k in range(CC):
                    last = pe.matmul(psQ[:, C:2 * C], yT_sb[:, k, :], wvT[:, k, :], start=(k == 0), stop=(k == CC - 1))
                last.then_inc(more_z, 1)

            pe.wait_ge(rounds_known, 1)
            listed = pe.value_load(sched[0:1, 3, 0:1], min_val=0, max_val=NT)
            with pe.If(listed > 0):
                with pe.Fori(0, listed) as m:
                    t = pe.value_load(sched[0:1, 0, bass.ds(m, 1)], min_val=0, max_val=NT - 1)
                    r = pe.value_load(sched[0:1, 1, bass.ds(t, 1)], min_val=1, max_val=N // K)
                    before = pe.value_load(sched[0:1, 2, bass.ds(t, 1)], min_val=0, max_val=NT * N // K)
                    with pe.Fori(0, r) as i:
                        more_round(before + i)

            pe.sem_inc(lg_done, 2)
            pe.wait_ge(route_consts, 4)

            def route(q, b):
                def rows_transposed(u):
                    wait_alone(pe, xg_ready, q * QT + u + 1)
                    if u >= 2:
                        wait_alone(pe, xgT_ready, q * QT + u - 1)
                    for k in range(CC):
                        last = pe.transpose(psXT[:, u % 2, k * P:(k + 1) * P], xg[:, b, u, k * P:(k + 1) * P], ident[:])
                    last.then_inc(xg_ps, 1)
                rows_transposed(0)
                rows_transposed(1)
                for u in range(QT):
                    pe.wait_ge(xgT_ready, q * QT + u + 1)
                    if u == 0:
                        wait_alone(pe, lg_ready, q + 1)
                    for k in range(CC):
                        last = pe.matmul(psL[:, u * E:(u + 1) * E], xgT[:, u % 2, k * P:(k + 1) * P], wr[:, k, :],
                                         start=(k == 0), stop=(k == CC - 1))
                    last.then_inc(lg_done, 1)
                    if u + 2 < QT:
                        rows_transposed(u + 2)
                wait_alone(pe, oh_ready, q + 1)
                both = oh[:, 2].rearrange("p t e -> p (t e)")
                pe.matmul(psR[:, 0], tri[:], both, start=True, stop=True)
                pe.matmul(psR[:, 1], ones[:], both, start=True, stop=True).then_inc(rank_ps, 1)
            with pe.Fori(0, NT // QT // 2) as i:
                route(i * 2, 0)
                route(i * 2 + 1, 1)

            pe.sem_inc(x_ps, 1)
            pe.wait_ge(planned, 1)
            LAG = 3

            def rows_turned(n):
                wait_alone(pe, xin_loaded, n * 16 + 16)
                if not isinstance(n, int):
                    wait_alone(pe, xl_ready, n)
                for q in range(TS):
                    for k in range(CC):
                        last = pe.transpose(psX[:, k * T + q * P:k * T + (q + 1) * P], x_in[:, q, k * P:(k + 1) * P], ident[:])
                last.then_inc(x_ps, 1)
            rows_turned(0)

            def tile(n, b, parts):
                wait_alone(pe, xl_ready, n + 1)
                cols = slice(0, parts * P)

                def first(hc):
                    wait_alone(pe, hf_ready, n * HC + hc + 1)
                    m = slice(hc * P, (hc + 1) * P)
                    for k in range(CC):
                        pe.matmul(psH[:, hc % 4, cols], w1_hi[:, b, k, m], x_hi[:, k, cols], start=(k == 0), stop=False)
                        pe.matmul(psH[:, hc % 4, cols], w1_hi[:, b, k, m], x_lo[:, k, cols], start=False, stop=False)
                        last = pe.matmul(psH[:, hc % 4, cols], w1_lo[:, b, k, m], x_hi[:, k, cols], start=False, stop=(k == CC - 1))
                    last.then_inc(h_ps, 1)

                def second(hc):
                    wait_alone(pe, hl_ready, n * HC + hc + 1 + HC)
                    if hc == 0:
                        wait_alone(pe, yo_ready, n * TS + TS)
                    for q in range(parts):
                        m = slice(q * P, (q + 1) * P)
                        pe.matmul(psE[:, q, 0:C], h_hi[:, hc, m], w2_hi[:, b, hc, :], start=(hc == 0), stop=False)
                        pe.matmul(psE[:, q, 0:C], h_hi[:, hc, m], w2_lo[:, b, hc, :], start=False, stop=False)
                        last = pe.matmul(psE[:, q, 0:C], h_lo[:, hc, m], w2_hi[:, b, hc, :], start=False, stop=(hc == HC - 1))
                        if hc == HC - 1:
                            last.then_inc(e_ps, 1 if q + 1 < parts else TS - q)
                for hc in range(HC + LAG):
                    if hc < HC:
                        first(hc)
                    if hc == HC:
                        rows_turned(n + 1)
                    if hc >= LAG:
                        second(hc - LAG)

            def sizes(e):
                return (pe.value_load(plan[0:1, 5, bass.ds(e, 1)], min_val=1, max_val=N // T),
                        pe.value_load(plan[0:1, 6, bass.ds(e, 1)], min_val=0, max_val=1),
                        pe.value_load(plan[0:1, 1, bass.ds(e, 1)], min_val=0, max_val=MAX_TILES))

            def tiles(e, b, full, half, before):
                wait_alone(pe, w_split, e * 2 + 2 + 2)
                with pe.Fori(0, full) as i:
                    tile(before + i, b, TS)
                with pe.If(half > 0):
                    tile(before + full, b, 1)
            with pe.Fori(0, E // 2) as e:
                both = sizes(e * 2), sizes(e * 2 + 1)
                tiles(e * 2, 0, *both[0])
                tiles(e * 2 + 1, 1, *both[1])

        @block.scalar
        def _(act):
            for i in range(4):
                w = slice(i * XL, (i + 1) * XL)
                act.wait_ge(var1_ready, i + 1)
                act.activation(rstd[:, w], nr[:, 0, w], ACT.Sqrt).then_inc(rstd_sqrt, 1)
                if i == 0:
                    act.wait_ge(w_t, 2)
                    act.copy(wqk[:].rearrange("p k c -> p (k c)"), psQ[:]).then_inc(w_sb, 1)
                    act.copy(wvT[:].rearrange("p k c -> p (k c)"), psT[:]).then_inc(w_sb, 1)
                    act.copy(b1T[:], psY[:, 0:E * HC]).then_inc(w_sb, 1)
                else:
                    act.wait_ge(ln_ready, i)
                    for t in range((i - 1) * XL, i * XL):
                        act.activation(row_all[:, t, :], x_all[:, t, :], ACT.Identity, bias=less_mean[:, t:t + 1],
                                       scale=rstd[:, t:t + 1]).then_inc(xn_ready, 1)

            def tile(a, t):
                return a[:, bass.ds(t, 1), :].rearrange("p a c -> p (a c)")

            def step(t, u):
                first, over = isinstance(t, int) and t < GT, isinstance(t, int) and t >= NT - GT
                b = u % 2
                query = not (over and t + 1 >= NT)
                if query:
                    act.copy(xt[:], tile(row_all, t + 1)).then_inc(xt_ready, 1)
                if not (first and t < 2):
                    act.wait_ge(z_ps, t - 1)
                    act.copy(tile(z_all, t - 2), psQ[:, C:2 * C]).then_inc(z_copied, 1)
                if not (first and t < 1):
                    act.wait_ge(y_ps, t + GT)
                    act.copy(yT_sb[:].rearrange("p k c -> p (k c)"), psY[:, 0:C]).then_inc(y_used, 1)
                if query:
                    queries(t + 1, (u + 1) % 2, 0 if over and t + 3 >= NT else 1)
                act.wait_ge(sm_ready, t + 1 + 2)
                act.activation(p[:, b, :], sm[:, b, :], ACT.Exp, bias=ml[:, b, 0:1], scale=-1.0, accum_out=ml[:, b, 1:2]).then_inc(p_ready, 1)
                act.wait_ge(p_ready, t + 1)
                for k in range(K):
                    act.activation(diag[:, b, k, :], ident[:], ACT.Copy, scale=p[:, b, k:k + 1]).then_inc(diag_ready, 1)
                act.copy(tile(ml_all, t), ml[:, b, :])

            def queries(t, b, degrees):
                act.wait_ge(xT_ps, t + 1)
                act.copy(xT[:].rearrange("p k c -> p (k c)"), psT[:, 0:C]).then_inc(xT_ready, 1)
                if degrees == 1:
                    act.copy(deg_all[:, bass.ds(t + 2, 1)], psT[:, C:C + 1]).then_inc(deg_copied, 1)
                elif degrees > 1:
                    act.copy(deg_all[:, 0:degrees], psT[:, C:C + degrees]).then_inc(deg_copied, 1)
                act.wait_ge(q_ps, t + 1)
                act.wait_ge(sm_ready, t + 1)
                act.copy(q_sb[:, b, :], psQ[:, 0:C]).then_inc(q_ready, 1)

            act.wait_ge(xn_ready, NT - XL)
            act.wait_ge(last_ready, XL)
            act.copy(xt[:], row_all[:, 0, :]).then_inc(xt_ready, 1)
            queries(0, 0, 3)
            for u in range(GT):
                step(u, u)
            with act.Fori(0, NG - 2) as i:
                for u in range(GT):
                    step(i * GT + (GT + u), u)
            for u in range(GT):
                step(NT - GT + u, u)
            act.wait_ge(z_ps, NT - 1)
            act.copy(z_all[:, NT - 2, :], psQ[:, C:2 * C]).then_inc(z_copied, 1)
            act.wait_ge(y_ps, NT + GT)
            act.copy(yT_sb[:].rearrange("p k c -> p (k c)"), psY[:, 0:C]).then_inc(y_used, 1)
            act.wait_ge(z_ps, NT)
            act.copy(z_all[:, NT - 1, :], psQ[:, C:2 * C]).then_inc(z_copied, 1)

            def more_round(t, n):
                wait_alone(act, more_free, n + 1)
                act.copy(xt[:], row_all[:, bass.ds(t, 1), :].rearrange("p a c -> p (a c)")).then_inc(more_xt, 1)
                for q in range(NQ):
                    if q >= 2:
                        wait_alone(act, more_step, n * MORE + 2 * (q - 2) + 2)
                    wait_alone(act, more_codes, n * NQ + q + 1)
                    act.copy(quarter[q % 2], codes[:, q % 2, :]).then_inc(more_copied, 1)
                wait_alone(act, more_xTps, n + 1)
                act.copy(xT[:].rearrange("p k c -> p (k c)"), psT[:, 0:C]).then_inc(more_xT, 1)
                wait_alone(act, more_qps, n + 1)
                act.copy(q_sb[:, 0, :], psQ[:, 0:C]).then_inc(more_q, 1)
                wait_alone(act, more_m, n + 1)
                act.activation(p[:, 0, :], sm[:, 0, :], ACT.Exp, bias=run[:, 2:3], accum_out=run[:, 3:4]).then_inc(more_p, 1)
                act.activation(run[:, 4:5], run[:, 0:1], ACT.Exp, bias=run[:, 2:3]).then_inc(more_p, 1)
                wait_alone(act, more_p, n * 2 + 2)
                for k in range(K):
                    act.activation(diag[:, 0, k, :], ident[:], ACT.Copy, scale=p[:, 0, k:k + 1]).then_inc(more_diag, 1)
                wait_alone(act, more_yps, n + 1)
                act.copy(yT_sb[:].rearrange("p k c -> p (k c)"), psY[:, 0:C]).then_inc(more_yT, 1)
            act.wait_ge(rounds_known, 1)
            listed = act.value_load(sched[0:1, 3, 0:1], min_val=0, max_val=NT)
            with act.If(listed > 0):
                with act.Fori(0, listed) as m:
                    t = act.value_load(sched[0:1, 0, bass.ds(m, 1)], min_val=0, max_val=NT - 1)
                    r = act.value_load(sched[0:1, 1, bass.ds(t, 1)], min_val=1, max_val=N // K)
                    before = act.value_load(sched[0:1, 2, bass.ds(t, 1)], min_val=0, max_val=NT * N // K)
                    with act.Fori(0, r) as i:
                        more_round(t, before + i)

            act.sem_inc(lg_ready, 1)
            act.wait_ge(attention_done, 1)

            def route(q, b):
                act.wait_ge(var_ready, q + 1)
                act.activation(rs2[:, b, 0], rs2[:, b, 2], ACT.Sqrt).then_inc(std_ready, 1)
                act.wait_ge(norm_ready, q + 1)
                wait_alone(act, xg_free, q + 1)
                for u in range(QT + 2):
                    if u < QT:
                        act.activation(xg[:, b, u, :], tile(x_all, q * QT + u), ACT.Identity, bias=rs2[:, b, 4, u:u + 1],
                                       scale=rs2[:, b, 0, u:u + 1]).then_inc(xg_ready, 1)
                    if u >= 2:
                        t = q * QT + (u - 2)
                        wait_alone(act, lg_done, t + 1)
                        act.wait_ge(xg_ps, t + 1)
                        act.copy(xgT[:, u % 2, :], psXT[:, u % 2, 0:C]).then_inc(xgT_ready, 1)
                act.wait_ge(lg_done, q * QT + QT + 2)
                act.copy(lg[:, 0].rearrange("p t e -> p (t e)"), psL[:, 0:QT * E]).then_inc(lg_ready, 1)
            with act.Fori(0, NT // QT // 2) as i:
                route(i * 2, 0)
                route(i * 2 + 1, 1)
            act.wait_ge(planned, 1)
            act.activation(gates[:, 1], d_all[:], ACT.Exp).then_inc(d_exp, 1)

            act.sem_inc(hf_ready, 4)

            def part_of_x(n):
                act.wait_ge(x_ps, n + 1 + 1)
                act.copy(x_hi[:].rearrange("p k t -> p (k t)"), psX[:]).then_inc(xh_ready, 1)
            part_of_x(0)

            def tiles(e, b):
                act.copy(b1e[:, b, :], b1T[:, bass.ds(e * HC, HC)]).then_inc(b1_moved, 1)
                wait_alone(act, b1_moved, e + 1)
                count = act.value_load(plan[0:1, 0, bass.ds(e, 1)], min_val=1, max_val=N // T)
                before = act.value_load(plan[0:1, 1, bass.ds(e, 1)], min_val=0, max_val=MAX_TILES)
                with act.Fori(0, count) as i:
                    n = before + i
                    for hc in range(HC):
                        wait_alone(act, hl_ready, n * HC + hc + 1)
                        act.wait_ge(h_ps, n * HC + hc + 1)
                        act.activation(h_f[:, hc, :], psH[:, hc % 4, 0:T], ACT.Relu, bias=b1e[:, b, hc:hc + 1]).then_inc(hf_ready, 1)
                    part_of_x(n + 1)
            with act.Fori(0, E // 2) as e:
                tiles(e * 2, 0)
                tiles(e * 2 + 1, 1)
    return nc


_INS = ["x", "adj", "L0_gnn_Wq", "L0_gnn_Wk", "L0_gnn_Wv", "L0_ffn_W_router", "L0_ffn_W1", "L0_ffn_b1", "L0_ffn_W2", "L0_ffn_b2"]


def kernel(**inputs):
    import concourse.bacc as bacc
    from concourse.bass_utils import run_bass_kernel_spmd

    nc = bacc.Bacc("TRN2", target_bir_lowering=False, num_devices=1)
    arrays, args = {}, []
    for name in _INS:
        a = np.ascontiguousarray(inputs[name])
        arrays[f"in_{name}"] = a
        args.append(nc.dram_tensor(f"in_{name}", a.shape, mybir.dt.from_np(a.dtype), kind="ExternalInput").ap())
    out = nc.dram_tensor("out", (N, C), F32, kind="ExternalOutput").ap()
    attention_and_experts(nc, *args, out)
    r = run_bass_kernel_spmd(nc, [arrays], core_ids=[0])
    return r.results[0]["out"]
```
